# Optimizing a Trainium2 kernel written in Bass

```python
import numpy as np
import jax
import jax.numpy as jnp

def _softmax(x, axis=-1):
    return jax.nn.softmax(x, axis=axis)

def _gelu(x):
    return jax.nn.gelu(x, approximate=True)

def _silu(x):
    return jax.nn.silu(x)

def _sigmoid(x):
    return jax.nn.sigmoid(x)

def _layernorm(x, axis=-1, eps=1e-05):
    m = jnp.mean(x, axis=axis, keepdims=True)
    v = jnp.var(x, axis=axis, keepdims=True)
    return (x - m) / jnp.sqrt(v + eps)

def _scatter_add(tgt, idx, src, axis=0):
    return tgt.at[idx].add(src)

def _segment_sum(src, seg, n):
    return jax.ops.segment_sum(src, seg, n)
kernel_name = 'mk_xattn_seq_d4_seqx_r4_7d72c7'

def setup_inputs(seed: int=0):
    np.random.seed(seed)
    _w = jnp.asarray

    def _rec_inputs():
        import jax
        import jax.numpy as jnp
        _rk = jax.random.key(seed)
        x = 7.22e-05 + 1 * jax.random.normal(jax.random.fold_in(_rk, 1), (8, 256, 512), jnp.float32)
        _lenS = 256 - jax.random.randint(jax.random.fold_in(_rk, 7), (8,), 0, max(1, 256 // 4) + 1, jnp.int32)
        _lenS2 = 256 - jax.random.randint(jax.random.fold_in(_rk, 8), (8,), 0, max(1, 256 // 4) + 1, jnp.int32)
        _ctx_2048P = jax.random.normal(jax.random.fold_in(_rk, 11), (8, 16, 512), jnp.float32)
        _ctx_2048c = jax.random.dirichlet(jax.random.fold_in(_rk, 511), 0.3 * jnp.ones((16,), jnp.float32), (8, 256))
        _ctx_2048t = jnp.einsum('bsk,bkd->bsd', _ctx_2048c, _ctx_2048P)
        _ctx_2048t = _ctx_2048t * jax.lax.rsqrt(jnp.mean(jnp.square(_ctx_2048t)) + 1e-12) * 0.953939
        ctx_2048 = 4.13588e-05 + 0.999923 * (_ctx_2048t + 0.3 * jax.random.normal(jax.random.fold_in(_rk, 611), (8, 256, 512), jnp.float32))
        _validS = jnp.arange(256)[None, :] < _lenS[:, None]
        _validS2 = jnp.arange(256)[None, :] < _lenS2[:, None]
        _causal = jnp.tril(jnp.ones((256, 256), dtype=bool))
        mask_BxS2_bf1 = jnp.ones((8, 256), dtype=bool)
        mask_1x1xSxS2_fc1 = jnp.where(jnp.broadcast_to(_validS2[0:1, None, None, :], (1, 1, 256, 256)), 1.0, 0.0).astype(jnp.float32)
        mask_Bx1xSxS2_ff1 = jnp.where(jnp.ones((8, 1, 256, 256), dtype=bool), 1.0, 0.0).astype(jnp.float32)
        return (x, ctx_2048, mask_BxS2_bf1, mask_1x1xSxS2_fc1, mask_Bx1xSxS2_ff1)
    x, ctx_2048, mask_BxS2_bf1, mask_1x1xSxS2_fc1, mask_Bx1xSxS2_ff1 = _rec_inputs()

    def _L0_xattn_setup():
        import jax, jax.numpy as jnp
        import numpy as np
        B, CQ, CKV, LQ, LKV, HEADS = (4, 256, 256, 512, 512, 16)

        def _conv1x1(W, x):
            return jnp.einsum('oi,bil->bol', W, x)

        def _linear_interp(x, L_out):
            B_, C_, L_in = x.shape
            if L_in == L_out:
                return x
            scale = L_in / L_out
            pos = (jnp.arange(L_out, dtype=x.dtype) + 0.5) * scale - 0.5
            pos = jnp.clip(pos, 0.0, L_in - 1)
            lo = jnp.floor(pos).astype(jnp.int32)
            hi = jnp.minimum(lo + 1, L_in - 1)
            w = pos - lo.astype(x.dtype)
            return x[:, :, lo] * (1.0 - w) + x[:, :, hi] * w
        key = jax.random.key(seed)
        ks = jax.random.split(key, 7)
        winit = 1.0 / np.sqrt(CQ)
        return {'query': jax.random.normal(ks[0], (B, CQ, LQ), dtype=jnp.float32), 'context': jax.random.normal(ks[1], (B, CKV, LKV), dtype=jnp.float32), 'Wq': jax.random.normal(ks[2], (CQ, CQ), dtype=jnp.float32) * winit, 'Wk': jax.random.normal(ks[3], (CQ, CKV), dtype=jnp.float32) * winit, 'Wv': jax.random.normal(ks[4], (CQ, CKV), dtype=jnp.float32) * winit, 'Wo': jax.random.normal(ks[5], (CQ, CQ), dtype=jnp.float32) * winit, 'bo': jnp.zeros((CQ,), dtype=jnp.float32), 'heads': HEADS}
    _L0_xattn_all = _L0_xattn_setup()
    _L0_xattn_in = {k: v for k, v in _L0_xattn_all.items() if k in ('Wq', 'Wk', 'Wv', 'Wo', 'bo')}
    del _L0_xattn_all

    def _L1_xattn_setup():
        import jax, jax.numpy as jnp
        import numpy as np
        D = 512
        H = 16
        HD = D // H
        INNER = 4 * D
        EPS = 1e-05

        def layer_norm(x, w, b):
            mu = jnp.mean(x, axis=-1, keepdims=True)
            var = jnp.mean(jnp.square(x - mu), axis=-1, keepdims=True)
            return (x - mu) * jax.lax.rsqrt(var + EPS) * w + b
        key = jax.random.key(seed)
        ks = jax.random.split(key, 12)
        B, LQ, LK = (4, 256, 512)
        std = 0.02
        inp = {'hidden_states': jax.random.normal(ks[0], (B, LQ, D), jnp.float32), 'encoder_hidden_states': jax.random.normal(ks[1], (B, LK, D), jnp.float32), 'encoder_attention_mask': jnp.ones((B, LK), dtype=bool), 'ln1_w': jnp.ones((D,), jnp.float32), 'ln1_b': jnp.zeros((D,), jnp.float32), 'q_w': jax.random.normal(ks[2], (D, D), jnp.float32) * std, 'q_b': jnp.zeros((D,), jnp.float32), 'k_w': jax.random.normal(ks[3], (D, D), jnp.float32) * std, 'k_b': jnp.zeros((D,), jnp.float32), 'v_w': jax.random.normal(ks[4], (D, D), jnp.float32) * std, 'v_b': jnp.zeros((D,), jnp.float32), 'cproj_w': jax.random.normal(ks[5], (D, D), jnp.float32) * std, 'cproj_b': jnp.zeros((D,), jnp.float32), 'ln2_w': jnp.ones((D,), jnp.float32), 'ln2_b': jnp.zeros((D,), jnp.float32), 'fc_w': jax.random.normal(ks[6], (D, INNER), jnp.float32) * std, 'fc_b': jnp.zeros((INNER,), jnp.float32), 'proj_w': jax.random.normal(ks[7], (INNER, D), jnp.float32) * std, 'proj_b': jnp.zeros((D,), jnp.float32)}
        return inp
    _L1_xattn_all = _L1_xattn_setup()
    _L1_xattn_in = {k: v for k, v in _L1_xattn_all.items() if k in ('ln1_w', 'ln1_b', 'q_w', 'q_b', 'k_w', 'k_b', 'v_w', 'v_b', 'cproj_w', 'cproj_b', 'ln2_w', 'ln2_b', 'fc_w', 'fc_b', 'proj_w', 'proj_b')}
    del _L1_xattn_all

    def _L2_xattn_setup():
        import jax, jax.numpy as jnp
        import numpy as np
        D_MODEL = 256
        N_HEAD = 16
        D_HEAD = 64
        IDX_LIST = [256, 512]
        SCALE = 1.0 / D_HEAD ** 0.5
        LN_EPS = 1e-05
        key = jax.random.key(seed)
        ks = jax.random.split(key, 9)
        s = 0.02
        B, L = (2, 512)
        return {'z1ss': jax.random.normal(ks[0], (B, D_MODEL, L), dtype=jnp.float32), 'u1ss': jax.random.normal(ks[1], (B, D_MODEL, L), dtype=jnp.float32), 'Wqkv0': jax.random.normal(ks[2], (3 * N_HEAD * D_HEAD, D_MODEL), dtype=jnp.float32) * s, 'Wqkv1': jax.random.normal(ks[3], (3 * N_HEAD * D_HEAD, D_MODEL), dtype=jnp.float32) * s, 'Winj0': jax.random.normal(ks[4], (3 * N_HEAD * D_HEAD, D_MODEL), dtype=jnp.float32) * s, 'Winj1': jax.random.normal(ks[5], (3 * N_HEAD * D_HEAD, D_MODEL), dtype=jnp.float32) * s, 'Wo': jax.random.normal(ks[6], (D_MODEL, N_HEAD * D_HEAD), dtype=jnp.float32) * s, 'bo': jax.random.normal(ks[7], (D_MODEL,), dtype=jnp.float32) * s, 'r_w_bias': jax.random.uniform(ks[8], (N_HEAD, D_HEAD), minval=-0.05, maxval=0.05, dtype=jnp.float32)}
    _L2_xattn_all = _L2_xattn_setup()
    _L2_xattn_in = {k: v for k, v in _L2_xattn_all.items() if k in ('Wqkv0', 'Wqkv1', 'Winj0', 'Winj1', 'Wo', 'bo', 'r_w_bias')}
    del _L2_xattn_all

    def _L3_xattn_setup():
        import jax, jax.numpy as jnp
        import numpy as np
        H = 512
        NH = 16
        HD = H // NH
        EPS = 1e-05

        def gelu(x):
            return 0.5 * x * (1.0 + jnp.tanh(0.7978845608028654 * x * (1.0 + 0.044715 * x * x)))

        def layernorm(x, scale, bias):
            m = jnp.mean(x, axis=-1, keepdims=True)
            v = jnp.mean(jnp.square(x - m), axis=-1, keepdims=True)
            return (x - m) * jax.lax.rsqrt(v + EPS) * scale + bias

        def split_heads(x):
            b, s, _ = x.shape
            return x.reshape(b, s, NH, HD).transpose(0, 2, 1, 3)

        def merge_heads(x):
            b, nh, s, hd = x.shape
            return x.transpose(0, 2, 1, 3).reshape(b, s, nh * hd)

        def attention(q, k, v, mask):
            scores = jnp.einsum('bhqd,bhkd->bhqk', q, k) / jnp.sqrt(jnp.float32(HD))
            scores = scores * mask - 10000.0 * (1.0 - mask)
            probs = jax.nn.softmax(scores, axis=-1)
            return jnp.einsum('bhqk,bhkd->bhqd', probs, v)
        key = jax.random.key(seed)
        ks = jax.random.split(key, 16)
        b, s, t = (2, 256, 256)
        w = lambda k, i, o: jax.random.normal(k, (i, o), jnp.float32) * 0.02
        inp = {'hidden_states': jax.random.normal(ks[0], (b, s, H), jnp.float32), 'encoder_states': jax.random.normal(ks[1], (b, t, H), jnp.float32), 'ltor_mask': jnp.tril(jnp.ones((1, 1, s, s), jnp.float32)), 'cross_mask': jnp.ones((b, 1, s, t), jnp.float32), 'ln1_s': jnp.ones((H,), jnp.float32), 'ln1_b': jnp.zeros((H,), jnp.float32), 'w_qkv': w(ks[2], H, 3 * H), 'b_qkv': jnp.zeros((3 * H,), jnp.float32), 'w_ao': w(ks[3], H, H), 'b_ao': jnp.zeros((H,), jnp.float32), 'ln2_s': jnp.ones((H,), jnp.float32), 'ln2_b': jnp.zeros((H,), jnp.float32), 'w_q': w(ks[4], H, H), 'b_q': jnp.zeros((H,), jnp.float32), 'w_kv': w(ks[5], H, 2 * H), 'b_kv': jnp.zeros((2 * H,), jnp.float32), 'w_co': w(ks[6], H, H), 'b_co': jnp.zeros((H,), jnp.float32), 'ln3_s': jnp.ones((H,), jnp.float32), 'ln3_b': jnp.zeros((H,), jnp.float32), 'w1': w(ks[7], H, 4 * H), 'b1': jnp.zeros((4 * H,), jnp.float32), 'w2': w(ks[8], 4 * H, H), 'b2': jnp.zeros((H,), jnp.float32)}
        return inp
    _L3_xattn_all = _L3_xattn_setup()
    _L3_xattn_in = {k: v for k, v in _L3_xattn_all.items() if k in ('ln1_s', 'ln1_b', 'w_qkv', 'b_qkv', 'w_ao', 'b_ao', 'ln2_s', 'ln2_b', 'w_q', 'b_q', 'w_kv', 'b_kv', 'w_co', 'b_co', 'ln3_s', 'ln3_b', 'w1', 'b1', 'w2', 'b2')}
    del _L3_xattn_all
    return {'x': x, 'ctx_2048': ctx_2048, 'mask_BxS2_bf1': mask_BxS2_bf1, 'mask_1x1xSxS2_fc1': mask_1x1xSxS2_fc1, 'mask_Bx1xSxS2_ff1': mask_Bx1xSxS2_ff1, 'L0_xattn_Wq': _L0_xattn_in['Wq'], 'L0_xattn_Wk': _L0_xattn_in['Wk'], 'L0_xattn_Wv': _L0_xattn_in['Wv'], 'L0_xattn_Wo': _L0_xattn_in['Wo'], 'L0_xattn_bo': _L0_xattn_in['bo'], 'L1_xattn_ln1_w': _L1_xattn_in['ln1_w'], 'L1_xattn_ln1_b': _L1_xattn_in['ln1_b'], 'L1_xattn_q_w': _L1_xattn_in['q_w'], 'L1_xattn_q_b': _L1_xattn_in['q_b'], 'L1_xattn_k_w': _L1_xattn_in['k_w'], 'L1_xattn_k_b': _L1_xattn_in['k_b'], 'L1_xattn_v_w': _L1_xattn_in['v_w'], 'L1_xattn_v_b': _L1_xattn_in['v_b'], 'L1_xattn_cproj_w': _L1_xattn_in['cproj_w'], 'L1_xattn_cproj_b': _L1_xattn_in['cproj_b'], 'L1_xattn_ln2_w': _L1_xattn_in['ln2_w'], 'L1_xattn_ln2_b': _L1_xattn_in['ln2_b'], 'L1_xattn_fc_w': _L1_xattn_in['fc_w'], 'L1_xattn_fc_b': _L1_xattn_in['fc_b'], 'L1_xattn_proj_w': _L1_xattn_in['proj_w'], 'L1_xattn_proj_b': _L1_xattn_in['proj_b'], 'L2_xattn_Wqkv0': _L2_xattn_in['Wqkv0'], 'L2_xattn_Wqkv1': _L2_xattn_in['Wqkv1'], 'L2_xattn_Winj0': _L2_xattn_in['Winj0'], 'L2_xattn_Winj1': _L2_xattn_in['Winj1'], 'L2_xattn_Wo': _L2_xattn_in['Wo'], 'L2_xattn_bo': _L2_xattn_in['bo'], 'L2_xattn_r_w_bias': _L2_xattn_in['r_w_bias'], 'L3_xattn_ln1_s': _L3_xattn_in['ln1_s'], 'L3_xattn_ln1_b': _L3_xattn_in['ln1_b'], 'L3_xattn_w_qkv': _L3_xattn_in['w_qkv'], 'L3_xattn_b_qkv': _L3_xattn_in['b_qkv'], 'L3_xattn_w_ao': _L3_xattn_in['w_ao'], 'L3_xattn_b_ao': _L3_xattn_in['b_ao'], 'L3_xattn_ln2_s': _L3_xattn_in['ln2_s'], 'L3_xattn_ln2_b': _L3_xattn_in['ln2_b'], 'L3_xattn_w_q': _L3_xattn_in['w_q'], 'L3_xattn_b_q': _L3_xattn_in['b_q'], 'L3_xattn_w_kv': _L3_xattn_in['w_kv'], 'L3_xattn_b_kv': _L3_xattn_in['b_kv'], 'L3_xattn_w_co': _L3_xattn_in['w_co'], 'L3_xattn_b_co': _L3_xattn_in['b_co'], 'L3_xattn_ln3_s': _L3_xattn_in['ln3_s'], 'L3_xattn_ln3_b': _L3_xattn_in['ln3_b'], 'L3_xattn_w1': _L3_xattn_in['w1'], 'L3_xattn_b1': _L3_xattn_in['b1'], 'L3_xattn_w2': _L3_xattn_in['w2'], 'L3_xattn_b2': _L3_xattn_in['b2']}

def reference(x, ctx_2048, mask_BxS2_bf1, mask_1x1xSxS2_fc1, mask_Bx1xSxS2_ff1, L0_xattn_Wq, L0_xattn_Wk, L0_xattn_Wv, L0_xattn_Wo, L0_xattn_bo, L1_xattn_ln1_w, L1_xattn_ln1_b, L1_xattn_q_w, L1_xattn_q_b, L1_xattn_k_w, L1_xattn_k_b, L1_xattn_v_w, L1_xattn_v_b, L1_xattn_cproj_w, L1_xattn_cproj_b, L1_xattn_ln2_w, L1_xattn_ln2_b, L1_xattn_fc_w, L1_xattn_fc_b, L1_xattn_proj_w, L1_xattn_proj_b, L2_xattn_Wqkv0, L2_xattn_Wqkv1, L2_xattn_Winj0, L2_xattn_Winj1, L2_xattn_Wo, L2_xattn_bo, L2_xattn_r_w_bias, L3_xattn_ln1_s, L3_xattn_ln1_b, L3_xattn_w_qkv, L3_xattn_b_qkv, L3_xattn_w_ao, L3_xattn_b_ao, L3_xattn_ln2_s, L3_xattn_ln2_b, L3_xattn_w_q, L3_xattn_b_q, L3_xattn_w_kv, L3_xattn_b_kv, L3_xattn_w_co, L3_xattn_b_co, L3_xattn_ln3_s, L3_xattn_ln3_b, L3_xattn_w1, L3_xattn_b1, L3_xattn_w2, L3_xattn_b2):
    import jax
    import jax.numpy as jnp

    def _L0_xattn_ref(query, context, Wq, Wk, Wv, Wo, bo, heads):
        import jax, jax.numpy as jnp
        import numpy as np
        B, CQ, CKV, LQ, LKV, HEADS = (4, 256, 256, 512, 512, 16)

        def _conv1x1(W, x):
            return jnp.einsum('oi,bil->bol', W, x)

        def _linear_interp(x, L_out):
            B_, C_, L_in = x.shape
            if L_in == L_out:
                return x
            scale = L_in / L_out
            pos = (jnp.arange(L_out, dtype=x.dtype) + 0.5) * scale - 0.5
            pos = jnp.clip(pos, 0.0, L_in - 1)
            lo = jnp.floor(pos).astype(jnp.int32)
            hi = jnp.minimum(lo + 1, L_in - 1)
            w = pos - lo.astype(x.dtype)
            return x[:, :, lo] * (1.0 - w) + x[:, :, hi] * w
        B_, Cq, Lq = query.shape
        H = heads
        D = Cq // H
        scale = D ** (-0.5)
        q = _conv1x1(Wq, query).reshape(B_, H, D, Lq)
        k = _conv1x1(Wk, context)
        v = _conv1x1(Wv, context)
        if k.shape[2] != Lq:
            k = _linear_interp(k, Lq)
            v = _linear_interp(v, Lq)
        k = k.reshape(B_, H, D, Lq)
        v = v.reshape(B_, H, D, Lq)
        attn = jnp.einsum('bhdi,bhdj->bhij', q, k) * scale
        attn = jax.nn.softmax(attn, axis=-1)
        out = jnp.einsum('bhij,bhdj->bhdi', attn, v).reshape(B_, Cq, Lq)
        return _conv1x1(Wo, out) + bo[None, :, None] + query

    def _L1_xattn_ref(hidden_states, encoder_hidden_states, encoder_attention_mask, ln1_w, ln1_b, q_w, q_b, k_w, k_b, v_w, v_b, cproj_w, cproj_b, ln2_w, ln2_b, fc_w, fc_b, proj_w, proj_b):
        import jax, jax.numpy as jnp
        import numpy as np
        D = 512
        H = 16
        HD = D // H
        INNER = 4 * D
        EPS = 1e-05

        def layer_norm(x, w, b):
            mu = jnp.mean(x, axis=-1, keepdims=True)
            var = jnp.mean(jnp.square(x - mu), axis=-1, keepdims=True)
            return (x - mu) * jax.lax.rsqrt(var + EPS) * w + b
        B, LQ, _ = hidden_states.shape
        LK = encoder_hidden_states.shape[1]
        residual = hidden_states
        x = layer_norm(hidden_states, ln1_w, ln1_b)
        q = (x @ q_w + q_b).reshape(B, LQ, H, HD).transpose(0, 2, 1, 3)
        k = (encoder_hidden_states @ k_w + k_b).reshape(B, LK, H, HD).transpose(0, 2, 1, 3)
        v = (encoder_hidden_states @ v_w + v_b).reshape(B, LK, H, HD).transpose(0, 2, 1, 3)
        scale = 1.0 / np.sqrt(HD).astype(np.float32)
        scores = jnp.einsum('bhqd,bhkd->bhqk', q, k) * scale
        mask = encoder_attention_mask[:, None, None, :]
        mask_value = jnp.finfo(scores.dtype).min
        scores = jnp.where(mask, scores, mask_value)
        attn = jax.nn.softmax(scores, axis=-1)
        out = jnp.einsum('bhqk,bhkd->bhqd', attn, v)
        out = out.transpose(0, 2, 1, 3).reshape(B, LQ, D)
        out = out @ cproj_w + cproj_b
        hidden = out + residual
        residual = hidden
        y = layer_norm(hidden, ln2_w, ln2_b)
        y = jax.nn.gelu(y @ fc_w + fc_b, approximate=True)
        y = y @ proj_w + proj_b
        return residual + y

    def _L2_xattn_ref(z1ss, u1ss, Wqkv0, Wqkv1, Winj0, Winj1, Wo, bo, r_w_bias):
        import jax, jax.numpy as jnp
        import numpy as np
        D_MODEL = 256
        N_HEAD = 16
        D_HEAD = 64
        IDX_LIST = [256, 512]
        SCALE = 1.0 / D_HEAD ** 0.5
        LN_EPS = 1e-05
        bsz, d_model, qlen = z1ss.shape
        bounds = [0] + IDX_LIST
        Wq_list, Wi_list = ([Wqkv0, Wqkv1], [Winj0, Winj1])
        chunks = []
        for i in range(len(IDX_LIST)):
            s, e = (bounds[i], bounds[i + 1])
            h = jnp.einsum('od,bdl->bol', Wq_list[i], z1ss[:, :, s:e])
            h = h + jnp.einsum('od,bdl->bol', Wi_list[i], u1ss[:, :, s:e])
            chunks.append(h)
        w_heads = jnp.concatenate(chunks, axis=2)
        q, k, v = jnp.split(w_heads, 3, axis=1)
        q = q[:, :, -qlen:]
        klen = k.shape[2]
        q = q.reshape(bsz, N_HEAD, D_HEAD, qlen)
        k = k.reshape(bsz, N_HEAD, D_HEAD, klen)
        v = v.reshape(bsz, N_HEAD, D_HEAD, klen)
        rq = q + r_w_bias[None, :, :, None]
        score = jnp.einsum('bndi,bndj->bnij', rq, k) * SCALE
        prob = jax.nn.softmax(score, axis=-1)
        attn_vec = jnp.einsum('bnij,bndj->bndi', prob, v)
        attn_vec = attn_vec.reshape(bsz, N_HEAD * D_HEAD, qlen)
        attn_out = jnp.einsum('od,bdl->bol', Wo, attn_vec) + bo[None, :, None]
        x = attn_out + z1ss
        m = jnp.mean(x, axis=1, keepdims=True)
        var = jnp.var(x, axis=1, keepdims=True)
        return (x - m) * jax.lax.rsqrt(var + LN_EPS)

    def _L3_xattn_ref(hidden_states, encoder_states, ltor_mask, cross_mask, ln1_s, ln1_b, w_qkv, b_qkv, w_ao, b_ao, ln2_s, ln2_b, w_q, b_q, w_kv, b_kv, w_co, b_co, ln3_s, ln3_b, w1, b1, w2, b2):
        import jax, jax.numpy as jnp
        import numpy as np
        H = 512
        NH = 16
        HD = H // NH
        EPS = 1e-05

        def gelu(x):
            return 0.5 * x * (1.0 + jnp.tanh(0.7978845608028654 * x * (1.0 + 0.044715 * x * x)))

        def layernorm(x, scale, bias):
            m = jnp.mean(x, axis=-1, keepdims=True)
            v = jnp.mean(jnp.square(x - m), axis=-1, keepdims=True)
            return (x - m) * jax.lax.rsqrt(v + EPS) * scale + bias

        def split_heads(x):
            b, s, _ = x.shape
            return x.reshape(b, s, NH, HD).transpose(0, 2, 1, 3)

        def merge_heads(x):
            b, nh, s, hd = x.shape
            return x.transpose(0, 2, 1, 3).reshape(b, s, nh * hd)

        def attention(q, k, v, mask):
            scores = jnp.einsum('bhqd,bhkd->bhqk', q, k) / jnp.sqrt(jnp.float32(HD))
            scores = scores * mask - 10000.0 * (1.0 - mask)
            probs = jax.nn.softmax(scores, axis=-1)
            return jnp.einsum('bhqk,bhkd->bhqd', probs, v)
        ln_out = layernorm(hidden_states, ln1_s, ln1_b)
        qkv = ln_out @ w_qkv + b_qkv
        q, k, v = jnp.split(qkv, 3, axis=-1)
        ctx = merge_heads(attention(split_heads(q), split_heads(k), split_heads(v), ltor_mask))
        attn_out = ctx @ w_ao + b_ao
        x = hidden_states + attn_out
        ln_out = layernorm(x, ln2_s, ln2_b)
        q = ln_out @ w_q + b_q
        kv = encoder_states @ w_kv + b_kv
        k, v = jnp.split(kv, 2, axis=-1)
        ctx = merge_heads(attention(split_heads(q), split_heads(k), split_heads(v), cross_mask))
        cross_out = ctx @ w_co + b_co
        x = x + cross_out
        ln_out = layernorm(x, ln3_s, ln3_b)
        mlp_out = gelu(ln_out @ w1 + b1) @ w2 + b2
        return x + mlp_out
    x = _L0_xattn_ref(x, ctx_2048, L0_xattn_Wq, L0_xattn_Wk, L0_xattn_Wv, L0_xattn_Wo, L0_xattn_bo, 16)
    x = _L1_xattn_ref(x, ctx_2048, mask_BxS2_bf1, L1_xattn_ln1_w, L1_xattn_ln1_b, L1_xattn_q_w, L1_xattn_q_b, L1_xattn_k_w, L1_xattn_k_b, L1_xattn_v_w, L1_xattn_v_b, L1_xattn_cproj_w, L1_xattn_cproj_b, L1_xattn_ln2_w, L1_xattn_ln2_b, L1_xattn_fc_w, L1_xattn_fc_b, L1_xattn_proj_w, L1_xattn_proj_b)
    x = _L2_xattn_ref(x, ctx_2048, L2_xattn_Wqkv0, L2_xattn_Wqkv1, L2_xattn_Winj0, L2_xattn_Winj1, L2_xattn_Wo, L2_xattn_bo, L2_xattn_r_w_bias)
    x = _L3_xattn_ref(x, ctx_2048, mask_1x1xSxS2_fc1, mask_Bx1xSxS2_ff1, L3_xattn_ln1_s, L3_xattn_ln1_b, L3_xattn_w_qkv, L3_xattn_b_qkv, L3_xattn_w_ao, L3_xattn_b_ao, L3_xattn_ln2_s, L3_xattn_ln2_b, L3_xattn_w_q, L3_xattn_b_q, L3_xattn_w_kv, L3_xattn_b_kv, L3_xattn_w_co, L3_xattn_b_co, L3_xattn_ln3_s, L3_xattn_ln3_b, L3_xattn_w1, L3_xattn_b1, L3_xattn_w2, L3_xattn_b2)
    return x

_drawn_inputs = setup_inputs


def setup_inputs(seed=0):
    import zlib

    import numpy as np

    out = dict(_drawn_inputs(seed))
    spreads = {'L0_xattn_bo': (0.0, 0.1),
     'L1_xattn_ln1_w': (1.0, 0.6),
     'L1_xattn_ln1_b': (0.0, 0.8),
     'L1_xattn_q_b': (0.0, 0.8),
     'L1_xattn_k_b': (0.0, 2.0),
     'L1_xattn_v_b': (0.0, 0.8),
     'L1_xattn_cproj_b': (0.0, 0.733),
     'L1_xattn_ln2_w': (1.0, 0.2),
     'L1_xattn_ln2_b': (0.0, 0.676),
     'L1_xattn_fc_b': (0.0, 0.322),
     'L1_xattn_proj_b': (0.0, 0.8),
     'L3_xattn_ln1_s': (1.0, 0.6),
     'L3_xattn_ln1_b': (0.0, 0.464),
     'L3_xattn_b_qkv': (0.0, 0.1),
     'L3_xattn_b_ao': (0.0, 0.1),
     'L3_xattn_ln2_s': (1.0, 0.6),
     'L3_xattn_ln2_b': (0.0, 0.8),
     'L3_xattn_b_q': (0.0, 2.0),
     'L3_xattn_b_kv': (0.0, 0.1),
     'L3_xattn_b_co': (0.0, 0.1),
     'L3_xattn_ln3_s': (1.0, 0.2),
     'L3_xattn_ln3_b': (0.0, 0.345),
     'L3_xattn_b1': (0.0, 0.1),
     'L3_xattn_b2': (0.0, 0.1)}
    factors = {'L1_xattn_q_w': 7.748,
     'L1_xattn_k_w': 7.766,
     'L1_xattn_v_w': 4.158,
     'L1_xattn_cproj_w': 3.832,
     'L2_xattn_Wqkv0': 4.822,
     'L2_xattn_Wqkv1': 4.656,
     'L2_xattn_Winj0': 7.337,
     'L2_xattn_Winj1': 7.191,
     'L2_xattn_Wo': 2.925,
     'L2_xattn_bo': 25.128,
     'L2_xattn_r_w_bias': 8.0,
     'L3_xattn_w_qkv': 2.824,
     'L3_xattn_w_q': 7.449}
    for name, (base, spread) in spreads.items():
        noise = np.random.default_rng([zlib.crc32(name.encode()), seed]).standard_normal(out[name].shape)
        drawn = base * np.exp(spread * noise) if base else spread * noise
        out[name] = jnp.asarray(drawn.astype(out[name].dtype))
    for name, factor in factors.items():
        out[name] = (out[name] * factor).astype(out[name].dtype)
    return out
```

```python
from contextlib import ExitStack

import concourse.bass as bass
from concourse import mybir
from concourse.alu_op_type import AluOpType as ALU

F32 = mybir.dt.float32
U8 = mybir.dt.uint8
ACT = mybir.ActivationFunctionType
AX = mybir.AxisListType

P = 128
NB = 8
ROWS = 256
COLS = 512
BANK = 512
EPS = 1e-5
KEY_MASKED = -3.0e38
LOWEST = -3.4e38
TURN_LAG = 2
MIX_LAG = 4


class Count:

    def __init__(self, sem, per):
        self.sem, self.per = sem, per

    def prime(self, eng):
        eng.sem_inc(self.sem, self.per)

    def at(self, b, k):
        return b * self.per + (self.per + k)


def attention_stage(nc, name, x_in, x_out, kv_in, weights, cols, ident_dram, *, head_dim, queries,
                    keys, halves=1, norm=None, self_kv=False, kv_also_q=False, key_mask=None,
                    score_mask=None, channel_out=False, v_row=None, out_row=None, norm_out=False):
    cols_dram, at_col, n_cols = cols
    NG = weights["o"].shape[0] // P
    CH = NG * P
    G = P // head_dim
    H = NG * G
    NI = queries // P
    NJ = keys // P
    II = BANK // keys
    SPG = NI // II
    QW = II * P
    U = H * SPG
    S = NG * SPG
    TILES = min(G, 4)
    TW = P // TILES
    HPT = G // TILES
    VW = TW
    HL = queries // halves
    KX = (2 if norm is None else 4)
    KC = 0 if self_kv else kv_in.shape[1] // P
    scale = float(head_dim) ** -0.5
    sources_q = (["x"] * KX) if not kv_also_q else ["x"] * KX + ["c"] * KC
    if self_kv or kv_also_q:
        sources_kv = sources_q
    else:
        sources_kv = ["c"] * KC
    chunk_q = [i if i < KX else i - KX for i in range(len(sources_q))]
    chunk_kv = chunk_q if (self_kv or kv_also_q) else list(range(KC))
    OC = 2
    plan, banks = [], []

    def bank_item(kind, idx, engine):
        plan.append((kind, idx, len(banks)))
        banks.append(engine)

    vblocks = [(j, o) for j in range(NJ) for o in range((CH + BANK - 1) // BANK)]
    VN = min(CH, BANK)
    if not self_kv and not kv_also_q:
        bank_item("k", 0, "act")
        for i in range(len(vblocks)):
            bank_item("v", i, "dve")
        if norm:
            for i in range(2):
                bank_item("turnx", i, "dve")
        bank_item("q", 0, "act")
    else:
        if norm:
            for i in range(2):
                bank_item("turnx", i, "dve")
        bank_item("q", 0, "act")
        bank_item("k", 0, "act")
        for i in range(len(vblocks)):
            bank_item("v", i, "dve")
    upg = U // NG
    for n in range(U + MIX_LAG + 1):
        if n < U:
            g, r = divmod(n, upg)
            if g + 1 < NG and r == upg // 2:
                bank_item("q", g + 1, "act")
            if g + 1 < NG and r == upg // 2 + 1:
                bank_item("k", g + 1, "act")
            plan.append(("score", n, None))
        t = n - TURN_LAG
        if 0 <= t < U:
            plan.append(("turn", t, None))
        m = n - MIX_LAG
        if 0 <= m < U and m % G == G - 1:
            plan.append(("mix", m // G, None))
    for o in range(OC):
        bank_item("out", o, "dve")
    if norm_out:
        for i in range(2):
            bank_item("stat", i, "dve" if i == 0 else "act")
    NP = len(banks)
    act_items = [p for p in range(NP) if banks[p] == "act"]
    dve_items = [p for p in range(NP) if banks[p] == "dve"]
    assert len(act_items) >= 1 and len(dve_items) >= 1
    last_x = max(p for k, i, p in plan if k in (("q", "k", "v") if kv_also_q else ("q",)))
    last_c = max(p for k, i, p in plan if k in (("q", "k", "v") if kv_also_q else ("k", "v")))
    last_out = max(p for k, i, p in plan if k == "out")

    with ExitStack() as ctx:
        def sb(what, shape, dt=F32):
            return ctx.enter_context(nc.sbuf_tensor(f"{name}_{what}", shape, dt))

        sems = []

        def sem(what):
            sems.append(nc.alloc_semaphore(f"{name}_{what}"))
            return sems[-1]

        ident = sb("ident", [P, P])
        w_q = [[sb(f"wq{h}_{i}", [P, CH]) for i in range(len(sources_q))] for h in range(halves)]
        w_k = [[sb(f"wk{h}_{i}", [P, CH]) for i in range(len(sources_kv))] for h in range(halves)]
        w_v = [[sb(f"wv{h}_{i}", [P, CH]) for i in range(len(sources_kv))] for h in range(halves)]
        OW = weights["o"].shape[1]
        w_o = sb("wo", [P, NG, OW])
        col = sb("cols", [P, n_cols])
        head_mask = sb("head_mask", [P, G])
        x_sb = sb("x", [P, 2, COLS])
        res = sb("res", [P, 2, COLS])
        if norm:
            xn = sb("xn", [P, 2, COLS])
            xt = sb("xt", [P, 4, ROWS])
        c_sb = None if self_kv else sb("ctx", [P, KC, keys])
        q_flat = sb("q_flat", [P, 2, queries])
        q_pad = sb("q_pad", [P, 2, G, queries])
        k_sb = sb("k", [P, 2, keys])
        v_sb = sb("v", [P, NJ, H * VW if HPT > 1 else CH])
        probs = sb("probs", [P, 3, BANK])
        turned = sb("turned", [P, 2, G, BANK])
        neg_max = sb("neg_max", [P, 4, II])
        row_sum = sb("row_sum", [P, 2, II, G])
        inv_sum = sb("inv_sum", [P, 2, II, G])
        inv_wide = sb("inv_wide", [P, 2, II, P])
        inv_cols = sb("inv_cols", [P, 2, QW])
        mixed = sb("mixed", [P, NG, queries])
        y_sb = sb("y", [P, 2, COLS])
        if v_row is not None:
            v_bias = sb("v_bias", [P, CH])
        if out_row is not None:
            o_bias = sb("o_bias", [P, COLS])
        if key_mask is not None:
            mask_raw = sb("mask_raw", [P, keys], key_mask.dtype)
            mask_add = sb("mask_add", [P, 1, keys])
        if score_mask is not None:
            mask_mul = sb("mask_mul", [P, II, keys])
            mask_add = sb("mask_add", [P, II, keys])
        masked = (key_mask is not None) or (score_mask is not None)
        if masked:
            s_masked = sb("s_masked", [P, 3, BANK])
            row_max = sb("row_max", [P, 4, II])
        if norm:
            stats = sb("stats", [P, 2, 6])
            mean_var = sb("mean_var", [P, 2, 2])
            std = sb("std", [P, 2])
            rstd = sb("rstd", [P, 2])
        if norm_out:
            ones = sb("ones", [P, P])
            dev = sb("dev", [P, 2, COLS])
            sq = sb("sq", [P, 2, COLS])
            std_n = sb("std_n", [P, COLS])
            rstd_n = sb("rstd_n", [P, COLS])
        eps_col = sb("eps", [P, 1])
        q_bias = sb("q_bias", [P, NG])

        def ps(what, shape):
            return ctx.enter_context(nc.psum_tensor(f"{name}_{what}", shape, F32))

        ps_proj = [ps(f"proj{i}", [P, BANK]) for i in range(2)]
        ps_score = [ps(f"score{i}", [P, BANK]) for i in range(2)]
        ps_turn = [ps(f"turn{i}", [P, BANK]) for i in range(2)]
        ps_mix = [ps(f"mix{i}", [P, 2, BANK // 2]) for i in range(2)]

        weights_in = sem("weights_in")
        consts_in = sem("consts_in")
        x_loaded = sem("x_loaded")
        c_loaded = sem("c_loaded")
        res_loaded = sem("res_loaded")
        mask_loaded = sem("mask_loaded")
        stored = sem("stored")
        setup = sem("setup")
        passed_dve = sem("passed_dve")
        passed_pool = sem("passed_pool")
        chain = sem("dve_chain")
        pool_chain = sem("pool_chain")
        proj = Count(sem("proj_ready"), NP)
        took_act = Count(sem("proj_taken_act"), len(act_items))
        took_dve = Count(sem("proj_taken_dve"), len(dve_items))
        q_padded = Count(sem("q_padded"), NG)
        scored = Count(sem("scores_ready"), U)
        maxed = Count(sem("max_ready"), U)
        exped = Count(sem("probs_ready"), U)
        turn_done = Count(sem("turn_ready"), U)
        act_turns = [u for u in range(U) if u % 2 == 0]
        dve_turns = [u for u in range(U) if u % 2 == 1]
        kept_act = Count(sem("turned_kept_act"), len(act_turns))
        kept_dve = Count(sem("turned_kept_dve"), len(dve_turns))
        inv_ready = Count(sem("inv_sums_ready"), S)
        mix_done = Count(sem("mix_ready"), S)
        mix_taken = Count(sem("mix_taken"), S)
        xn_used = Count(sem("x_normed"), 1)
        std_ready = Count(sem("std_ready"), 1)
        var_ready = Count(sem("var_ready"), 1)
        res_ready = Count(sem("residual_ready"), 1)
        mask_ready = Count(sem("mask_ready"), 1)
        sq_ready = Count(sem("squares_ready"), 1)
        normed_out = Count(sem("normed_out"), 1)
        y_ready, y_signals = (normed_out, 1) if norm_out else (took_dve, dve_items.index(last_out) + 1)
        chain_per = {"dve": (3 if norm else 0) + (0 if not masked else U if key_mask is not None else 2 * U)
                     + 2 * S + (1 if norm_out else 0), "pool": 1}
        chain_at = {"stats": 2}
        n_setup = 2 + (1 if norm_out else 0) + (1 if HPT > 1 else 0)

        x_src = x_in.rearrange("b (k p) l -> b p k l", p=P)
        y_dst = x_out.rearrange("b (k p) l -> b p k l", p=P)
        if not self_kv:
            c_src = kv_in.rearrange("b (k p) l -> b p k l", p=P)

        def score_end(g):
            return (g + 1) * upg

        def turns_before(which, n):
            return len([u for u in which if u < n])

        n_weights = halves * (len(sources_q) + 2 * len(sources_kv)) + 1
        n_consts = 3 + (v_row is not None) + (out_row is not None)

        with nc.Block() as block:
            @block.sync
            def _(sp):
                sp.dma_start(head_mask[:, :], weights["head_mask"]).then_inc(consts_in, 16)
                sp.dma_start(col[:, :], cols_dram).then_inc(consts_in, 16)
                sp.dma_start(ident[:, :], ident_dram).then_inc(consts_in, 16)
                if v_row is not None:
                    sp.dma_start(v_bias[:, :], v_row.partition_broadcast(P)).then_inc(consts_in, 16)
                if out_row is not None:
                    sp.dma_start(o_bias[:, :], out_row.partition_broadcast(P)).then_inc(consts_in, 16)
                for key, tiles in (("k", w_k), ("v", w_v), ("q", w_q)):
                    for h in range(halves):
                        for i, tile in enumerate(tiles[h]):
                            sp.dma_start(tile[:, :], weights[key][h][i]).then_inc(weights_in, 16)
                sp.dma_start(w_o[:, :, :], weights["o"].rearrange("(g p) o -> p g o", p=P)).then_inc(weights_in, 16)
                sp.sem_inc(stored, 16)
                with sp.Fori(0, NB) as b:
                    sp.wait_ge(y_ready.sem, y_ready.at(b, y_signals))
                    sp.dma_start(y_dst[b], y_sb[:, :, :]).then_inc(stored, 16)
                sp.wait_ge(stored, 16 * NB + 16)

            @block.gpsimd
            def _(pool):
                for c in (q_padded, res_ready, mask_ready):
                    c.prime(pool)
                nc.gpsimd.memset(eps_col[:, :], EPS).then_inc(setup, 1)
                if norm_out:
                    nc.gpsimd.memset(ones[:, :], 1.0 / ROWS).then_inc(setup, 1)
                if HPT > 1:
                    nc.gpsimd.memset(v_sb[:, :, :], 0.0).then_inc(setup, 1)
                pool.wait_ge(consts_in, 16 * n_consts)
                nc.gpsimd.tensor_scalar(q_bias[:, :], col[:, at_col["q"]:at_col["q"] + NG], scale, 1.0,
                                        ALU.mult, ALU.mult).then_inc(setup, 1)

                def batch(b):
                    link = [0]
                    per_chain = chain_per["pool"]

                    def linked(ins):
                        link[0] += 1
                        ins.then_inc(pool_chain, 1)
                        pool.wait_ge(pool_chain, b * per_chain + link[0])
                        pool.sem_inc(passed_pool, 1)

                    if norm:
                        pool.wait_ge(xn_used.sem, xn_used.at(b, 0))
                        pool.sem_inc(passed_pool, 1)
                    else:
                        pool.wait_ge(proj.sem, proj.at(b, last_x + 1 - NP))
                        pool.sem_inc(passed_pool, 1)
                    pool.dma_start(x_sb[:, :, :], x_src[b]).then_inc(x_loaded, 16)
                    if not self_kv:
                        pool.wait_ge(proj.sem, proj.at(b, last_c + 1 - NP))
                        pool.sem_inc(passed_pool, 1)
                        pool.dma_start(c_sb[:, :, :], c_src[b]).then_inc(c_loaded, 16)
                    pool.wait_ge(y_ready.sem, y_ready.at(b, y_signals - y_ready.per))
                    pool.sem_inc(passed_pool, 1)
                    pool.dma_start(res[:, :, :], x_src[b]).then_inc(res_loaded, 16)
                    if key_mask is not None:
                        pool.dma_start(mask_raw[:, :], key_mask[b].partition_broadcast(P)).then_inc(mask_loaded, 16)
                    if score_mask is not None:
                        pool.dma_start(mask_mul[:, :, :], score_mask(b)).then_inc(mask_loaded, 16)
                    if masked:
                        pool.wait_ge(mask_loaded, 16 * b + 16)
                        pool.sem_inc(passed_pool, 1)
                        if key_mask is not None:
                            linked(nc.gpsimd.tensor_copy(mask_add[:, 0, :], mask_raw[:, :]))
                            nc.gpsimd.tensor_scalar(mask_add[:, 0, :], mask_add[:, 0, :], -KEY_MASKED, KEY_MASKED,
                                                    ALU.mult, ALU.add).then_inc(mask_ready.sem, 1)
                        else:
                            nc.gpsimd.tensor_scalar(mask_add[:, :, :], mask_mul[:, :, :], 10000.0, -10000.0,
                                                    ALU.mult, ALU.add).then_inc(mask_ready.sem, 1)
                    pool.wait_ge(res_loaded, 16 * b + 16)
                    pool.sem_inc(passed_pool, 1)
                    if out_row is not None:
                        for t in range(2):
                            ins = nc.gpsimd.tensor_tensor(res[:, t, :], res[:, t, :], o_bias[:, :], ALU.add)
                        ins.then_inc(res_ready.sem, 1)
                    for g in range(NG):
                        p = next(q for k, i, q in plan if k == "q" and i == g)
                        pool.wait_ge(took_act.sem, took_act.at(b, act_items.index(p) + 1))
                        pool.sem_inc(passed_pool, 1)
                        pool.wait_ge(scored.sem, scored.at(b, score_end(g - 2)))
                        pool.sem_inc(passed_pool, 1)
                        for h in range(G):
                            ins = nc.gpsimd.tensor_scalar(q_pad[:, g % 2, h, :], q_flat[:, g % 2, :],
                                                          head_mask[:, h:h + 1], 1.0, ALU.mult, ALU.mult)
                        ins.then_inc(q_padded.sem, 1)

                with pool.Fori(0, NB) as b:
                    batch(b)

            @block.scalar
            def _(act):
                for c in (took_act, exped, kept_act, std_ready, sq_ready, var_ready):
                    c.prime(act)
                act.wait_ge(consts_in, 16 * n_consts)
                act.wait_ge(setup, n_setup)

                def batch(b):
                    for kind, i, p in plan:
                        if kind == "turnx" and i == 0:
                            act.wait_ge(chain, b * chain_per["dve"] + chain_at["stats"])
                            nc.scalar.activation(std[:, :], mean_var[:, :, 1], ACT.Sqrt, bias=eps_col[:, 0:1]
                                                 ).then_inc(std_ready.sem, 1)
                        elif kind == "q":
                            act.wait_ge(proj.sem, proj.at(b, p + 1))
                            act.wait_ge(q_padded.sem, q_padded.at(b, i - 1))
                            nc.scalar.activation(q_flat[:, i % 2, :], ps_proj[p % 2][:, 0:queries], ACT.Identity,
                                                 bias=q_bias[:, i:i + 1], scale=scale
                                                 ).then_inc(took_act.sem, 1)
                        elif kind == "k":
                            act.wait_ge(proj.sem, proj.at(b, p + 1))
                            act.wait_ge(scored.sem, scored.at(b, score_end(i - 2)))
                            nc.scalar.activation(k_sb[:, i % 2, :], ps_proj[p % 2][:, 0:keys], ACT.Identity,
                                                 bias=col[:, at_col["k"] + i:at_col["k"] + i + 1]
                                                 ).then_inc(took_act.sem, 1)
                        elif kind == "score":
                            act.wait_ge(maxed.sem, maxed.at(b, i + 1))
                            act.wait_ge(turn_done.sem, turn_done.at(b, i - 2))
                            act.wait_ge(inv_ready.sem, inv_ready.at(b, i // G - 1))
                            src = s_masked[:, i % 3, :] if masked else ps_score[i % 2][:, :]
                            for t in range(II):
                                ins = nc.scalar.activation(
                                    probs[:, i % 3, t * keys:(t + 1) * keys], src[:, t * keys:(t + 1) * keys],
                                    ACT.Exp, bias=neg_max[:, i % 4, t:t + 1],
                                    accum_out=row_sum[:, (i // G) % 2, t, i % G:i % G + 1])
                            ins.then_inc(exped.sem, 1)
                        elif kind == "turn" and i % 2 == 0:
                            act.wait_ge(turn_done.sem, turn_done.at(b, i + 1))
                            act.wait_ge(mix_done.sem, mix_done.at(b, i // G - 1))
                            nc.scalar.activation(turned[:, (i // G) % 2, i % G, :], ps_turn[i % 2][:, :], ACT.Copy
                                                 ).then_inc(kept_act.sem, 1)
                        elif kind == "stat" and i == 0:
                            act.wait_ge(took_dve.sem, took_dve.at(b, dve_items.index(p) + 1))
                            nc.scalar.activation(sq[:, :, :], dev[:, :, :], ACT.Square).then_inc(sq_ready.sem, 1)
                        elif kind == "stat" and i == 1:
                            act.wait_ge(proj.sem, proj.at(b, p + 1))
                            nc.scalar.activation(std_n[:, :], ps_proj[p % 2][:, :], ACT.Sqrt, bias=eps_col[:, 0:1]
                                                 ).then_inc(took_act.sem, 1)

                with act.Fori(0, NB) as b:
                    batch(b)

            @block.vector
            def _(dve):
                for c in (took_dve, maxed, kept_dve, inv_ready, mix_taken, xn_used, normed_out):
                    c.prime(dve)
                dve.wait_ge(setup, n_setup)
                dve.wait_ge(consts_in, 16 * n_consts)

                def batch(b):
                    link = [0]
                    per_chain = chain_per["dve"]

                    def linked(ins, apart=False):
                        link[0] += 1
                        ins.then_inc(chain, 1)
                        dve.wait_ge(chain, b * per_chain + link[0])
                        if apart:
                            dve.sem_inc(passed_dve, 1)

                    for kind, i, p in plan:
                        if kind == "turnx" and i == 0:
                            dve.wait_ge(x_loaded, 16 * b + 16)
                            for t in range(2):
                                last = nc.vector.bn_stats(stats[:, t, :], x_sb[:, t, :])
                            linked(last, apart=True)
                            for t in range(2):
                                last = nc.vector.bn_aggr(mean_var[:, t, :], stats[:, t, :])
                            linked(last)
                            assert link[0] == chain_at["stats"]
                            dve.wait_ge(std_ready.sem, std_ready.at(b, 1))
                            linked(nc.vector.reciprocal(rstd[:, :], std[:, :]))
                            for t in range(2):
                                last = nc.vector.tensor_scalar(xn[:, t, :], x_sb[:, t, :], mean_var[:, t, 0:1],
                                                               rstd[:, t:t + 1], ALU.subtract, ALU.mult)
                            last.then_inc(xn_used.sem, 1)
                        if kind == "turnx":
                            dve.wait_ge(proj.sem, proj.at(b, p + 1))
                            for k in (2 * i, 2 * i + 1):
                                a, c = at_col["ln_w"] + k, at_col["ln_b"] + k
                                last = nc.vector.tensor_scalar(
                                    xt[:, k, :], ps_proj[p % 2][:, (k % 2) * ROWS:(k % 2 + 1) * ROWS],
                                    col[:, a:a + 1], col[:, c:c + 1], ALU.mult, ALU.add)
                            last.then_inc(took_dve.sem, 1)
                        elif kind == "v":
                            j, o = vblocks[i]
                            dve.wait_ge(proj.sem, proj.at(b, p + 1))
                            src = ps_proj[p % 2][:, 0:VN]
                            if HPT > 1:
                                w = TW // HPT
                                dst = v_sb[:, j, :].rearrange("p (t e w) -> p t e w", e=HPT, w=VW)
                                sv = src.rearrange("p (t e w) -> p t e w", e=HPT, w=w)
                                for e in range(HPT):
                                    last = nc.vector.tensor_copy(dst[:, :, e, e * w:(e + 1) * w], sv[:, :, e, :])
                            elif v_row is not None:
                                last = nc.vector.tensor_tensor(v_sb[:, j, o * VN:(o + 1) * VN], src,
                                                               v_bias[:, o * VN:(o + 1) * VN], ALU.add)
                            else:
                                last = nc.vector.tensor_copy(v_sb[:, j, o * VN:(o + 1) * VN], src)
                            last.then_inc(took_dve.sem, 1)
                        elif kind == "score":
                            if masked and i == 0:
                                dve.wait_ge(mask_ready.sem, mask_ready.at(b, 1))
                            dve.wait_ge(scored.sem, scored.at(b, i + 1))
                            dve.wait_ge(exped.sem, exped.at(b, i - 2))
                            if key_mask is not None:
                                dve.sem_inc(passed_dve, 1)
                            s = ps_score[i % 2][:, :].rearrange("p (t k) -> p t k", t=II)
                            if not masked:
                                nc.vector.tensor_reduce(neg_max[:, i % 4, :], s, AX.X, ALU.max, negate=True
                                                        ).then_inc(maxed.sem, 1)
                            else:
                                sm = s_masked[:, i % 3, :].rearrange("p (t k) -> p t k", t=II)
                                if score_mask is not None:
                                    linked(nc.vector.tensor_tensor(sm, s, mask_mul[:, :, :], ALU.mult), apart=True)
                                for t in range(II):
                                    m = mask_add[:, t if score_mask is not None else 0, :]
                                    last = nc.vector.tensor_tensor_reduce(
                                        sm[:, t, :], sm[:, t, :] if score_mask is not None else s[:, t, :], m,
                                        1.0, LOWEST, ALU.add, ALU.max, row_max[:, i % 4, t:t + 1])
                                linked(last)
                                nc.vector.tensor_scalar(neg_max[:, i % 4, :], row_max[:, i % 4, :], -1.0, None,
                                                        ALU.mult).then_inc(maxed.sem, 1)
                        elif kind == "turn":
                            if i % 2 == 1:
                                dve.wait_ge(turn_done.sem, turn_done.at(b, i + 1))
                                dve.wait_ge(mix_done.sem, mix_done.at(b, i // G - 1))
                                nc.vector.tensor_copy(turned[:, (i // G) % 2, i % G, :], ps_turn[i % 2][:, :]
                                                      ).then_inc(kept_dve.sem, 1)
                            if i % G == G - 1:
                                s = i // G
                                dve.wait_ge(exped.sem, exped.at(b, i + 1))
                                dve.wait_ge(mix_done.sem, mix_done.at(b, s - 1))
                                linked(nc.vector.reciprocal(inv_sum[:, s % 2, :, :], row_sum[:, s % 2, :, :]))
                                src = inv_sum[:, s % 2, :, :].unsqueeze(3).to_broadcast([P, II, G, head_dim])
                                dst = inv_wide[:, s % 2, :, :].rearrange("p t (g d) -> p t g d", g=G)
                                nc.vector.tensor_copy(dst, src).then_inc(inv_ready.sem, 1)
                        elif kind == "mix":
                            g, st = divmod(i, SPG)
                            dve.wait_ge(mix_done.sem, mix_done.at(b, i + 1))
                            linked(nc.vector.tensor_copy(inv_cols[:, i % 2, :], ps_mix[i % 2][:, 1, 0:QW]))
                            nc.vector.tensor_tensor(mixed[:, g, st * QW:(st + 1) * QW], ps_mix[i % 2][:, 0, 0:QW],
                                                    inv_cols[:, i % 2, :], ALU.mult).then_inc(mix_taken.sem, 1)
                        elif kind == "out":
                            dve.wait_ge(proj.sem, proj.at(b, p + 1))
                            if i == 0:
                                if out_row is not None:
                                    dve.wait_ge(res_ready.sem, res_ready.at(b, 1))
                                else:
                                    dve.wait_ge(res_loaded, 16 * b + 16)
                                dve.wait_ge(stored, 16 * b + 16)
                            if out_row is not None:
                                last = nc.vector.tensor_tensor(y_sb[:, i, :], ps_proj[p % 2][:, :], res[:, i, :], ALU.add)
                            else:
                                dst = dev if norm_out else y_sb
                                last = nc.vector.scalar_tensor_tensor(
                                    dst[:, i, :], ps_proj[p % 2][:, :], col[:, at_col["o"] + i:at_col["o"] + i + 1],
                                    res[:, i, :], ALU.add, ALU.add)
                            last.then_inc(took_dve.sem, 1)
                        elif kind == "stat" and i == 0:
                            dve.wait_ge(proj.sem, proj.at(b, p + 1))
                            for t in range(2):
                                last = nc.vector.tensor_tensor(dev[:, t, :], dev[:, t, :], ps_proj[p % 2][:, :],
                                                               ALU.subtract)
                            last.then_inc(took_dve.sem, 1)
                        elif kind == "stat" and i == 1:
                            dve.wait_ge(took_act.sem, took_act.at(b, act_items.index(p) + 1))
                            linked(nc.vector.reciprocal(rstd_n[:, :], std_n[:, :]))
                            for t in range(2):
                                last = nc.vector.tensor_tensor(y_sb[:, t, :], dev[:, t, :], rstd_n[:, :], ALU.mult)
                            last.then_inc(normed_out.sem, 1)
                    assert link[0] == per_chain, (link[0], per_chain)

                with dve.Fori(0, NB) as b:
                    batch(b)

            @block.tensor
            def _(pe):
                for c in (proj, scored, turn_done, mix_done):
                    c.prime(pe)
                pe.wait_ge(consts_in, 16 * n_consts)
                pe.wait_ge(setup, n_setup)
                pe.wait_ge(weights_in, 16 * n_weights)

                def bank_free(b, p):
                    q = p - 2
                    which = banks[q % NP]
                    items, c = (act_items, took_act) if which == "act" else (dve_items, took_dve)
                    k = items.index(q % NP) + 1
                    pe.wait_ge(c.sem, c.at(b, k if q >= 0 else k - len(items)))

                def source(kind, k):
                    if kind == "x":
                        return xt[:, k, :] if norm else x_sb[:, k, :]
                    return c_sb[:, k, :]

                def batch(b):
                    seen = set()

                    def loaded(kind):
                        if kind in seen:
                            return
                        seen.add(kind)
                        if kind == "c":
                            pe.wait_ge(c_loaded, 16 * b + 16)
                        elif norm:
                            t = max(q for k, i, q in plan if k == "turnx")
                            pe.wait_ge(took_dve.sem, took_dve.at(b, dve_items.index(t) + 1))
                        else:
                            pe.wait_ge(x_loaded, 16 * b + 16)

                    for kind, i, p in plan:
                        if p is not None:
                            bank_free(b, p)
                            bank = ps_proj[p % 2]
                        if kind == "turnx":
                            pe.wait_ge(xn_used.sem, xn_used.at(b, 1))
                            for k in (2 * i, 2 * i + 1):
                                for t in range(2):
                                    a = (k % 2) * ROWS + t * P
                                    last = nc.tensor.transpose(bank[:, a:a + P], xn[:, t, k * P:(k + 1) * P], ident[:, :])
                            last.then_inc(proj.sem, 1)
                        elif kind in ("q", "k"):
                            w, srcs, chunks = (w_q, sources_q, chunk_q) if kind == "q" else (w_k, sources_kv, chunk_kv)
                            n = queries if kind == "q" else keys
                            hl = n // halves
                            for s in srcs:
                                loaded(s)
                            for h in range(halves):
                                for m, (s, k) in enumerate(zip(srcs, chunks)):
                                    last = nc.tensor.matmul(bank[:, h * hl:(h + 1) * hl],
                                                            w[h][m][:, i * P:(i + 1) * P],
                                                            source(s, k)[:, h * hl:(h + 1) * hl],
                                                            start=(m == 0), stop=(m == len(srcs) - 1))
                            last.then_inc(proj.sem, 1)
                        elif kind == "v":
                            j, o = vblocks[i]
                            h = j * halves // NJ
                            for s in sources_kv:
                                loaded(s)
                            for m, (s, k) in enumerate(zip(sources_kv, chunk_kv)):
                                last = nc.tensor.matmul(bank[:, 0:VN], source(s, k)[:, j * P:(j + 1) * P],
                                                        w_v[h][m][:, o * VN:(o + 1) * VN],
                                                        start=(m == 0), stop=(m == len(sources_kv) - 1))
                            last.then_inc(proj.sem, 1)
                        elif kind == "score":
                            g, r = divmod(i, upg)
                            st, h = divmod(r, G)
                            if r == 0:
                                pe.wait_ge(q_padded.sem, q_padded.at(b, g + 1))
                                kp = next(q for k, gg, q in plan if k == "k" and gg == g)
                                pe.wait_ge(took_act.sem, took_act.at(b, act_items.index(kp) + 1))
                            pe.wait_ge(exped.sem, exped.at(b, i - 1))
                            for t in range(II):
                                a = (st * II + t) * P
                                last = nc.tensor.matmul(ps_score[i % 2][:, t * keys:(t + 1) * keys],
                                                        q_pad[:, g % 2, h, a:a + P], k_sb[:, g % 2, :],
                                                        start=True, stop=True)
                            last.then_inc(scored.sem, 1)
                        elif kind == "turn":
                            pe.wait_ge(exped.sem, exped.at(b, i + 1))
                            j = i - 2
                            which, c = (act_turns, kept_act) if i % 2 == 0 else (dve_turns, kept_dve)
                            pe.wait_ge(c.sem, c.at(b, turns_before(which, j + 1)) if j >= 0 else c.at(b, 0))
                            for t in range(II):
                                for jc in range(NJ):
                                    a = (jc * II + t) * P
                                    last = nc.tensor.transpose(ps_turn[i % 2][:, a:a + P],
                                                               probs[:, i % 3, t * keys + jc * P:t * keys + (jc + 1) * P],
                                                               ident[:, :])
                            last.then_inc(turn_done.sem, 1)
                        elif kind == "mix":
                            g, st = divmod(i, SPG)
                            pe.wait_ge(inv_ready.sem, inv_ready.at(b, i + 1))
                            pe.wait_ge(mix_taken.sem, mix_taken.at(b, i - 1))
                            n = (i + 1) * G
                            pe.wait_ge(kept_act.sem, kept_act.at(b, turns_before(act_turns, n)))
                            pe.wait_ge(kept_dve.sem, kept_dve.at(b, turns_before(dve_turns, n)))
                            if i == 0:
                                v_last = max(q for k, gg, q in plan if k == "v")
                                pe.wait_ge(took_dve.sem, took_dve.at(b, dve_items.index(v_last) + 1))
                            bank = ps_mix[i % 2]
                            for t in range(II):
                                nc.tensor.transpose(bank[:, 1, t * P:(t + 1) * P], inv_wide[:, i % 2, t, :], ident[:, :])
                            steps = [(jc, e) for jc in range(NJ) for e in range(HPT)]
                            for jc, e in steps:
                                for t in range(TILES):
                                    h = t * HPT + e
                                    head = g * G + h
                                    vcols = v_sb[:, jc, head * VW:(head + 1) * VW]
                                    last = nc.tensor.matmul(bank[t * TW:(t + 1) * TW, 0, 0:QW], vcols,
                                                            turned[:, i % 2, h, jc * QW:(jc + 1) * QW],
                                                            start=((jc, e) == steps[0]), stop=((jc, e) == steps[-1]))
                            last.then_inc(mix_done.sem, 1)
                        elif kind == "out":
                            if i == 0:
                                pe.wait_ge(mix_taken.sem, mix_taken.at(b, S))
                            for g in range(NG):
                                if channel_out:
                                    lhs, rhs = w_o[:, g, i * P:(i + 1) * P], mixed[:, g, :]
                                else:
                                    lhs, rhs = mixed[:, g, i * P:(i + 1) * P], w_o[:, g, :]
                                last = nc.tensor.matmul(bank[:, :], lhs, rhs, start=(g == 0), stop=(g == NG - 1))
                            last.then_inc(proj.sem, 1)
                        elif kind == "stat":
                            if i == 0:
                                o = max(q for k, gg, q in plan if k == "out")
                                pe.wait_ge(took_dve.sem, took_dve.at(b, dve_items.index(o) + 1))
                            else:
                                pe.wait_ge(sq_ready.sem, sq_ready.at(b, 1))
                            src = dev if i == 0 else sq
                            for t in range(2):
                                last = nc.tensor.matmul(bank[:, :], ones[:, :], src[:, t, :], start=(t == 0), stop=(t == 1))
                            last.then_inc(proj.sem, 1)

                with pe.Fori(0, NB) as b:
                    batch(b)

        nc.clear_and_free_semaphores(sems)
        nc.all_engine_barrier()


def mlp_stage(nc, name, x_in, x_out, w_up, w_down, out_row, cols, ident_dram):
    cols_dram, at_col, n_cols = cols
    KD = COLS // P
    HC = w_up.shape[1] // P
    NBANK = 4
    plan, banks = [], []

    def bank_item(kind, idx, engine):
        plan.append((kind, idx, len(banks)))
        banks.append(engine)

    for i in range(2):
        bank_item("turnx", i, "dve")
    for i in range(HC // 2):
        bank_item("up", i, "act")
    for i in range(2):
        bank_item("out", i, "dve")
    NP = len(banks)
    act_items = [p for p in range(NP) if banks[p] == "act"]
    dve_items = [p for p in range(NP) if banks[p] == "dve"]
    with ExitStack() as ctx:
        def sb(what, shape, dt=F32):
            return ctx.enter_context(nc.sbuf_tensor(f"{name}_{what}", shape, dt))

        sems = []

        def sem(what):
            sems.append(nc.alloc_semaphore(f"{name}_{what}"))
            return sems[-1]

        ident = sb("ident", [P, P])
        up = sb("up", [P, KD, HC * P])
        down = sb("down", [P, HC, COLS])
        col = sb("cols", [P, n_cols])
        o_bias = sb("o_bias", [P, COLS])
        x_sb = sb("x", [P, 2, COLS])
        res = sb("res", [P, 2, COLS])
        xn = sb("xn", [P, 2, COLS])
        xt = sb("xt", [P, KD, ROWS])
        hidden = sb("hidden", [P, HC, ROWS])
        y_sb = sb("y", [P, 2, COLS])
        stats = sb("stats", [P, 2, 6])
        mean_var = sb("mean_var", [P, 2, 2])
        std = sb("std", [P, 2])
        rstd = sb("rstd", [P, 2])
        eps_col = sb("eps", [P, 1])
        ps_proj = [ctx.enter_context(nc.psum_tensor(f"{name}_proj{i}", [P, BANK], F32)) for i in range(NBANK)]

        weights_in = sem("weights_in")
        consts_in = sem("consts_in")
        x_loaded = sem("x_loaded")
        res_loaded = sem("res_loaded")
        stored = sem("stored")
        setup = sem("setup")
        passed_dve = sem("passed_dve")
        passed_pool = sem("passed_pool")
        chain = sem("dve_chain")
        proj = Count(sem("proj_ready"), NP)
        took_act = Count(sem("proj_taken_act"), len(act_items))
        took_dve = Count(sem("proj_taken_dve"), len(dve_items))
        xn_used = Count(sem("x_normed"), 1)
        std_ready = Count(sem("std_ready"), 1)
        res_ready = Count(sem("residual_ready"), 1)
        CHAIN = 3

        x_src = x_in.rearrange("b (k p) l -> b p k l", p=P)
        y_dst = x_out.rearrange("b (k p) l -> b p k l", p=P)

        with nc.Block() as block:
            @block.sync
            def _(sp):
                sp.dma_start(col[:, :], cols_dram).then_inc(consts_in, 16)
                sp.dma_start(ident[:, :], ident_dram).then_inc(consts_in, 16)
                sp.dma_start(o_bias[:, :], out_row.partition_broadcast(P)).then_inc(consts_in, 16)
                for k in range(KD):
                    sp.dma_start(up[:, k, :], w_up[k * P:(k + 1) * P, :]).then_inc(weights_in, 16)
                sp.dma_start(down[:, :, :], w_down.rearrange("(m p) o -> p m o", p=P)).then_inc(weights_in, 16)
                sp.sem_inc(stored, 16)
                with sp.Fori(0, NB) as b:
                    sp.wait_ge(took_dve.sem, took_dve.at(b, len(dve_items)))
                    sp.dma_start(y_dst[b], y_sb[:, :, :]).then_inc(stored, 16)
                sp.wait_ge(stored, 16 * NB + 16)

            @block.gpsimd
            def _(pool):
                res_ready.prime(pool)
                nc.gpsimd.memset(eps_col[:, :], EPS).then_inc(setup, 1)
                pool.wait_ge(consts_in, 16 * 3)
                with pool.Fori(0, NB) as b:
                    pool.wait_ge(xn_used.sem, xn_used.at(b, 0))
                    pool.sem_inc(passed_pool, 1)
                    pool.dma_start(x_sb[:, :, :], x_src[b]).then_inc(x_loaded, 16)
                    pool.wait_ge(took_dve.sem, took_dve.at(b, 0))
                    pool.sem_inc(passed_pool, 1)
                    pool.dma_start(res[:, :, :], x_src[b]).then_inc(res_loaded, 16)
                    pool.wait_ge(res_loaded, 16 * b + 16)
                    pool.sem_inc(passed_pool, 1)
                    for t in range(2):
                        ins = nc.gpsimd.tensor_tensor(res[:, t, :], res[:, t, :], o_bias[:, :], ALU.add)
                    ins.then_inc(res_ready.sem, 1)

            @block.scalar
            def _(act):
                took_act.prime(act)
                std_ready.prime(act)
                act.wait_ge(consts_in, 16 * 3)
                act.wait_ge(setup, 1)
                with act.Fori(0, NB) as b:
                    for kind, i, p in plan:
                        if kind == "turnx" and i == 0:
                            act.wait_ge(chain, b * CHAIN + 2)
                            nc.scalar.activation(std[:, :], mean_var[:, :, 1], ACT.Sqrt, bias=eps_col[:, 0:1]
                                                 ).then_inc(std_ready.sem, 1)
                        elif kind == "up":
                            act.wait_ge(proj.sem, proj.at(b, p + 1))
                            for e in range(2):
                                m = 2 * i + e
                                c = at_col["up"] + m
                                ins = nc.scalar.activation(hidden[:, m, :], ps_proj[p % NBANK][:, e * ROWS:(e + 1) * ROWS],
                                                           ACT.Gelu_apprx_tanh, bias=col[:, c:c + 1])
                            ins.then_inc(took_act.sem, 1)

            @block.vector
            def _(dve):
                took_dve.prime(dve)
                xn_used.prime(dve)
                dve.wait_ge(consts_in, 16 * 3)
                with dve.Fori(0, NB) as b:
                    dve.wait_ge(x_loaded, 16 * b + 16)
                    for t in range(2):
                        last = nc.vector.bn_stats(stats[:, t, :], x_sb[:, t, :])
                    last.then_inc(chain, 1)
                    dve.wait_ge(chain, b * CHAIN + 1)
                    dve.sem_inc(passed_dve, 1)
                    for t in range(2):
                        last = nc.vector.bn_aggr(mean_var[:, t, :], stats[:, t, :])
                    last.then_inc(chain, 1)
                    dve.wait_ge(std_ready.sem, std_ready.at(b, 1))
                    nc.vector.reciprocal(rstd[:, :], std[:, :]).then_inc(chain, 1)
                    dve.wait_ge(chain, b * CHAIN + 3)
                    for t in range(2):
                        last = nc.vector.tensor_scalar(xn[:, t, :], x_sb[:, t, :], mean_var[:, t, 0:1],
                                                       rstd[:, t:t + 1], ALU.subtract, ALU.mult)
                    last.then_inc(xn_used.sem, 1)
                    for kind, i, p in plan:
                        if kind == "turnx":
                            dve.wait_ge(proj.sem, proj.at(b, p + 1))
                            for k in (2 * i, 2 * i + 1):
                                a, c = at_col["ln_w"] + k, at_col["ln_b"] + k
                                last = nc.vector.tensor_scalar(
                                    xt[:, k, :], ps_proj[p % NBANK][:, (k % 2) * ROWS:(k % 2 + 1) * ROWS],
                                    col[:, a:a + 1], col[:, c:c + 1], ALU.mult, ALU.add)
                            last.then_inc(took_dve.sem, 1)
                        elif kind == "out":
                            if i == 0:
                                dve.wait_ge(res_ready.sem, res_ready.at(b, 1))
                                dve.wait_ge(stored, 16 * b + 16)
                            dve.wait_ge(proj.sem, proj.at(b, p + 1))
                            nc.vector.tensor_tensor(y_sb[:, i, :], ps_proj[p % NBANK][:, :], res[:, i, :], ALU.add
                                                    ).then_inc(took_dve.sem, 1)

            @block.tensor
            def _(pe):
                proj.prime(pe)
                pe.wait_ge(consts_in, 16 * 3)
                pe.wait_ge(weights_in, 16 * (KD + 1))
                with pe.Fori(0, NB) as b:
                    for kind, i, p in plan:
                        q = p - NBANK
                        items, c = (act_items, took_act) if banks[q % NP] == "act" else (dve_items, took_dve)
                        k = items.index(q % NP) + 1
                        pe.wait_ge(c.sem, c.at(b, k if q >= 0 else k - len(items)))
                        bank = ps_proj[p % NBANK]
                        if kind == "turnx":
                            pe.wait_ge(xn_used.sem, xn_used.at(b, 1))
                            for k in (2 * i, 2 * i + 1):
                                for t in range(2):
                                    a = (k % 2) * ROWS + t * P
                                    last = nc.tensor.transpose(bank[:, a:a + P], xn[:, t, k * P:(k + 1) * P], ident[:, :])
                        elif kind == "up":
                            if i == 0:
                                pe.wait_ge(took_dve.sem, took_dve.at(b, 2))
                            for e in range(2):
                                m = 2 * i + e
                                for k in range(KD):
                                    last = nc.tensor.matmul(bank[:, e * ROWS:(e + 1) * ROWS],
                                                            up[:, k, m * P:(m + 1) * P], xt[:, k, :],
                                                            start=(k == 0), stop=(k == KD - 1))
                        else:
                            pe.wait_ge(took_act.sem, took_act.at(b, len(act_items)))
                            for m in range(HC):
                                last = nc.tensor.matmul(bank[:, :], hidden[:, m, i * P:(i + 1) * P], down[:, m, :],
                                                        start=(m == 0), stop=(m == HC - 1))
                        last.then_inc(proj.sem, 1)

        nc.clear_and_free_semaphores(sems)
        nc.all_engine_barrier()


def program(nc, t, out):
    step = [nc.dram_tensor(f"step{i}", (NB, ROWS, COLS), F32).ap() for i in range(6)]
    ctx_c, ctx_t = t["ctx"], t["ctx_t"]

    def rows(name, first, n, c0, c1):
        return [t[name][first + i * P:first + (i + 1) * P, c0:c1] for i in range(n)]

    def cols(name, **at):
        return t[name], at, t[name].shape[1]

    attention_stage(nc, "l0", t["x"], step[0], ctx_c,
                    {"q": [rows("l0_wq", 0, 2, 0, 256)], "k": [rows("l0_wk", 0, 2, 0, 256)],
                     "v": [rows("l0_wv", 0, 2, 0, 256)], "o": t["l0_wo"], "head_mask": t["mask16"]},
                    cols("l0_cols", q=0, k=2, o=4), t["ident"],
                    head_dim=16, queries=512, keys=512, channel_out=True)
    attention_stage(nc, "l1", step[0], step[1], ctx_t,
                    {"q": [rows("l1_wq", 0, 4, 0, 512)], "k": [rows("l1_wk", 0, 4, 0, 512)],
                     "v": [rows("l1_wv", 0, 4, 0, 512)], "o": t["l1_wo"], "head_mask": t["mask32"]},
                    cols("l1_cols", q=0, k=4, ln_w=8, ln_b=12), t["ident"],
                    head_dim=32, queries=256, keys=256, norm=True, key_mask=t["key_mask"],
                    v_row=t["l1_vb"], out_row=t["l1_ob"])
    mlp_stage(nc, "m1", step[1], step[2], t["l1_up"], t["l1_down"], t["l1_db"],
              cols("m1_cols", ln_w=0, ln_b=4, up=8), t["ident"])
    l2 = {}
    for what, c0 in (("q", 0), ("k", 1024), ("v", 2048)):
        l2[what] = [rows(f"l2_z{h}", 0, 2, c0, c0 + 1024) + rows(f"l2_u{h}", 0, 2, c0, c0 + 1024) for h in range(2)]
    attention_stage(nc, "l2", step[2], step[3], ctx_c,
                    {**l2, "o": t["l2_wo"], "head_mask": t["mask64"]},
                    cols("l2_cols", q=0, k=8, o=16), t["ident"],
                    head_dim=64, queries=512, keys=512, halves=2, kv_also_q=True, channel_out=True, norm_out=True)
    causal = t["causal_mask"].rearrange("a c (t p) k -> a c p t k", p=P)
    attention_stage(nc, "l3s", step[3], step[4], None,
                    {"q": [rows("l3_qkv", 0, 4, 0, 512)], "k": [rows("l3_qkv", 0, 4, 512, 1024)],
                     "v": [rows("l3_qkv", 0, 4, 1024, 1536)], "o": t["l3_ao"], "head_mask": t["mask32"]},
                    cols("l3s_cols", q=0, k=4, ln_w=8, ln_b=12), t["ident"],
                    head_dim=32, queries=256, keys=256, norm=True, self_kv=True,
                    score_mask=lambda b: causal[0, 0], v_row=t["l3_svb"], out_row=t["l3_aob"])
    cross = t["cross_mask"].rearrange("b c (t p) k -> b (c p) t k", p=P)
    attention_stage(nc, "l3c", step[4], step[5], ctx_t,
                    {"q": [rows("l3_wq", 0, 4, 0, 512)], "k": [rows("l3_kv", 0, 4, 0, 512)],
                     "v": [rows("l3_kv", 0, 4, 512, 1024)], "o": t["l3_co"], "head_mask": t["mask32"]},
                    cols("l3c_cols", q=0, k=4, ln_w=8, ln_b=12), t["ident"],
                    head_dim=32, queries=256, keys=256, norm=True,
                    score_mask=lambda b: cross[b], v_row=t["l3_cvb"], out_row=t["l3_cob"])
    mlp_stage(nc, "m3", step[5], out, t["l3_up"], t["l3_down"], t["l3_db"],
              cols("m3_cols", ln_w=0, ln_b=4, up=8), t["ident"])


def layout(i):
    import numpy as np

    def a(name):
        return np.asarray(i[name])

    def col(*vectors):
        return np.ascontiguousarray(np.concatenate([v.reshape(-1, P).T for v in vectors], axis=1))

    def turned(m):
        return np.ascontiguousarray(m.T)

    def head_mask(d):
        return np.ascontiguousarray(np.kron(np.eye(P // d, dtype=np.float32), np.ones((d, 1), np.float32)))

    zero = np.zeros
    f = np.float32
    ctx = a("ctx_2048")
    qkv_b, kv_b = a("L3_xattn_b_qkv"), a("L3_xattn_b_kv")
    return {
        "x": a("x"), "ctx": ctx, "ctx_t": np.ascontiguousarray(ctx.transpose(0, 2, 1)),
        "ident": np.eye(P, dtype=f), "mask16": head_mask(16), "mask32": head_mask(32), "mask64": head_mask(64),
        "key_mask": a("mask_BxS2_bf1"), "causal_mask": a("mask_1x1xSxS2_fc1"), "cross_mask": a("mask_Bx1xSxS2_ff1"),
        "l0_wq": turned(a("L0_xattn_Wq")), "l0_wk": turned(a("L0_xattn_Wk")), "l0_wv": turned(a("L0_xattn_Wv")),
        "l0_wo": turned(a("L0_xattn_Wo")), "l0_cols": col(zero(256, f), zero(256, f), a("L0_xattn_bo")),
        "l1_wq": a("L1_xattn_q_w"), "l1_wk": a("L1_xattn_k_w"), "l1_wv": a("L1_xattn_v_w"), "l1_wo": a("L1_xattn_cproj_w"),
        "l1_cols": col(a("L1_xattn_q_b"), a("L1_xattn_k_b"), a("L1_xattn_ln1_w"), a("L1_xattn_ln1_b")),
        "l1_vb": a("L1_xattn_v_b"), "l1_ob": a("L1_xattn_cproj_b"),
        "l1_up": a("L1_xattn_fc_w"), "l1_down": a("L1_xattn_proj_w"), "l1_db": a("L1_xattn_proj_b"),
        "m1_cols": col(a("L1_xattn_ln2_w"), a("L1_xattn_ln2_b"), a("L1_xattn_fc_b")),
        "l2_z0": turned(a("L2_xattn_Wqkv0")), "l2_z1": turned(a("L2_xattn_Wqkv1")),
        "l2_u0": turned(a("L2_xattn_Winj0")), "l2_u1": turned(a("L2_xattn_Winj1")),
        "l2_wo": turned(a("L2_xattn_Wo")),
        "l2_cols": col(a("L2_xattn_r_w_bias").reshape(-1), zero(1024, f), a("L2_xattn_bo")),
        "l3_qkv": a("L3_xattn_w_qkv"), "l3_ao": a("L3_xattn_w_ao"),
        "l3s_cols": col(qkv_b[0:512], qkv_b[512:1024], a("L3_xattn_ln1_s"), a("L3_xattn_ln1_b")),
        "l3_svb": np.ascontiguousarray(qkv_b[1024:1536]), "l3_aob": a("L3_xattn_b_ao"),
        "l3_wq": a("L3_xattn_w_q"), "l3_kv": a("L3_xattn_w_kv"), "l3_co": a("L3_xattn_w_co"),
        "l3c_cols": col(a("L3_xattn_b_q"), kv_b[0:512], a("L3_xattn_ln2_s"), a("L3_xattn_ln2_b")),
        "l3_cvb": np.ascontiguousarray(kv_b[512:1024]), "l3_cob": a("L3_xattn_b_co"),
        "l3_up": a("L3_xattn_w1"), "l3_down": a("L3_xattn_w2"), "l3_db": a("L3_xattn_b2"),
        "m3_cols": col(a("L3_xattn_ln3_s"), a("L3_xattn_ln3_b"), a("L3_xattn_b1")),
    }


def kernel(**inputs):
    import concourse.bacc as bacc
    import numpy as np
    from concourse.bass_utils import run_bass_kernel_spmd

    nc = bacc.Bacc("TRN2", target_bir_lowering=False, num_devices=1)
    arrays = {f"in_{k}": np.ascontiguousarray(v) for k, v in layout(inputs).items()}
    t = {k[3:]: nc.dram_tensor(k, v.shape, mybir.dt.from_np(v.dtype), kind="ExternalInput").ap()
         for k, v in arrays.items()}
    out = nc.dram_tensor("out", (NB, ROWS, COLS), F32, kind="ExternalOutput").ap()
    program(nc, t, out)
    r = run_bass_kernel_spmd(nc, [arrays], core_ids=[0])
    return r.results[0]["out"]
```

```python
from contextlib import ExitStack

import concourse.bass as bass
from concourse import mybir
from concourse.alu_op_type import AluOpType as ALU

F32 = mybir.dt.float32
F32R = mybir.dt.float32r
ACT = mybir.ActivationFunctionType
AX = mybir.AxisListType

P = 128
NB = 8
ROWS = 256
COLS = 512
BANK = 512
EPS = 1e-5
KEY_MASKED = -3.0e38
LOWEST = -3.4e38
TURN_LAG = 2
MIX_LAG = 4


class Count:

    def __init__(self, sem, per):
        self.sem, self.per = sem, per


def wait(eng, count, b, k, back=0):
    value = b * count.per + (k - back * count.per)
    if not (isinstance(value, int) and value <= 0):
        eng.wait_ge(count.sem, value)


def iterations(eng, run):
    run(0, True, False)
    with eng.Fori(1, NB) as b:
        run(b, False, False)
    run(NB, False, True)


def raw(ap):
    return ap.bitcast(F32)


def product(nc, out, lhs, rhs, start, stop):
    nc.tensor.matmul(out, lhs[0], rhs[0], start=start, stop=False)
    nc.tensor.matmul(out, lhs[0], rhs[1], start=False, stop=False)
    return nc.tensor.matmul(out, lhs[1], rhs[0], start=False, stop=stop)


def attention_stage(nc, name, x_in, x_out, kv_in, weights, cols, ident_dram, *, head_dim, queries,
                    keys, halves=1, norm=False, self_kv=False, kv_also_q=False, key_mask=None,
                    fixed_mask=None, score_mask=None, channel_out=False, v_row=None, out_row=None,
                    norm_out=False, res_in=None):
    cols_dram, at_col, n_cols = cols
    NG = weights["o"].shape[0] // P
    CH = NG * P
    OW = weights["o"].shape[1]
    G = P // head_dim
    H = NG * G
    NI = queries // P
    NJ = keys // P
    II = BANK // keys
    SPG = NI // II
    QW = II * P
    UPG = SPG * G
    U = UPG * NG
    S = SPG * NG
    TILES = min(G, 4)
    TW = P // TILES
    HPT = G // TILES
    VN = min(CH, BANK)
    NV = NJ * (CH // VN)
    KX = 4 if norm else 2
    KC = 0 if self_kv else kv_in.shape[1] // P
    scale = float(head_dim) ** -0.5
    from_x = [("x", k) for k in range(KX)]
    from_c = [("c", k) for k in range(KC)]
    q_from = from_x + (from_c if kv_also_q else [])
    kv_from = q_from if (self_kv or kv_also_q) else from_c
    masked = key_mask is not None or fixed_mask is not None or score_mask is not None

    plan = []
    fill = {}
    if self_kv or kv_also_q:
        fill = {0: [("stats", 0)] if norm else [("split", "x"), ("split", "c")],
                1: [("norm", 0), ("turnx", 0), ("turnx", 1), ("xsplit", 0), ("xsplit", 1)] if norm else [],
                3: [("q", 0)]}
    else:
        fill = {0: [("split", "c")] + ([("stats", 0)] if norm else [("split", "x")]),
                1: [("norm", 0)] if norm else [],
                2: [("turnx", 0), ("turnx", 1), ("xsplit", 0), ("xsplit", 1)] if norm else [],
                3: [("q", 0)]}
    first = U - UPG
    for j in range(UPG + MIX_LAG + 2):
        if j < UPG:
            plan.append(("score", first + j, 1))
        plan += [(kind, i, 0) for kind, i in fill.get(j, [])]
        if j - TURN_LAG < UPG:
            plan.append(("turn", first + j - TURN_LAG, 1))
        if j == UPG:
            plan.append(("mask", 0, 0))
            plan.append(("k", 0, 0))
        m = first + j - MIX_LAG
        if m < U and m % G == G - 1:
            plan.append(("mix", m // G, 1))
        if m <= U and m % G == 0:
            plan.append(("keep", m // G - 1, 1))
    plan += [("v", i, 0) for i in range(NV)]
    plan += [("out", 0, 1), ("out", 1, 1), ("res", 0, 0)]
    for n in range(first):
        g, r = divmod(n, UPG)
        if r == 0:
            plan.append(("q", g + 1, 0))
        plan.append(("score", n, 0))
        if r == 0:
            plan.append(("k", g + 1, 0))
        if n >= TURN_LAG:
            plan.append(("turn", n - TURN_LAG, 0))
        if norm_out and n in (1, 4, 7):
            plan.append(("stat", (1, 4, 7).index(n), 1))
        m = n - MIX_LAG
        if m >= 0 and m % G == G - 1:
            plan.append(("mix", m // G, 0))
        if m > 0 and m % G == 0:
            plan.append(("keep", m // G - 1, 0))

    bank_users = [x for x, (kind, i, _) in enumerate(plan)
                  if kind in ("q", "k", "v", "turnx") or (kind == "stat" and i < 2)]
    assert len(bank_users) % 2 == 0
    bank_of = {x: n % 2 for n, x in enumerate(bank_users)}
    in_items = [plan[x][:2] for x in bank_users if plan[x][0] != "stat"]
    in_dve_items = [it for it in in_items if it[0] != "q"]

    with ExitStack() as ctx:
        def sb(what, shape, dt=F32):
            return ctx.enter_context(nc.sbuf_tensor(f"{name}_{what}", shape, dt))

        def pair(what, shape):
            return sb(what + "_high", shape, F32R), sb(what + "_low", shape, F32R)

        sems = []

        def sem(what):
            sems.append(nc.alloc_semaphore(f"{name}_{what}"))
            return sems[-1]

        def count(what, per):
            return Count(sem(what), per)

        ident = sb("ident", [P, P])
        col = sb("cols", [P, n_cols])
        head_mask = sb("head_mask", [P, G])
        w = {"q": pair("wq", [P, halves * len(q_from), CH]), "k": pair("wk", [P, halves * len(kv_from), CH]),
             "v": pair("wv", [P, halves * len(kv_from), CH]), "o": pair("wo", [P, NG, OW])}
        x_raw = sb("x_raw", [P, 2, COLS])
        res = sb("res", [P, 2, COLS])
        if norm:
            xn = sb("xn", [P, 2, COLS])
            xt32 = sb("xt32", [P, 4, ROWS])
            x2 = pair("x", [P, 4, ROWS])
            stats = sb("stats", [P, 2, 6])
            mean_var = sb("mean_var", [P, 2, 2])
            std = sb("std", [P, 2])
            rstd = sb("rstd", [P, 2])
        else:
            x2 = pair("x", [P, 2, COLS])
        if not self_kv:
            c_raw = sb("c_raw", [P, KC, keys])
            c2 = pair("c", [P, KC, keys])
        q_flat = sb("q_flat", [P, queries])
        q_part = sb("q_part", [P, queries], F32R)
        q2 = pair("q", [P, 2, G, queries])
        k2 = pair("k", [P, 2, keys])
        v_sb = sb("v", [P, NJ, H * TW if HPT > 1 else CH])
        probs = sb("probs", [P, 3, BANK])
        turned = sb("turned", [P, 2, G, BANK])
        neg_max = sb("neg_max", [P, 4, II])
        row_sum = sb("row_sum", [P, 2, II, G])
        inv_sum = sb("inv_sum", [P, 2, II, G])
        inv_wide = sb("inv_wide", [P, 2, II, P])
        inv_cols = sb("inv_cols", [P, QW])
        mixed32 = sb("mixed32", [P, 2, QW])
        mixed2 = pair("mixed", [P, NG, queries])
        y_sb = sb("y", [P, 2, COLS])
        eps_col = sb("eps", [P, 1])
        q_bias = sb("q_bias", [P, NG])
        if v_row is not None:
            v_bias = sb("v_bias", [P, CH])
        if out_row is not None:
            o_bias = sb("o_bias", [P, COLS])
        if key_mask is not None:
            mask_next = sb("mask_next", [P, keys], key_mask.dtype)
            mask_add = sb("mask_add", [P, 1, keys])
        elif masked:
            mask_mul = sb("mask_mul", [P, II, keys])
            mask_add = sb("mask_add", [P, II, keys])
            if score_mask is not None:
                mask_next = sb("mask_next", [P, II, keys])
        if masked:
            s_masked = sb("s_masked", [P, 3, BANK])
            row_max = sb("row_max", [P, 4, II])
        if norm_out:
            ones = sb("ones", [P, P])
            sq = y_sb
            std_n = sb("std_n", [P, COLS])
        STAGING = 4
        stage_of = turned[:, :, :, :].rearrange("p a g n -> p (a g) n")

        def ps(what, shape):
            return ctx.enter_context(nc.psum_tensor(f"{name}_{what}", shape, F32))

        ps_in = [ps(f"in{i}", [P, BANK]) for i in range(2)]
        ps_score = [ps(f"score{i}", [P, BANK]) for i in range(2)]
        ps_turn = [ps(f"turn{i}", [P, BANK]) for i in range(2)]
        ps_mix = [ps(f"mix{i}", [P, 2, BANK // 2]) for i in range(2)]

        w_loaded = [sem(f"weights_loaded{i}") for i in range(STAGING)]
        consts_in, x_loaded, c_loaded = sem("consts_in"), sem("x_loaded"), sem("c_loaded")
        res_loaded, mask_loaded = sem("res_loaded"), sem("mask_loaded")
        stored, setup = sem("stored"), sem("setup")
        passed_dve, passed_pool, passed_sp = sem("passed_dve"), sem("passed_pool"), sem("passed_sp")
        w_high, w_low = sem("weights_high"), sem("weights_low")
        in_ready = count("projected", len(in_items))
        scored, turned_ready, mix_ready = count("scored", U), count("turned", U), count("mixed", S + 2)
        stat_ready = count("stat_ready", 2)
        in_act, in_dve = count("in_taken_act", NG), count("in_taken_dve", len(in_dve_items))
        kept_act, kept_dve = count("turned_kept_act", U // 2), count("turned_kept_dve", U // 2)
        mix_taken, stat_taken = count("mix_taken", S + 2), count("stat_taken", 2)
        exped, maxed, inv_ready = count("exped", U), count("maxed", U), count("inverted", S)
        k_high, q_padded = count("k_high", NG), count("q_padded", NG)
        mixed_high, mixed_low = count("mixed_high", S), count("mixed_low", S)
        NXS = 2 if norm else 1
        x_high, x_low = count("x_high", NXS), count("x_low", NXS)
        c_high, c_low = count("c_high", 1), count("c_low", 1)
        mv_ready, std_ready, xn_ready = count("mean_var", 1), count("std", 1), count("x_normed", 1)
        res_ready, mask_ready = count("res_ready", 1), count("mask_ready", 1)
        sq_ready, std_n_ready, normed_out = count("squares", 1), count("std_n", 1), count("normed_out", 1)
        dve_chain = count("dve_chain", (2 if norm else 0) + 2 * S + (1 if norm_out else 0)
                          + (0 if not masked else U if key_mask is not None else 2 * U))
        pool_chain = count("pool_chain", 2 * NG + (1 if key_mask is not None else 0))
        n_setup = 2 + (1 if norm_out else 0) + (1 if HPT > 1 else 0) + (1 if fixed_mask is not None else 0)
        n_consts = 3 + (v_row is not None) + (out_row is not None) + (fixed_mask is not None)
        y_done, y_signals = (normed_out, 1) if norm_out else (mix_taken, S + 2)

        x_src = x_in.rearrange("b (k p) l -> b p k l", p=P)
        r_src = (x_in if res_in is None else res_in).rearrange("b (k p) l -> b p k l", p=P)
        y_dst = x_out.rearrange("b (k p) l -> b p k l", p=P)
        if not self_kv:
            c_src = kv_in.rearrange("b (k p) l -> b p k l", p=P)

        pieces = []
        for which, n_from in (("k", len(kv_from)), ("q", len(q_from)), ("v", len(kv_from))):
            for h in range(halves):
                for i in range(n_from):
                    pieces.append((which, h * n_from + i, weights[which][h][i]))
        for g in range(NG):
            pieces.append(("o", g, weights["o"][g * P:(g + 1) * P, :]))

        def pieces_through(which):
            return max(n for n, (kind, _, _) in enumerate(pieces) if kind == which) + 1

        def steps(first, last):
            for x, (kind, i, back) in enumerate(plan):
                if not (first and back) and not (last and not back):
                    yield x, kind, i, back

        with nc.Block() as block:
            @block.sync
            def _(sp):
                sp.dma_start(x_raw[:, :, :], x_src[0]).then_inc(x_loaded, 16)
                if not self_kv:
                    sp.dma_start(c_raw[:, :, :], c_src[0]).then_inc(c_loaded, 16)
                sp.dma_start(head_mask[:, :], weights["head_mask"]).then_inc(consts_in, 16)
                sp.dma_start(col[:, :], cols_dram).then_inc(consts_in, 16)
                sp.dma_start(ident[:, :], ident_dram).then_inc(consts_in, 16)
                if v_row is not None:
                    sp.dma_start(v_bias[:, :], v_row.partition_broadcast(P)).then_inc(consts_in, 16)
                if out_row is not None:
                    sp.dma_start(o_bias[:, :], out_row.partition_broadcast(P)).then_inc(consts_in, 16)
                if fixed_mask is not None:
                    sp.dma_start(mask_mul[:, :, :], fixed_mask).then_inc(consts_in, 16)
                for n, (which, block_i, src) in enumerate(pieces):
                    if n >= STAGING:
                        sp.wait_ge(w_low, n - STAGING + 1)
                    sp.dma_start(stage_of[:, n % STAGING, 0:src.shape[1]], src).then_inc(w_loaded[n % STAGING], 16)
                sp.sem_inc(stored, 16)

                def mask_load(b):
                    if key_mask is not None:
                        sp.dma_start(mask_next[:, :], key_mask[b].partition_broadcast(P)).then_inc(mask_loaded, 16)
                    elif score_mask is not None:
                        sp.dma_start(mask_next[:, :, :], score_mask(b)).then_inc(mask_loaded, 16)

                mask_load(0)
                sp.dma_start(res[:, :, :], r_src[0]).then_inc(res_loaded, 16)
                with sp.Fori(1, NB) as b:
                    if norm:
                        wait(sp, xn_ready, b, 0)
                    else:
                        wait(sp, x_low, b, 0)
                    sp.dma_start(x_raw[:, :, :], x_src[b]).then_inc(x_loaded, 16)
                    if not self_kv:
                        wait(sp, c_low, b, 0)
                        sp.dma_start(c_raw[:, :, :], c_src[b]).then_inc(c_loaded, 16)
                    if key_mask is not None or score_mask is not None:
                        wait(sp, mask_ready, b, 0)
                        sp.sem_inc(passed_sp, 1)
                        mask_load(b)
                    wait(sp, y_done, b, y_signals, back=1)
                    sp.dma_start(y_dst[b - 1], y_sb[:, :, :]).then_inc(stored, 16)
                    sp.dma_start(res[:, :, :], r_src[b]).then_inc(res_loaded, 16)
                wait(sp, y_done, NB, y_signals, back=1)
                sp.dma_start(y_dst[NB - 1], y_sb[:, :, :]).then_inc(stored, 16)
                sp.wait_ge(stored, 16 * NB + 16)

            @block.gpsimd
            def _(pool):
                nc.gpsimd.memset(eps_col[:, :], EPS).then_inc(setup, 1)
                if norm_out:
                    nc.gpsimd.memset(ones[:, :], 1.0 / ROWS).then_inc(setup, 1)
                if HPT > 1:
                    nc.gpsimd.memset(v_sb[:, :, :], 0.0).then_inc(setup, 1)
                pool.wait_ge(consts_in, 16 * n_consts)
                nc.gpsimd.tensor_scalar(q_bias[:, :], col[:, at_col["q"]:at_col["q"] + NG], scale, 1.0,
                                        ALU.mult, ALU.mult).then_inc(setup, 1)
                if fixed_mask is not None:
                    nc.gpsimd.tensor_scalar(mask_add[:, :, :], mask_mul[:, :, :], 10000.0, -10000.0,
                                            ALU.mult, ALU.add).then_inc(setup, 1)

                def run(b, first, last):
                    link = [0]

                    def linked(ins):
                        link[0] += 1
                        ins.then_inc(pool_chain.sem, 1)
                        wait(pool, pool_chain, b, link[0])
                        pool.sem_inc(passed_pool, 1)

                    for _, kind, i, back in steps(first, last):
                        if kind == "q":
                            wait(pool, in_act, b, i + 1)
                            wait(pool, scored, b, (i - 1) * UPG)
                            pool.sem_inc(passed_pool, 1)
                            flat = q_flat[:, :]
                            linked(nc.gpsimd.tensor_scalar(q_part[:, :], flat, 1.0, 1.0, ALU.mult, ALU.mult))
                            for h in range(G):
                                nc.gpsimd.tensor_scalar(q2[0][:, i % 2, h, :], flat, head_mask[:, h:h + 1], 1.0,
                                                        ALU.mult, ALU.mult)
                            linked(nc.gpsimd.tensor_tensor(q_part[:, :], flat, raw(q_part[:, :]), ALU.subtract))
                            for h in range(G):
                                ins = nc.gpsimd.tensor_scalar(q2[1][:, i % 2, h, :], raw(q_part[:, :]),
                                                              head_mask[:, h:h + 1], 1.0, ALU.mult, ALU.mult)
                            ins.then_inc(q_padded.sem, 1)
                        elif kind == "mask" and (key_mask is not None or score_mask is not None):
                            pool.wait_ge(mask_loaded, 16 * b + 16)
                            wait(pool, maxed, b, 0)
                            pool.sem_inc(passed_pool, 1)
                            if key_mask is not None:
                                linked(nc.gpsimd.tensor_copy(mask_add[:, 0, :], mask_next[:, :]))
                                nc.gpsimd.tensor_scalar(mask_add[:, 0, :], mask_add[:, 0, :], -KEY_MASKED,
                                                        KEY_MASKED, ALU.mult, ALU.add).then_inc(mask_ready.sem, 1)
                            else:
                                nc.gpsimd.tensor_scalar(mask_mul[:, :, :], mask_next[:, :, :], 1.0, 1.0,
                                                        ALU.mult, ALU.mult)
                                nc.gpsimd.tensor_scalar(mask_add[:, :, :], mask_next[:, :, :], 10000.0, -10000.0,
                                                        ALU.mult, ALU.add).then_inc(mask_ready.sem, 1)
                        elif kind == "res" and out_row is not None:
                            pool.wait_ge(res_loaded, 16 * b + 16)
                            pool.sem_inc(passed_pool, 1)
                            for t in range(2):
                                ins = nc.gpsimd.tensor_tensor(res[:, t, :], res[:, t, :], o_bias[:, :], ALU.add)
                            ins.then_inc(res_ready.sem, 1)

                iterations(pool, run)

            @block.scalar
            def _(act):
                for n, (which, i, src) in enumerate(pieces):
                    act.wait_ge(w_loaded[n % STAGING], 16 * (n // STAGING + 1))
                    nc.scalar.activation(w[which][0][:, i, :], stage_of[:, n % STAGING, 0:src.shape[1]], ACT.Copy
                                         ).then_inc(w_high, 1)
                act.wait_ge(consts_in, 16 * n_consts)
                act.wait_ge(setup, n_setup)

                def run(b, first, last):
                    for x, kind, i, back in steps(first, last):
                        if kind == "split":
                            src, dst, loaded, high = ((x_raw, x2, x_loaded, x_high) if i == "x"
                                                      else (c_raw, c2, c_loaded, c_high))
                            act.wait_ge(loaded, 16 * b + 16)
                            wait(act, in_ready, b, 0)
                            nc.scalar.activation(dst[0][:, :, :], src[:, :, :], ACT.Copy).then_inc(high.sem, 1)
                        elif kind == "norm":
                            wait(act, mv_ready, b, 1)
                            nc.scalar.activation(std[:, :], mean_var[:, :, 1], ACT.Sqrt, bias=eps_col[:, 0:1]
                                                 ).then_inc(std_ready.sem, 1)
                        elif kind == "xsplit":
                            wait(act, in_dve, b, in_dve_items.index(("turnx", i)) + 1)
                            wait(act, in_ready, b, 0)
                            nc.scalar.activation(x2[0][:, 2 * i:2 * i + 2, :], xt32[:, 2 * i:2 * i + 2, :], ACT.Copy
                                                 ).then_inc(x_high.sem, 1)
                        elif kind == "q":
                            wait(act, in_ready, b, in_items.index((kind, i)) + 1)
                            wait(act, q_padded, b, i)
                            nc.scalar.activation(q_flat[:, :], ps_in[bank_of[x]][:, 0:queries], ACT.Identity,
                                                 bias=q_bias[:, i:i + 1], scale=scale).then_inc(in_act.sem, 1)
                        elif kind == "k":
                            wait(act, in_ready, b, in_items.index((kind, i)) + 1)
                            wait(act, scored, b, (i - 1) * UPG)
                            c = at_col["k"] + i
                            nc.scalar.activation(k2[0][:, i % 2, :], ps_in[bank_of[x]][:, 0:keys], ACT.Identity,
                                                 bias=col[:, c:c + 1]).then_inc(k_high.sem, 1)
                        elif kind == "score":
                            wait(act, maxed, b, i + 1, back)
                            wait(act, turned_ready, b, i - 2, back)
                            wait(act, inv_ready, b, i // G - 1, back)
                            src = s_masked[:, i % 3, :] if masked else ps_score[i % 2][:, :]
                            for t in range(II):
                                ins = nc.scalar.activation(
                                    probs[:, i % 3, t * keys:(t + 1) * keys], src[:, t * keys:(t + 1) * keys],
                                    ACT.Exp, bias=neg_max[:, i % 4, t:t + 1],
                                    accum_out=row_sum[:, (i // G) % 2, t, i % G:i % G + 1])
                            ins.then_inc(exped.sem, 1)
                        elif kind == "turn" and i % 2 == 0:
                            wait(act, turned_ready, b, i + 1, back)
                            wait(act, mix_ready, b, i // G - 1, back)
                            nc.scalar.activation(turned[:, (i // G) % 2, i % G, :], ps_turn[i % 2][:, :], ACT.Copy
                                                 ).then_inc(kept_act.sem, 1)
                        elif kind == "keep":
                            g, st = divmod(i, SPG)
                            wait(act, mix_taken, b, i + 1, back)
                            nc.scalar.activation(mixed2[0][:, g, st * QW:(st + 1) * QW], mixed32[:, i % 2, :],
                                                 ACT.Copy).then_inc(mixed_high.sem, 1)
                        elif kind == "stat" and i == 0:
                            act.wait_ge(stored, b * 16)
                            wait(act, stat_taken, b, 1, back)
                            nc.scalar.activation(sq[:, :, :], res[:, :, :], ACT.Square).then_inc(sq_ready.sem, 1)
                        elif kind == "stat" and i == 1:
                            wait(act, stat_taken, b, 2, back)
                            nc.scalar.activation(std_n[:, :], std_n[:, :], ACT.Sqrt).then_inc(std_n_ready.sem, 1)

                iterations(act, run)

            @block.vector
            def _(dve):
                for n, (which, i, src) in enumerate(pieces):
                    dve.wait_ge(w_high, n + 1)
                    nc.vector.tensor_tensor(w[which][1][:, i, :], stage_of[:, n % STAGING, 0:src.shape[1]],
                                            raw(w[which][0][:, i, :]), ALU.subtract).then_inc(w_low, 1)
                dve.wait_ge(consts_in, 16 * n_consts)
                dve.wait_ge(setup, n_setup)
                chained = {}

                def run(b, first, last):
                    done = [0]

                    def linked(ins, back, apart=False):
                        done[0] += 1
                        ins.then_inc(dve_chain.sem, 1)
                        left = chained.get("first", 0)
                        value = done[0] if first else b * dve_chain.per + (done[0] + left - dve_chain.per)
                        dve.wait_ge(dve_chain.sem, value)
                        if apart:
                            dve.sem_inc(passed_dve, 1)

                    for x, kind, i, back in steps(first, last):
                        if kind == "split":
                            src, dst, high, low = ((x_raw, x2, x_high, x_low) if i == "x"
                                                   else (c_raw, c2, c_high, c_low))
                            wait(dve, high, b, 1)
                            nc.vector.tensor_tensor(dst[1][:, :, :], src[:, :, :], raw(dst[0][:, :, :]), ALU.subtract
                                                    ).then_inc(low.sem, 1)
                        elif kind == "stats":
                            dve.wait_ge(x_loaded, 16 * b + 16)
                            for t in range(2):
                                ins = nc.vector.bn_stats(stats[:, t, :], x_raw[:, t, :])
                            linked(ins, back, apart=True)
                            for t in range(2):
                                ins = nc.vector.bn_aggr(mean_var[:, t, :], stats[:, t, :])
                            ins.then_inc(mv_ready.sem, 1)
                        elif kind == "norm":
                            wait(dve, std_ready, b, 1)
                            linked(nc.vector.reciprocal(rstd[:, :], std[:, :]), back)
                            for t in range(2):
                                ins = nc.vector.tensor_scalar(xn[:, t, :], x_raw[:, t, :], mean_var[:, t, 0:1],
                                                              rstd[:, t:t + 1], ALU.subtract, ALU.mult)
                            ins.then_inc(xn_ready.sem, 1)
                        elif kind == "turnx":
                            wait(dve, in_ready, b, in_items.index((kind, i)) + 1)
                            for k in (2 * i, 2 * i + 1):
                                a, c = at_col["ln_w"] + k, at_col["ln_b"] + k
                                ins = nc.vector.tensor_scalar(
                                    xt32[:, k, :], ps_in[bank_of[x]][:, (k % 2) * ROWS:(k % 2 + 1) * ROWS],
                                    col[:, a:a + 1], col[:, c:c + 1], ALU.mult, ALU.add)
                            ins.then_inc(in_dve.sem, 1)
                        elif kind == "xsplit":
                            wait(dve, x_high, b, i + 1)
                            nc.vector.tensor_tensor(x2[1][:, 2 * i:2 * i + 2, :], xt32[:, 2 * i:2 * i + 2, :],
                                                    raw(x2[0][:, 2 * i:2 * i + 2, :]), ALU.subtract
                                                    ).then_inc(x_low.sem, 1)
                        elif kind == "k":
                            wait(dve, k_high, b, i + 1)
                            c = at_col["k"] + i
                            nc.vector.scalar_tensor_tensor(k2[1][:, i % 2, :], ps_in[bank_of[x]][:, 0:keys],
                                                           col[:, c:c + 1], raw(k2[0][:, i % 2, :]), ALU.add,
                                                           ALU.subtract).then_inc(in_dve.sem, 1)
                        elif kind == "v":
                            j, o = i % NJ, i // NJ
                            wait(dve, in_ready, b, in_items.index((kind, i)) + 1)
                            wait(dve, mix_ready, b, -2)
                            src = ps_in[bank_of[x]][:, 0:VN]
                            if HPT > 1:
                                wide = TW // HPT
                                dst = v_sb[:, j, :].rearrange("p (t e w) -> p t e w", e=HPT, w=TW)
                                sv = src.rearrange("p (t e w) -> p t e w", e=HPT, w=wide)
                                for e in range(HPT):
                                    ins = nc.vector.tensor_copy(dst[:, :, e, e * wide:(e + 1) * wide], sv[:, :, e, :])
                            elif v_row is not None:
                                ins = nc.vector.tensor_tensor(v_sb[:, j, o * VN:(o + 1) * VN], src,
                                                              v_bias[:, o * VN:(o + 1) * VN], ALU.add)
                            else:
                                ins = nc.vector.tensor_copy(v_sb[:, j, o * VN:(o + 1) * VN], src)
                            ins.then_inc(in_dve.sem, 1)
                        elif kind == "score":
                            if i == 0 and (key_mask is not None or score_mask is not None):
                                wait(dve, mask_ready, b, 1)
                            wait(dve, scored, b, i + 1, back)
                            wait(dve, exped, b, i - 2, back)
                            if key_mask is not None:
                                dve.sem_inc(passed_dve, 1)
                            s = ps_score[i % 2][:, :].rearrange("p (t k) -> p t k", t=II)
                            if not masked:
                                nc.vector.tensor_reduce(neg_max[:, i % 4, :], s, AX.X, ALU.max, negate=True
                                                        ).then_inc(maxed.sem, 1)
                            else:
                                sm = s_masked[:, i % 3, :].rearrange("p (t k) -> p t k", t=II)
                                if key_mask is None:
                                    linked(nc.vector.tensor_tensor(sm, s, mask_mul[:, :, :], ALU.mult), back, apart=True)
                                for t in range(II):
                                    ins = nc.vector.tensor_tensor_reduce(
                                        sm[:, t, :], s[:, t, :] if key_mask is not None else sm[:, t, :],
                                        mask_add[:, 0 if key_mask is not None else t, :],
                                        1.0, LOWEST, ALU.add, ALU.max, row_max[:, i % 4, t:t + 1])
                                linked(ins, back)
                                nc.vector.tensor_scalar(neg_max[:, i % 4, :], row_max[:, i % 4, :], -1.0, None,
                                                        ALU.mult).then_inc(maxed.sem, 1)
                        elif kind == "turn":
                            if i % 2 == 1:
                                wait(dve, turned_ready, b, i + 1, back)
                                wait(dve, mix_ready, b, i // G - 1, back)
                                nc.vector.tensor_copy(turned[:, (i // G) % 2, i % G, :], ps_turn[i % 2][:, :]
                                                      ).then_inc(kept_dve.sem, 1)
                            if i % G == G - 1:
                                s = i // G
                                wait(dve, exped, b, i + 1, back)
                                wait(dve, mix_ready, b, s - 1, back)
                                linked(nc.vector.reciprocal(inv_sum[:, s % 2, :, :], row_sum[:, s % 2, :, :]), back)
                                src = inv_sum[:, s % 2, :, :].unsqueeze(3).to_broadcast([P, II, G, head_dim])
                                dst = inv_wide[:, s % 2, :, :].rearrange("p t (g d) -> p t g d", g=G)
                                nc.vector.tensor_copy(dst, src).then_inc(inv_ready.sem, 1)
                        elif kind == "mix":
                            wait(dve, mix_ready, b, i + 1, back)
                            wait(dve, mix_taken, b, i, back)
                            linked(nc.vector.tensor_copy(inv_cols[:, :], ps_mix[i % 2][:, 1, 0:QW]), back)
                            wait(dve, mixed_low, b, i - 1, back)
                            nc.vector.tensor_tensor(mixed32[:, i % 2, :], ps_mix[i % 2][:, 0, 0:QW],
                                                    inv_cols[:, :], ALU.mult).then_inc(mix_taken.sem, 1)
                        elif kind == "keep":
                            g, st = divmod(i, SPG)
                            at = slice(st * QW, (st + 1) * QW)
                            wait(dve, mixed_high, b, i + 1, back)
                            nc.vector.tensor_tensor(mixed2[1][:, g, at], mixed32[:, i % 2, :],
                                                    raw(mixed2[0][:, g, at]), ALU.subtract).then_inc(mixed_low.sem, 1)
                        elif kind == "out":
                            wait(dve, mix_ready, b, S + i + 1, back)
                            ps_out = ps_mix[i % 2][:, :, :].rearrange("p a n -> p (a n)")
                            if i == 0:
                                if out_row is not None:
                                    wait(dve, res_ready, b, 1, back)
                                else:
                                    dve.wait_ge(res_loaded, b * 16)
                                dve.wait_ge(stored, b * 16)
                            dst = res if norm_out else y_sb
                            if "o" in at_col:
                                c = at_col["o"] + i
                                ins = nc.vector.scalar_tensor_tensor(dst[:, i, :], ps_out, col[:, c:c + 1],
                                                                     res[:, i, :], ALU.add, ALU.add)
                            else:
                                ins = nc.vector.tensor_tensor(dst[:, i, :], ps_out, res[:, i, :], ALU.add)
                            ins.then_inc(mix_taken.sem, 1)
                        elif kind == "stat" and i == 0:
                            wait(dve, stat_ready, b, 1, back)
                            for t in range(2):
                                ins = nc.vector.tensor_tensor(res[:, t, :], res[:, t, :], ps_in[bank_of[x]][:, :],
                                                              ALU.subtract)
                            ins.then_inc(stat_taken.sem, 1)
                        elif kind == "stat" and i == 1:
                            wait(dve, stat_ready, b, 2, back)
                            nc.vector.tensor_scalar(std_n[:, :], ps_in[bank_of[x]][:, :], 1.0, EPS, ALU.mult, ALU.add
                                                    ).then_inc(stat_taken.sem, 1)
                        elif kind == "stat" and i == 2:
                            wait(dve, std_n_ready, b, 1, back)
                            linked(nc.vector.reciprocal(std_n[:, :], std_n[:, :]), back)
                            for t in range(2):
                                ins = nc.vector.tensor_tensor(y_sb[:, t, :], res[:, t, :], std_n[:, :], ALU.mult)
                            ins.then_inc(normed_out.sem, 1)
                    if first:
                        chained["first"] = done[0]

                iterations(dve, run)

            @block.tensor
            def _(pe):
                pe.wait_ge(consts_in, 16 * n_consts)
                pe.wait_ge(setup, n_setup)

                def bank_free(x, b, first, last):
                    n = bank_users.index(x) - 2
                    while n >= 0 and (first if plan[bank_users[n]][2] else last):
                        n -= 2
                    kind, i, back = plan[bank_users[n]]
                    assert n >= 0 or not back
                    back += 1 if n < 0 else 0
                    if kind == "stat":
                        wait(pe, stat_taken, b, i + 1, back)
                    elif kind == "q":
                        wait(pe, in_act, b, i + 1, back)
                    else:
                        wait(pe, in_dve, b, in_dve_items.index((kind, i)) + 1, back)

                def operand(src, part, at):
                    kind, k = src
                    return (x2 if kind == "x" else c2)[part][:, k, at]

                def run(b, first, last):
                    seen = set()

                    def have(kinds):
                        for kind, _ in kinds:
                            if kind not in seen:
                                seen.add(kind)
                                wait(pe, x_low if kind == "x" else c_low, b, NXS if kind == "x" else 1)

                    def weights_split(which):
                        if first and which not in seen:
                            seen.add(which)
                            pe.wait_ge(w_low, pieces_through(which))

                    for x, kind, i, back in steps(first, last):
                        if x in bank_of:
                            bank_free(x, b, first, last)
                            bank = ps_in[bank_of[x]]
                        if kind == "turnx":
                            wait(pe, xn_ready, b, 1)
                            for k in (2 * i, 2 * i + 1):
                                for t in range(2):
                                    a = (k % 2) * ROWS + t * P
                                    ins = nc.tensor.transpose(bank[:, a:a + P], xn[:, t, k * P:(k + 1) * P], ident[:, :])
                            ins.then_inc(in_ready.sem, 1)
                        elif kind in ("q", "k"):
                            srcs = q_from if kind == "q" else kv_from
                            have(srcs)
                            weights_split(kind)
                            hl = (queries if kind == "q" else keys) // halves
                            for h in range(halves):
                                at = slice(h * hl, (h + 1) * hl)
                                for m, s in enumerate(srcs):
                                    wb = h * len(srcs) + m
                                    ins = product(nc, bank[:, at],
                                                  [part[:, wb, i * P:(i + 1) * P] for part in w[kind]],
                                                  [operand(s, e, at) for e in range(2)],
                                                  m == 0, m == len(srcs) - 1)
                            ins.then_inc(in_ready.sem, 1)
                        elif kind == "v":
                            j, o = i % NJ, i // NJ
                            have(kv_from)
                            weights_split(kind)
                            at = slice(j * P, (j + 1) * P)
                            for m, s in enumerate(kv_from):
                                wb = (j * halves // NJ) * len(kv_from) + m
                                ins = product(nc, bank[:, 0:VN], [operand(s, e, at) for e in range(2)],
                                              [part[:, wb, o * VN:(o + 1) * VN] for part in w["v"]],
                                              m == 0, m == len(kv_from) - 1)
                            ins.then_inc(in_ready.sem, 1)
                        elif kind == "score":
                            g, r = divmod(i, UPG)
                            st, h = divmod(r, G)
                            if r == 0:
                                wait(pe, q_padded, b, g + 1, back)
                                wait(pe, in_dve, b, in_dve_items.index(("k", g)) + 1, back)
                            wait(pe, exped, b, i - 1, back)
                            for t in range(II):
                                a = (st * II + t) * P
                                ins = product(nc, ps_score[i % 2][:, t * keys:(t + 1) * keys],
                                              [part[:, g % 2, h, a:a + P] for part in q2],
                                              [part[:, g % 2, :] for part in k2], True, True)
                            ins.then_inc(scored.sem, 1)
                        elif kind == "turn":
                            wait(pe, exped, b, i + 1, back)
                            wait(pe, kept_act if i % 2 == 0 else kept_dve, b, i // 2, back)
                            for t in range(II):
                                for jc in range(NJ):
                                    a = (jc * II + t) * P
                                    c = t * keys + jc * P
                                    ins = nc.tensor.transpose(ps_turn[i % 2][:, a:a + P], probs[:, i % 3, c:c + P],
                                                              ident[:, :])
                            ins.then_inc(turned_ready.sem, 1)
                        elif kind == "mix":
                            g, st = divmod(i, SPG)
                            wait(pe, inv_ready, b, i + 1, back)
                            wait(pe, mix_taken, b, i - 1, back)
                            wait(pe, kept_act, b, (i + 1) * G // 2, back)
                            wait(pe, kept_dve, b, (i + 1) * G // 2, back)
                            if i == 0:
                                wait(pe, in_dve, b, in_dve_items.index(("v", NV - 1)) + 1, back)
                            bank = ps_mix[i % 2]
                            for t in range(II):
                                nc.tensor.transpose(bank[:, 1, t * P:(t + 1) * P], inv_wide[:, i % 2, t, :], ident[:, :])
                            order = [(jc, e) for jc in range(NJ) for e in range(HPT)]
                            for jc, e in order:
                                for t in range(TILES):
                                    h = t * HPT + e
                                    head = g * G + h
                                    ins = nc.tensor.matmul(bank[t * TW:(t + 1) * TW, 0, 0:QW],
                                                           v_sb[:, jc, head * TW:(head + 1) * TW],
                                                           turned[:, i % 2, h, jc * QW:(jc + 1) * QW],
                                                           start=((jc, e) == order[0]), stop=((jc, e) == order[-1]))
                            ins.then_inc(mix_ready.sem, 1)
                        elif kind == "out":
                            if i == 0:
                                wait(pe, mixed_low, b, S, back)
                                pe.wait_ge(w_low, len(pieces))
                            wait(pe, mix_taken, b, S + i - 1, back)
                            bank = ps_mix[i % 2][:, :, :].rearrange("p a n -> p (a n)")
                            for g in range(NG):
                                part_w = [part[:, g, i * P:(i + 1) * P] if channel_out else part[:, g, :]
                                          for part in w["o"]]
                                part_m = [part[:, g, :] if channel_out else part[:, g, i * P:(i + 1) * P]
                                          for part in mixed2]
                                lhs, rhs = (part_w, part_m) if channel_out else (part_m, part_w)
                                ins = product(nc, bank, lhs, rhs, g == 0, g == NG - 1)
                            ins.then_inc(mix_ready.sem, 1)
                        elif kind == "stat" and i < 2:
                            if i == 0:
                                wait(pe, mix_taken, b, S + 2, back)
                            else:
                                wait(pe, sq_ready, b, 1, back)
                            src = res if i == 0 else sq
                            for t in range(2):
                                ins = nc.tensor.matmul(bank[:, :], ones[:, :], src[:, t, :], start=(t == 0), stop=(t == 1))
                            ins.then_inc(stat_ready.sem, 1)

                iterations(pe, run)

        nc.clear_and_free_semaphores(sems)
        nc.all_engine_barrier()


class Primed(Count):

    def prime(self, eng):
        eng.sem_inc(self.sem, self.per)

    def at(self, b, k):
        return b * self.per + (self.per + k)


def mlp_stage(nc, name, x_in, x_out, w_up, w_down, out_row, cols, ident_dram):
    cols_dram, at_col, n_cols = cols
    KD = COLS // P
    HC = w_up.shape[1] // P
    NBANK = 4
    plan, banks = [], []

    def bank_item(kind, idx, engine):
        plan.append((kind, idx, len(banks)))
        banks.append(engine)

    for i in range(2):
        bank_item("turnx", i, "dve")
    for i in range(HC // 2):
        bank_item("up", i, "act")
    for i in range(2):
        bank_item("out", i, "dve")
    NP = len(banks)
    act_items = [p for p in range(NP) if banks[p] == "act"]
    dve_items = [p for p in range(NP) if banks[p] == "dve"]
    with ExitStack() as ctx:
        def sb(what, shape, dt=F32):
            return ctx.enter_context(nc.sbuf_tensor(f"{name}_{what}", shape, dt))

        sems = []

        def sem(what):
            sems.append(nc.alloc_semaphore(f"{name}_{what}"))
            return sems[-1]

        ident = sb("ident", [P, P])
        up = sb("up", [P, KD, HC * P])
        down = sb("down", [P, HC, COLS])
        col = sb("cols", [P, n_cols])
        o_bias = sb("o_bias", [P, COLS])
        x_sb = sb("x", [P, 2, COLS])
        res = sb("res", [P, 2, COLS])
        xn = sb("xn", [P, 2, COLS])
        xt = sb("xt", [P, KD, ROWS])
        hidden = sb("hidden", [P, HC, ROWS])
        y_sb = sb("y", [P, 2, COLS])
        stats = sb("stats", [P, 2, 6])
        mean_var = sb("mean_var", [P, 2, 2])
        std = sb("std", [P, 2])
        rstd = sb("rstd", [P, 2])
        eps_col = sb("eps", [P, 1])
        ps_proj = [ctx.enter_context(nc.psum_tensor(f"{name}_proj{i}", [P, BANK], F32)) for i in range(NBANK)]

        weights_in = sem("weights_in")
        consts_in = sem("consts_in")
        x_loaded = sem("x_loaded")
        res_loaded = sem("res_loaded")
        stored = sem("stored")
        setup = sem("setup")
        passed_dve = sem("passed_dve")
        passed_pool = sem("passed_pool")
        chain = sem("dve_chain")
        proj = Primed(sem("proj_ready"), NP)
        took_act = Primed(sem("proj_taken_act"), len(act_items))
        took_dve = Primed(sem("proj_taken_dve"), len(dve_items))
        xn_used = Primed(sem("x_normed"), 1)
        std_ready = Primed(sem("std_ready"), 1)
        res_ready = Primed(sem("residual_ready"), 1)
        CHAIN = 3

        x_src = x_in.rearrange("b (k p) l -> b p k l", p=P)
        y_dst = x_out.rearrange("b (k p) l -> b p k l", p=P)

        with nc.Block() as block:
            @block.sync
            def _(sp):
                sp.dma_start(col[:, :], cols_dram).then_inc(consts_in, 16)
                sp.dma_start(ident[:, :], ident_dram).then_inc(consts_in, 16)
                sp.dma_start(o_bias[:, :], out_row.partition_broadcast(P)).then_inc(consts_in, 16)
                for k in range(KD):
                    sp.dma_start(up[:, k, :], w_up[k * P:(k + 1) * P, :]).then_inc(weights_in, 16)
                sp.dma_start(down[:, :, :], w_down.rearrange("(m p) o -> p m o", p=P)).then_inc(weights_in, 16)
                sp.sem_inc(stored, 16)
                with sp.Fori(0, NB) as b:
                    sp.wait_ge(took_dve.sem, took_dve.at(b, len(dve_items)))
                    sp.dma_start(y_dst[b], y_sb[:, :, :]).then_inc(stored, 16)
                sp.wait_ge(stored, 16 * NB + 16)

            @block.gpsimd
            def _(pool):
                res_ready.prime(pool)
                nc.gpsimd.memset(eps_col[:, :], EPS).then_inc(setup, 1)
                pool.wait_ge(consts_in, 16 * 3)
                with pool.Fori(0, NB) as b:
                    pool.wait_ge(xn_used.sem, xn_used.at(b, 0))
                    pool.sem_inc(passed_pool, 1)
                    pool.dma_start(x_sb[:, :, :], x_src[b]).then_inc(x_loaded, 16)
                    pool.wait_ge(took_dve.sem, took_dve.at(b, 0))
                    pool.sem_inc(passed_pool, 1)
                    pool.dma_start(res[:, :, :], x_src[b]).then_inc(res_loaded, 16)
                    pool.wait_ge(res_loaded, 16 * b + 16)
                    pool.sem_inc(passed_pool, 1)
                    for t in range(2):
                        ins = nc.gpsimd.tensor_tensor(res[:, t, :], res[:, t, :], o_bias[:, :], ALU.add)
                    ins.then_inc(res_ready.sem, 1)

            @block.scalar
            def _(act):
                took_act.prime(act)
                std_ready.prime(act)
                act.wait_ge(consts_in, 16 * 3)
                act.wait_ge(setup, 1)
                with act.Fori(0, NB) as b:
                    for kind, i, p in plan:
                        if kind == "turnx" and i == 0:
                            act.wait_ge(chain, b * CHAIN + 2)
                            nc.scalar.activation(std[:, :], mean_var[:, :, 1], ACT.Sqrt, bias=eps_col[:, 0:1]
                                                 ).then_inc(std_ready.sem, 1)
                        elif kind == "up":
                            act.wait_ge(proj.sem, proj.at(b, p + 1))
                            for e in range(2):
                                m = 2 * i + e
                                c = at_col["up"] + m
                                ins = nc.scalar.activation(hidden[:, m, :], ps_proj[p % NBANK][:, e * ROWS:(e + 1) * ROWS],
                                                           ACT.Gelu_apprx_tanh, bias=col[:, c:c + 1])
                            ins.then_inc(took_act.sem, 1)

            @block.vector
            def _(dve):
                took_dve.prime(dve)
                xn_used.prime(dve)
                dve.wait_ge(consts_in, 16 * 3)
                with dve.Fori(0, NB) as b:
                    dve.wait_ge(x_loaded, 16 * b + 16)
                    for t in range(2):
                        last = nc.vector.bn_stats(stats[:, t, :], x_sb[:, t, :])
                    last.then_inc(chain, 1)
                    dve.wait_ge(chain, b * CHAIN + 1)
                    dve.sem_inc(passed_dve, 1)
                    for t in range(2):
                        last = nc.vector.bn_aggr(mean_var[:, t, :], stats[:, t, :])
                    last.then_inc(chain, 1)
                    dve.wait_ge(std_ready.sem, std_ready.at(b, 1))
                    nc.vector.reciprocal(rstd[:, :], std[:, :]).then_inc(chain, 1)
                    dve.wait_ge(chain, b * CHAIN + 3)
                    for t in range(2):
                        last = nc.vector.tensor_scalar(xn[:, t, :], x_sb[:, t, :], mean_var[:, t, 0:1],
                                                       rstd[:, t:t + 1], ALU.subtract, ALU.mult)
                    last.then_inc(xn_used.sem, 1)
                    for kind, i, p in plan:
                        if kind == "turnx":
                            dve.wait_ge(proj.sem, proj.at(b, p + 1))
                            for k in (2 * i, 2 * i + 1):
                                a, c = at_col["ln_w"] + k, at_col["ln_b"] + k
                                last = nc.vector.tensor_scalar(
                                    xt[:, k, :], ps_proj[p % NBANK][:, (k % 2) * ROWS:(k % 2 + 1) * ROWS],
                                    col[:, a:a + 1], col[:, c:c + 1], ALU.mult, ALU.add)
                            last.then_inc(took_dve.sem, 1)
                        elif kind == "out":
                            if i == 0:
                                dve.wait_ge(res_ready.sem, res_ready.at(b, 1))
                                dve.wait_ge(stored, 16 * b + 16)
                            dve.wait_ge(proj.sem, proj.at(b, p + 1))
                            nc.vector.tensor_tensor(y_sb[:, i, :], ps_proj[p % NBANK][:, :], res[:, i, :], ALU.add
                                                    ).then_inc(took_dve.sem, 1)

            @block.tensor
            def _(pe):
                proj.prime(pe)
                pe.wait_ge(consts_in, 16 * 3)
                pe.wait_ge(weights_in, 16 * (KD + 1))
                with pe.Fori(0, NB) as b:
                    for kind, i, p in plan:
                        q = p - NBANK
                        items, c = (act_items, took_act) if banks[q % NP] == "act" else (dve_items, took_dve)
                        k = items.index(q % NP) + 1
                        pe.wait_ge(c.sem, c.at(b, k if q >= 0 else k - len(items)))
                        bank = ps_proj[p % NBANK]
                        if kind == "turnx":
                            pe.wait_ge(xn_used.sem, xn_used.at(b, 1))
                            for k in (2 * i, 2 * i + 1):
                                for t in range(2):
                                    a = (k % 2) * ROWS + t * P
                                    last = nc.tensor.transpose(bank[:, a:a + P], xn[:, t, k * P:(k + 1) * P], ident[:, :])
                        elif kind == "up":
                            if i == 0:
                                pe.wait_ge(took_dve.sem, took_dve.at(b, 2))
                            for e in range(2):
                                m = 2 * i + e
                                for k in range(KD):
                                    last = nc.tensor.matmul(bank[:, e * ROWS:(e + 1) * ROWS],
                                                            up[:, k, m * P:(m + 1) * P], xt[:, k, :],
                                                            start=(k == 0), stop=(k == KD - 1))
                        else:
                            pe.wait_ge(took_act.sem, took_act.at(b, len(act_items)))
                            for m in range(HC):
                                last = nc.tensor.matmul(bank[:, :], hidden[:, m, i * P:(i + 1) * P], down[:, m, :],
                                                        start=(m == 0), stop=(m == HC - 1))
                        last.then_inc(proj.sem, 1)

        nc.clear_and_free_semaphores(sems)
        nc.all_engine_barrier()


def program(nc, t, out):
    step = [nc.dram_tensor(f"step{i}", (NB, ROWS, COLS), F32).ap() for i in range(7)]
    ctx_c, ctx_t = t["ctx"], t["ctx_t"]

    def rows(name, first, n, c0, c1):
        return [t[name][first + i * P:first + (i + 1) * P, c0:c1] for i in range(n)]

    def cols(name, **at):
        return t[name], at, t[name].shape[1]

    attention_stage(nc, "l0", t["x"], step[0], ctx_c,
                    {"q": [rows("l0_wq", 0, 2, 0, 256)], "k": [rows("l0_wk", 0, 2, 0, 256)],
                     "v": [rows("l0_wv", 0, 2, 0, 256)], "o": t["l0_wo"], "head_mask": t["mask16"]},
                    cols("l0_cols", q=0, k=2, o=4), t["ident"],
                    head_dim=16, queries=512, keys=512, channel_out=True)
    attention_stage(nc, "l1", step[0], step[1], ctx_t,
                    {"q": [rows("l1_wq", 0, 4, 0, 512)], "k": [rows("l1_wk", 0, 4, 0, 512)],
                     "v": [rows("l1_wv", 0, 4, 0, 512)], "o": t["l1_wo"], "head_mask": t["mask32"]},
                    cols("l1_cols", q=0, k=4, ln_w=8, ln_b=12), t["ident"],
                    head_dim=32, queries=256, keys=256, norm=True, key_mask=t["key_mask"],
                    v_row=t["l1_vb"], out_row=t["l1_ob"])
    mlp_stage(nc, "m1", step[1], step[2], t["l1_up"], t["l1_down"], t["l1_db"],
              cols("m1_cols", ln_w=0, ln_b=4, up=8), t["ident"])
    for part, x_out, more in ((0, step[6], dict(cols=cols("l2_cols", q=0, k=8, o=16))),
                              (1, step[3], dict(cols=cols("l2_cols", q=4, k=12), res_in=step[6], norm_out=True))):
        l2 = {}
        for what, c0 in (("q", 0), ("k", 1024), ("v", 2048)):
            c0 += part * 512
            l2[what] = [rows(f"l2_z{h}", 0, 2, c0, c0 + 512) + rows(f"l2_u{h}", 0, 2, c0, c0 + 512) for h in range(2)]
        attention_stage(nc, f"l2{'ab'[part]}", step[2], x_out, ctx_c,
                        {**l2, "o": t["l2_wo"][part * 512:(part + 1) * 512, :], "head_mask": t["mask64"]},
                        ident_dram=t["ident"], head_dim=64, queries=512, keys=512, halves=2, kv_also_q=True,
                        channel_out=True, **more)
    causal = t["causal_mask"].rearrange("a c (t p) k -> a c p t k", p=P)
    attention_stage(nc, "l3s", step[3], step[4], None,
                    {"q": [rows("l3_qkv", 0, 4, 0, 512)], "k": [rows("l3_qkv", 0, 4, 512, 1024)],
                     "v": [rows("l3_qkv", 0, 4, 1024, 1536)], "o": t["l3_ao"], "head_mask": t["mask32"]},
                    cols("l3s_cols", q=0, k=4, ln_w=8, ln_b=12), t["ident"],
                    head_dim=32, queries=256, keys=256, norm=True, self_kv=True,
                    fixed_mask=causal[0, 0], v_row=t["l3_svb"], out_row=t["l3_aob"])
    cross = t["cross_mask"].rearrange("b c (t p) k -> b (c p) t k", p=P)
    attention_stage(nc, "l3c", step[4], step[5], ctx_t,
                    {"q": [rows("l3_wq", 0, 4, 0, 512)], "k": [rows("l3_kv", 0, 4, 0, 512)],
                     "v": [rows("l3_kv", 0, 4, 512, 1024)], "o": t["l3_co"], "head_mask": t["mask32"]},
                    cols("l3c_cols", q=0, k=4, ln_w=8, ln_b=12), t["ident"],
                    head_dim=32, queries=256, keys=256, norm=True,
                    score_mask=lambda b: cross[b], v_row=t["l3_cvb"], out_row=t["l3_cob"])
    mlp_stage(nc, "m3", step[5], out, t["l3_up"], t["l3_down"], t["l3_db"],
              cols("m3_cols", ln_w=0, ln_b=4, up=8), t["ident"])


def layout(i):
    import numpy as np

    def a(name):
        return np.asarray(i[name])

    def col(*vectors):
        return np.ascontiguousarray(np.concatenate([v.reshape(-1, P).T for v in vectors], axis=1))

    def turned(m):
        return np.ascontiguousarray(m.T)

    def head_mask(d):
        return np.ascontiguousarray(np.kron(np.eye(P // d, dtype=np.float32), np.ones((d, 1), np.float32)))

    zero = np.zeros
    f = np.float32
    ctx = a("ctx_2048")
    qkv_b, kv_b = a("L3_xattn_b_qkv"), a("L3_xattn_b_kv")
    return {
        "x": a("x"), "ctx": ctx, "ctx_t": np.ascontiguousarray(ctx.transpose(0, 2, 1)),
        "ident": np.eye(P, dtype=f), "mask16": head_mask(16), "mask32": head_mask(32), "mask64": head_mask(64),
        "key_mask": a("mask_BxS2_bf1"), "causal_mask": a("mask_1x1xSxS2_fc1"), "cross_mask": a("mask_Bx1xSxS2_ff1"),
        "l0_wq": turned(a("L0_xattn_Wq")), "l0_wk": turned(a("L0_xattn_Wk")), "l0_wv": turned(a("L0_xattn_Wv")),
        "l0_wo": turned(a("L0_xattn_Wo")), "l0_cols": col(zero(256, f), zero(256, f), a("L0_xattn_bo")),
        "l1_wq": a("L1_xattn_q_w"), "l1_wk": a("L1_xattn_k_w"), "l1_wv": a("L1_xattn_v_w"), "l1_wo": a("L1_xattn_cproj_w"),
        "l1_cols": col(a("L1_xattn_q_b"), a("L1_xattn_k_b"), a("L1_xattn_ln1_w"), a("L1_xattn_ln1_b")),
        "l1_vb": a("L1_xattn_v_b"), "l1_ob": a("L1_xattn_cproj_b"),
        "l1_up": a("L1_xattn_fc_w"), "l1_down": a("L1_xattn_proj_w"), "l1_db": a("L1_xattn_proj_b"),
        "m1_cols": col(a("L1_xattn_ln2_w"), a("L1_xattn_ln2_b"), a("L1_xattn_fc_b")),
        "l2_z0": turned(a("L2_xattn_Wqkv0")), "l2_z1": turned(a("L2_xattn_Wqkv1")),
        "l2_u0": turned(a("L2_xattn_Winj0")), "l2_u1": turned(a("L2_xattn_Winj1")),
        "l2_wo": turned(a("L2_xattn_Wo")),
        "l2_cols": col(a("L2_xattn_r_w_bias").reshape(-1), zero(1024, f), a("L2_xattn_bo")),
        "l3_qkv": a("L3_xattn_w_qkv"), "l3_ao": a("L3_xattn_w_ao"),
        "l3s_cols": col(qkv_b[0:512], qkv_b[512:1024], a("L3_xattn_ln1_s"), a("L3_xattn_ln1_b")),
        "l3_svb": np.ascontiguousarray(qkv_b[1024:1536]), "l3_aob": a("L3_xattn_b_ao"),
        "l3_wq": a("L3_xattn_w_q"), "l3_kv": a("L3_xattn_w_kv"), "l3_co": a("L3_xattn_w_co"),
        "l3c_cols": col(a("L3_xattn_b_q"), kv_b[0:512], a("L3_xattn_ln2_s"), a("L3_xattn_ln2_b")),
        "l3_cvb": np.ascontiguousarray(kv_b[512:1024]), "l3_cob": a("L3_xattn_b_co"),
        "l3_up": a("L3_xattn_w1"), "l3_down": a("L3_xattn_w2"), "l3_db": a("L3_xattn_b2"),
        "m3_cols": col(a("L3_xattn_ln3_s"), a("L3_xattn_ln3_b"), a("L3_xattn_b1")),
    }


def kernel(**inputs):
    import concourse.bacc as bacc
    import numpy as np
    from concourse.bass_utils import run_bass_kernel_spmd

    nc = bacc.Bacc("TRN2", target_bir_lowering=False, num_devices=1)
    arrays = {f"in_{k}": np.ascontiguousarray(v) for k, v in layout(inputs).items()}
    t = {k[3:]: nc.dram_tensor(k, v.shape, mybir.dt.from_np(v.dtype), kind="ExternalInput").ap()
         for k, v in arrays.items()}
    out = nc.dram_tensor("out", (NB, ROWS, COLS), F32, kind="ExternalOutput").ap()
    program(nc, t, out)
    r = run_bass_kernel_spmd(nc, [arrays], core_ids=[0])
    return r.results[0]["out"]
```

```python
from contextlib import ExitStack

import concourse.bass as bass
from concourse import mybir
from concourse.alu_op_type import AluOpType as ALU

F32 = mybir.dt.float32
F32R = mybir.dt.float32r
ACT = mybir.ActivationFunctionType
AX = mybir.AxisListType

P = 128
NB = 8
ROWS = 256
COLS = 512
BANK = 512
EPS = 1e-5
KEY_MASKED = -3.0e38
LOWEST = -3.4e38
TURN_LAG = 2
MIX_LAG = 4
SLOTS = 4
STAT_AT = (7, 9, 11, 13)


class Count:

    def __init__(self, sem, per, base=0):
        self.sem, self.per, self.base = sem, per, base


def wait(eng, count, b, k, back=0):
    value = b * count.per + (k - back * count.per + count.base)
    if not (isinstance(value, int) and value <= count.base):
        eng.wait_ge(count.sem, value)


def chain_value(b, count, done, chained):
    if "first" not in chained:
        return done
    return b * count.per + (done + chained["first"] - count.per)


def iterations(eng, run):
    run(0, True, False)
    with eng.Fori(1, NB) as b:
        run(b, False, False)
    run(NB, False, True)


def raw(ap):
    return ap.bitcast(F32)


def product(nc, out, lhs, rhs, start, stop):
    nc.tensor.matmul(out, lhs[0], rhs[0], start=start, stop=False)
    nc.tensor.matmul(out, lhs[0], rhs[1], start=False, stop=False)
    return nc.tensor.matmul(out, lhs[1], rhs[0], start=False, stop=stop)


def attention_stage(nc, name, x_in, x_out, kv_in, weights, cols, ident_dram, *, head_dim, queries,
                    keys, halves=1, norm=False, self_kv=False, kv_also_q=False, key_mask=None,
                    fixed_mask=None, score_mask=None, channel_out=False, v_row=None, out_row=None,
                    norm_out=False, res_in=None):
    cols_dram, at_col, n_cols = cols
    NG = weights["o"].shape[0] // P
    CH = NG * P
    OW = weights["o"].shape[1]
    G = P // head_dim
    H = NG * G
    NI = queries // P
    NJ = keys // P
    II = BANK // keys
    SPG = NI // II
    QW = II * P
    UPG = SPG * G
    U = UPG * NG
    S = SPG * NG
    TILES = min(G, 4)
    TW = P // TILES
    HPT = G // TILES
    VN = min(CH, BANK)
    NV = NJ * (CH // VN)
    KX = 4 if norm else 2
    KC = 0 if self_kv else kv_in.shape[1] // P
    scale = float(head_dim) ** -0.5
    from_x = [("x", k) for k in range(KX)]
    from_c = [("c", k) for k in range(KC)]
    q_from = from_x + (from_c if kv_also_q else [])
    kv_from = q_from if (self_kv or kv_also_q) else from_c
    masked = key_mask is not None or fixed_mask is not None or score_mask is not None

    BACK = 10 if norm else UPG
    first_back = U - BACK
    aside = {}

    def put(p, *items):
        aside.setdefault(p, []).extend(items)

    if norm:
        put(-10, ("stats", 0))
        put(-9, ("root", 0))
        put(-8, ("norm", 0))
        put(-6, ("turnx", 0), ("turnx", 1))
        put(-5, ("xsplit", 0), ("xsplit", 1))
        if not self_kv:
            put(-4, ("split", "c"))
        put(-3, ("q", 0))
        put(-2, ("k", 0))
    else:
        q_at = -max(2 * G, 4)
        put(q_at - 4, ("split", "x"))
        put(q_at - 2, ("split", "c"))
        put(q_at, ("q", 0))
        put(-2, ("k", 0))
    for i in range(NV):
        put(min(MIX_LAG - 1 + i * G // NV, first_back - 1), ("v", i))

    plan = []
    for p in range(-BACK, first_back):
        def at_unit(kind, x, per=1):
            total = U // per
            return (kind, x % total, 1 if x < 0 else 0)

        n = p % U
        g, r = divmod(n, UPG)
        if p == 0:
            plan.append(("mask", 0, 0))
        if p == -6:
            plan.append(("res", 0, 1))
        if r == 0 and g + 1 < NG:
            plan.append(("q", g + 1, int(p < 0)))
        plan.append(at_unit("score", p))
        if r == 0 and g + 1 < NG:
            plan.append(("k", g + 1, int(p < 0)))
        before = [item for item in aside.get(p, []) if item[0] != "v"]
        plan += [(kind, i, 0) for kind, i in before]
        plan.append(at_unit("turn", p - TURN_LAG))
        m = p - MIX_LAG
        if m % G == 0:
            plan.append(at_unit("keep", m // G - 1, G))
        if p == MIX_LAG + 1:
            plan.append(("out", 0, 1))
        if p == min(MIX_LAG + G - 1, MIX_LAG + 2, first_back - 1):
            plan.append(("out", 1, 1))
        if m % G == G - 1:
            plan.append(at_unit("mix", m // G, G))
        plan += [(kind, i, 0) for kind, i in aside.get(p, []) if kind == "v"]
        if norm_out and p in STAT_AT:
            plan.append(("stat", STAT_AT.index(p), 1))

    bank_users = [x for x, (kind, i, _) in enumerate(plan)
                  if kind in ("q", "k", "v", "turnx", "out") or (kind == "stat" and i < 2)]
    assert len(bank_users) % 2 == 0
    bank_of = {x: n % 2 for n, x in enumerate(bank_users)}
    in_items = [plan[x][:2] for back in (0, 1) for x in bank_users
                if plan[x][0] not in ("out", "stat") and plan[x][2] == back]
    in_dve_items = [it for it in in_items if it[0] != "q"]

    with ExitStack() as ctx:
        def sb(what, shape, dt=F32):
            return ctx.enter_context(nc.sbuf_tensor(f"{name}_{what}", shape, dt))

        def pair(what, shape):
            return sb(what + "_high", shape, F32R), sb(what + "_low", shape, F32R)

        sems = []

        def sem(what):
            sems.append(nc.alloc_semaphore(f"{name}_{what}"))
            return sems[-1]

        def count(what, per, base=0):
            return Count(sem(what), per, base)

        ident = sb("ident", [P, P])
        col = sb("cols", [P, n_cols])
        head_mask = sb("head_mask", [P, G])
        w = {"q": pair("wq", [P, halves * len(q_from), CH]), "k": pair("wk", [P, halves * len(kv_from), CH]),
             "v": pair("wv", [P, halves * len(kv_from), CH]), "o": pair("wo", [P, NG, OW])}
        x_raw = sb("x_raw", [P, 2, COLS])
        res = sb("res", [P, 2, COLS])
        if norm:
            xn = sb("xn", [P, 2, COLS])
            xt32 = sb("xt32", [P, 4, ROWS])
            x2 = pair("x", [P, 4, ROWS])
            stats = sb("stats", [P, 2, 6])
            mean_var = sb("mean_var", [P, 2, 2])
            std = sb("std", [P, 2])
            rstd = sb("rstd", [P, 2])
        else:
            x2 = pair("x", [P, 2, COLS])
        if not self_kv:
            c_raw = sb("c_raw", [P, KC, keys])
            c2 = pair("c", [P, KC, keys])
        q_flat = sb("q_flat", [P, queries])
        q_part = sb("q_part", [P, queries], F32R)
        q2 = pair("q", [P, 2, G, queries])
        k2 = pair("k", [P, 2, keys])
        v_sb = sb("v", [P, NJ, H * TW if HPT > 1 else CH])
        probs = sb("probs", [P, SLOTS, BANK])
        turned = sb("turned", [P, 2, G, BANK])
        neg_max = sb("neg_max", [P, SLOTS, II])
        row_sum = sb("row_sum", [P, 2, II, G])
        inv_sum = sb("inv_sum", [P, 2, II, G])
        inv_wide = sb("inv_wide", [P, 2, II, P])
        inv_cols = sb("inv_cols", [P, QW])
        mixed32 = sb("mixed32", [P, 2, QW])
        mixed2 = pair("mixed", [P, NG, queries])
        y_sb = sb("y", [P, 2, COLS])
        eps_col = sb("eps", [P, 1])
        q_bias = sb("q_bias", [P, NG])
        if v_row is not None:
            v_bias = sb("v_bias", [P, CH])
        if out_row is not None:
            o_bias = sb("o_bias", [P, COLS])
        if key_mask is not None:
            mask_next = sb("mask_next", [P, keys], key_mask.dtype)
            mask_add = sb("mask_add", [P, 1, keys])
        elif masked:
            mask_mul = sb("mask_mul", [P, II, keys])
            mask_add = sb("mask_add", [P, II, keys])
            if score_mask is not None:
                mask_next = sb("mask_next", [P, II, keys])
        if masked:
            s_masked = sb("s_masked", [P, SLOTS, BANK])
            row_max = sb("row_max", [P, SLOTS, II])
        if norm_out:
            ones = sb("ones", [P, P])
            sq = y_sb
            rstd_n = y_sb[:, 1, :]
        staging = ([turned[:, a, g, :] for a in range(2) for g in range(2)] + [probs[:, a, :] for a in range(2)]
                   + [y_sb[:, a, :] for a in range(2)])
        STAGING = len(staging)

        def ps(what, shape):
            return ctx.enter_context(nc.psum_tensor(f"{name}_{what}", shape, F32))

        ps_in = [ps(f"in{i}", [P, BANK]) for i in range(2)]
        SCORES = 3 if 4 * QW <= BANK else 2
        ps_score = [ps(f"score{i}", [P, BANK]) for i in range(SCORES)]
        ps_turn = [ps(f"turn{i}", [P, BANK]) for i in range(2)]
        ps_mix = [ps(f"mix{i}", [P, BANK]) for i in range(4 - SCORES)]
        mix_at = [ps_mix[i % len(ps_mix)][:, (i // len(ps_mix)) * 2 * QW:][:, 0:2 * QW]
                  .rearrange("p (a n) -> p a n", a=2) for i in range(2)]

        w_loaded = [sem(f"weights_loaded{i}") for i in range(STAGING)]
        consts_in, x_loaded, c_loaded = sem("consts_in"), sem("x_loaded"), sem("c_loaded")
        res_loaded, mask_loaded = sem("res_loaded"), sem("mask_loaded")
        stored, setup = sem("stored"), sem("setup")
        passed_dve, passed_pool, passed_sp = sem("passed_dve"), sem("passed_pool"), sem("passed_sp")
        w_high, w_low = sem("weights_high"), sem("weights_low")
        in_ready = count("projected", len(in_items))
        scored, turned_ready, mix_ready = count("scored", U), count("turned", U), count("mixed", S)
        out_ready, stat_ready = count("out_ready", 2), count("stat_ready", 2)
        in_act, in_dve = count("in_taken_act", NG), count("in_taken_dve", len(in_dve_items))
        kept_act, kept_dve = count("turned_kept_act", U // 2), count("turned_kept_dve", U // 2)
        mix_taken, out_taken = count("mix_taken", S, base=1), count("out_taken", 2, base=2)
        stat_taken = count("stat_taken", 2)
        exped, maxed, inv_ready = count("exped", U), count("maxed", U), count("inverted", S)
        k_high, q_padded = count("k_high", NG), count("q_padded", NG * G)
        mixed_high, mixed_low = count("mixed_high", S), count("mixed_low", S, base=1)
        NXS = 2 if norm else 1
        x_high, x_low = count("x_high", NXS), count("x_low", NXS)
        c_high, c_low = count("c_high", 1), count("c_low", 1)
        mv_ready, std_ready, xn_ready = count("mean_var", 1), count("std", 1), count("x_normed", 1)
        res_ready, mask_ready = count("res_ready", 1), count("mask_ready", 1)
        sq_ready, std_n_ready, normed_out = count("squares", 1), count("std_n", 1), count("normed_out", 1)
        dve_chain = count("dve_chain", (2 if norm else 0) + 2 * S + (1 if norm_out else 0)
                          + (0 if not masked else U if key_mask is not None else 2 * U))
        pool_chain = count("pool_chain", 2 * NG + (1 if key_mask is not None else 0))
        n_setup = 2 + (1 if norm_out else 0) + (1 if HPT > 1 else 0) + (1 if fixed_mask is not None else 0)
        n_consts = 3 + (v_row is not None) + (out_row is not None) + (fixed_mask is not None)
        y_done, y_signals = (normed_out, 1) if norm_out else (out_taken, 2)

        x_src = x_in.rearrange("b (k p) l -> b p k l", p=P)
        r_src = (x_in if res_in is None else res_in).rearrange("b (k p) l -> b p k l", p=P)
        y_dst = x_out.rearrange("b (k p) l -> b p k l", p=P)
        if not self_kv:
            c_src = kv_in.rearrange("b (k p) l -> b p k l", p=P)

        pieces = []
        for which, n_from in (("q", len(q_from)), ("k", len(kv_from)), ("v", len(kv_from))):
            for h in range(halves):
                for i in range(n_from):
                    pieces.append((which, h * n_from + i, weights[which][h][i]))
        for g in range(NG):
            pieces.append(("o", g, weights["o"][g * P:(g + 1) * P, :]))

        def pieces_through(which):
            return max(n for n, (kind, _, _) in enumerate(pieces) if kind == which) + 1

        def freed(i, slots):
            before = i - slots if i >= slots else max(u for u in range(U) if u % slots == i % slots) - U
            return before + 1

        def steps(first, last):
            for x, (kind, i, back) in enumerate(plan):
                if not (first and back) and not (last and not back):
                    yield x, kind, i, back

        with nc.Block() as block:
            @block.sync
            def _(sp):
                sp.dma_start(x_raw[:, :, :], x_src[0]).then_inc(x_loaded, 16)
                if not self_kv:
                    sp.dma_start(c_raw[:, :, :], c_src[0]).then_inc(c_loaded, 16)
                sp.dma_start(head_mask[:, :], weights["head_mask"]).then_inc(consts_in, 16)
                sp.dma_start(col[:, :], cols_dram).then_inc(consts_in, 16)
                sp.dma_start(ident[:, :], ident_dram).then_inc(consts_in, 16)
                if v_row is not None:
                    sp.dma_start(v_bias[:, :], v_row.partition_broadcast(P)).then_inc(consts_in, 16)
                if out_row is not None:
                    sp.dma_start(o_bias[:, :], out_row.partition_broadcast(P)).then_inc(consts_in, 16)
                if fixed_mask is not None:
                    sp.dma_start(mask_mul[:, :, :], fixed_mask).then_inc(consts_in, 16)
                def mask_load(b):
                    if key_mask is not None:
                        sp.dma_start(mask_next[:, :], key_mask[b].partition_broadcast(P)).then_inc(mask_loaded, 16)
                    elif score_mask is not None:
                        sp.dma_start(mask_next[:, :, :], score_mask(b)).then_inc(mask_loaded, 16)

                for n, (which, block_i, src) in enumerate(pieces):
                    if n == pieces_through("k"):
                        mask_load(0)
                        sp.dma_start(res[:, :, :], r_src[0]).then_inc(res_loaded, 16)
                    if n >= STAGING:
                        sp.wait_ge(w_low, n - STAGING + 1)
                    sp.dma_start(staging[n % STAGING][:, 0:src.shape[1]], src).then_inc(w_loaded[n % STAGING], 16)
                sp.sem_inc(stored, 16)


                def inputs(b):
                    if norm:
                        wait(sp, xn_ready, b, 0)
                    else:
                        wait(sp, x_low, b, 0)
                    sp.dma_start(x_raw[:, :, :], x_src[b]).then_inc(x_loaded, 16)
                    if not self_kv:
                        wait(sp, c_low, b, 0)
                        sp.dma_start(c_raw[:, :, :], c_src[b]).then_inc(c_loaded, 16)
                    if key_mask is not None or score_mask is not None:
                        wait(sp, mask_ready, b, 0)
                        sp.sem_inc(passed_sp, 1)
                        mask_load(b)

                def output(b):
                    wait(sp, y_done, b, y_signals, back=1)
                    sp.dma_start(y_dst[b - 1], y_sb[:, :, :]).then_inc(stored, 16)
                    sp.dma_start(res[:, :, :], r_src[b]).then_inc(res_loaded, 16)

                inputs(1)
                with sp.Fori(1, NB - 1) as b:
                    inputs(b + 1)
                    output(b)
                output(NB - 1)
                wait(sp, y_done, NB, y_signals, back=1)
                sp.dma_start(y_dst[NB - 1], y_sb[:, :, :]).then_inc(stored, 16)
                sp.wait_ge(stored, 16 * NB + 16)

            @block.gpsimd
            def _(pool):
                nc.gpsimd.memset(eps_col[:, :], EPS).then_inc(setup, 1)
                if norm_out:
                    nc.gpsimd.memset(ones[:, :], 1.0 / ROWS).then_inc(setup, 1)
                if HPT > 1:
                    nc.gpsimd.memset(v_sb[:, :, :], 0.0).then_inc(setup, 1)
                pool.wait_ge(consts_in, 16 * n_consts)
                nc.gpsimd.tensor_scalar(q_bias[:, :], col[:, at_col["q"]:at_col["q"] + NG], scale, 1.0,
                                        ALU.mult, ALU.mult).then_inc(setup, 1)
                if fixed_mask is not None:
                    nc.gpsimd.tensor_scalar(mask_add[:, :, :], mask_mul[:, :, :], 10000.0, -10000.0,
                                            ALU.mult, ALU.add).then_inc(setup, 1)

                chained = {}

                def run(b, first, last):
                    done = [0]

                    def linked(ins):
                        done[0] += 1
                        ins.then_inc(pool_chain.sem, 1)
                        pool.wait_ge(pool_chain.sem, chain_value(b, pool_chain, done[0], chained))
                        pool.sem_inc(passed_pool, 1)

                    for _, kind, i, back in steps(first, last):
                        if kind == "q":
                            wait(pool, in_act, b, i + 1, back)
                            wait(pool, scored, b, (i - 1) * UPG, back)
                            pool.sem_inc(passed_pool, 1)
                            flat = q_flat[:, :]
                            linked(nc.gpsimd.tensor_scalar(q_part[:, :], flat, 1.0, 1.0, ALU.mult, ALU.mult))
                            linked(nc.gpsimd.tensor_tensor(q_part[:, :], flat, raw(q_part[:, :]), ALU.subtract))
                            for h in range(G):
                                nc.gpsimd.tensor_scalar(q2[0][:, i % 2, h, :], flat, head_mask[:, h:h + 1], 1.0,
                                                        ALU.mult, ALU.mult)
                                ins = nc.gpsimd.tensor_scalar(q2[1][:, i % 2, h, :], raw(q_part[:, :]),
                                                              head_mask[:, h:h + 1], 1.0, ALU.mult, ALU.mult)
                                ins.then_inc(q_padded.sem, 1)
                        elif kind == "mask" and (key_mask is not None or score_mask is not None):
                            pool.wait_ge(mask_loaded, 16 * b + 16)
                            wait(pool, maxed, b, 0)
                            pool.sem_inc(passed_pool, 1)
                            if key_mask is not None:
                                linked(nc.gpsimd.tensor_copy(mask_add[:, 0, :], mask_next[:, :]))
                                nc.gpsimd.tensor_scalar(mask_add[:, 0, :], mask_add[:, 0, :], -KEY_MASKED,
                                                        KEY_MASKED, ALU.mult, ALU.add).then_inc(mask_ready.sem, 1)
                            else:
                                nc.gpsimd.tensor_scalar(mask_mul[:, :, :], mask_next[:, :, :], 1.0, 1.0,
                                                        ALU.mult, ALU.mult)
                                nc.gpsimd.tensor_scalar(mask_add[:, :, :], mask_next[:, :, :], 10000.0, -10000.0,
                                                        ALU.mult, ALU.add).then_inc(mask_ready.sem, 1)
                        elif kind == "res" and out_row is not None:
                            pool.wait_ge(res_loaded, b * 16)
                            pool.sem_inc(passed_pool, 1)
                            for t in range(2):
                                ins = nc.gpsimd.tensor_tensor(res[:, t, :], res[:, t, :], o_bias[:, :], ALU.add)
                            ins.then_inc(res_ready.sem, 1)
                    if first:
                        chained["first"] = done[0]

                iterations(pool, run)

            @block.scalar
            def _(act):
                split_until = [0]

                def split_weights(which):
                    for n in range(split_until[0], pieces_through(which)):
                        kind, i, src = pieces[n]
                        act.wait_ge(w_loaded[n % STAGING], 16 * (n // STAGING + 1))
                        nc.scalar.activation(w[kind][0][:, i, :], staging[n % STAGING][:, 0:src.shape[1]], ACT.Copy
                                             ).then_inc(w_high, 1)
                        split_until[0] = n + 1

                act.wait_ge(consts_in, 16 * n_consts)
                act.wait_ge(setup, n_setup)

                def run(b, first, last):
                    for x, kind, i, back in steps(first, last):
                        if first and kind in ("q", "k", "score"):
                            split_weights("o" if kind == "score" else kind)
                        if kind == "split":
                            src, dst, loaded, high = ((x_raw, x2, x_loaded, x_high) if i == "x"
                                                      else (c_raw, c2, c_loaded, c_high))
                            act.wait_ge(loaded, 16 * b + 16)
                            wait(act, in_ready, b, 0)
                            nc.scalar.activation(dst[0][:, :, :], src[:, :, :], ACT.Copy).then_inc(high.sem, 1)
                        elif kind == "root":
                            wait(act, mv_ready, b, 1)
                            nc.scalar.activation(std[:, :], mean_var[:, :, 1], ACT.Sqrt, bias=eps_col[:, 0:1]
                                                 ).then_inc(std_ready.sem, 1)
                        elif kind == "xsplit":
                            wait(act, in_dve, b, in_dve_items.index(("turnx", i)) + 1)
                            wait(act, in_ready, b, 0)
                            nc.scalar.activation(x2[0][:, 2 * i:2 * i + 2, :], xt32[:, 2 * i:2 * i + 2, :], ACT.Copy
                                                 ).then_inc(x_high.sem, 1)
                        elif kind == "q":
                            wait(act, in_ready, b, in_items.index((kind, i)) + 1, back)
                            wait(act, q_padded, b, i * G, back)
                            nc.scalar.activation(q_flat[:, :], ps_in[bank_of[x]][:, 0:queries], ACT.Identity,
                                                 bias=q_bias[:, i:i + 1], scale=scale).then_inc(in_act.sem, 1)
                        elif kind == "k":
                            wait(act, in_ready, b, in_items.index((kind, i)) + 1, back)
                            wait(act, scored, b, (i - 1) * UPG, back)
                            c = at_col["k"] + i
                            nc.scalar.activation(k2[0][:, i % 2, :], ps_in[bank_of[x]][:, 0:keys], ACT.Identity,
                                                 bias=col[:, c:c + 1]).then_inc(k_high.sem, 1)
                        elif kind == "score":
                            wait(act, maxed, b, i + 1, back)
                            wait(act, turned_ready, b, freed(i, SLOTS), back)
                            wait(act, inv_ready, b, i // G - 1, back)
                            src = s_masked[:, i % SLOTS, :] if masked else ps_score[i % SCORES][:, :]
                            for t in range(II):
                                ins = nc.scalar.activation(
                                    probs[:, i % SLOTS, t * keys:(t + 1) * keys], src[:, t * keys:(t + 1) * keys],
                                    ACT.Exp, bias=neg_max[:, i % SLOTS, t:t + 1],
                                    accum_out=row_sum[:, (i // G) % 2, t, i % G:i % G + 1])
                            ins.then_inc(exped.sem, 1)
                        elif kind == "turn" and i % 2 == 0:
                            wait(act, turned_ready, b, i + 1, back)
                            nc.scalar.activation(turned[:, (i // G) % 2, i % G, :], ps_turn[i % 2][:, :], ACT.Copy
                                                 ).then_inc(kept_act.sem, 1)
                        elif kind == "keep":
                            g, st = divmod(i, SPG)
                            wait(act, mix_taken, b, i + 1, back)
                            nc.scalar.activation(mixed2[0][:, g, st * QW:(st + 1) * QW], mixed32[:, i % 2, :],
                                                 ACT.Copy).then_inc(mixed_high.sem, 1)
                        elif kind == "stat" and i == 0:
                            act.wait_ge(stored, b * 16)
                            wait(act, stat_taken, b, 1, back)
                            nc.scalar.activation(sq[:, :, :], res[:, :, :], ACT.Square).then_inc(sq_ready.sem, 1)
                        elif kind == "stat" and i == 2:
                            wait(act, stat_taken, b, 2, back)
                            nc.scalar.activation(rstd_n, rstd_n, ACT.Sqrt).then_inc(std_n_ready.sem, 1)

                iterations(act, run)

            @block.vector
            def _(dve):
                split_until = [0]

                def split_weights(which):
                    for n in range(split_until[0], pieces_through(which)):
                        kind, i, src = pieces[n]
                        dve.wait_ge(w_high, n + 1)
                        nc.vector.tensor_tensor(w[kind][1][:, i, :], staging[n % STAGING][:, 0:src.shape[1]],
                                                raw(w[kind][0][:, i, :]), ALU.subtract).then_inc(w_low, 1)
                        split_until[0] = n + 1

                for c in (out_taken, mix_taken, mixed_low):
                    dve.sem_inc(c.sem, c.base)
                dve.wait_ge(consts_in, 16 * n_consts)
                dve.wait_ge(setup, n_setup)
                chained = {}

                def run(b, first, last):
                    done = [0]

                    def linked(ins, apart=False):
                        done[0] += 1
                        ins.then_inc(dve_chain.sem, 1)
                        dve.wait_ge(dve_chain.sem, chain_value(b, dve_chain, done[0], chained))
                        if apart:
                            dve.sem_inc(passed_dve, 1)

                    for x, kind, i, back in steps(first, last):
                        if first and kind in ("q", "k", "score"):
                            split_weights("o" if kind == "score" else kind)
                        if kind == "split":
                            src, dst, high, low = ((x_raw, x2, x_high, x_low) if i == "x"
                                                   else (c_raw, c2, c_high, c_low))
                            wait(dve, high, b, 1)
                            nc.vector.tensor_tensor(dst[1][:, :, :], src[:, :, :], raw(dst[0][:, :, :]), ALU.subtract
                                                    ).then_inc(low.sem, 1)
                        elif kind == "stats":
                            dve.wait_ge(x_loaded, 16 * b + 16)
                            for t in range(2):
                                ins = nc.vector.bn_stats(stats[:, t, :], x_raw[:, t, :])
                            linked(ins, apart=True)
                            for t in range(2):
                                ins = nc.vector.bn_aggr(mean_var[:, t, :], stats[:, t, :])
                            ins.then_inc(mv_ready.sem, 1)
                        elif kind == "norm":
                            wait(dve, std_ready, b, 1)
                            linked(nc.vector.reciprocal(rstd[:, :], std[:, :]))
                            for t in range(2):
                                ins = nc.vector.tensor_scalar(xn[:, t, :], x_raw[:, t, :], mean_var[:, t, 0:1],
                                                              rstd[:, t:t + 1], ALU.subtract, ALU.mult)
                            ins.then_inc(xn_ready.sem, 1)
                        elif kind == "turnx":
                            wait(dve, in_ready, b, in_items.index((kind, i)) + 1)
                            for k in (2 * i, 2 * i + 1):
                                a, c = at_col["ln_w"] + k, at_col["ln_b"] + k
                                ins = nc.vector.tensor_scalar(
                                    xt32[:, k, :], ps_in[bank_of[x]][:, (k % 2) * ROWS:(k % 2 + 1) * ROWS],
                                    col[:, a:a + 1], col[:, c:c + 1], ALU.mult, ALU.add)
                            ins.then_inc(in_dve.sem, 1)
                        elif kind == "xsplit":
                            wait(dve, x_high, b, i + 1)
                            nc.vector.tensor_tensor(x2[1][:, 2 * i:2 * i + 2, :], xt32[:, 2 * i:2 * i + 2, :],
                                                    raw(x2[0][:, 2 * i:2 * i + 2, :]), ALU.subtract
                                                    ).then_inc(x_low.sem, 1)
                        elif kind == "k":
                            wait(dve, k_high, b, i + 1, back)
                            c = at_col["k"] + i
                            nc.vector.scalar_tensor_tensor(k2[1][:, i % 2, :], ps_in[bank_of[x]][:, 0:keys],
                                                           col[:, c:c + 1], raw(k2[0][:, i % 2, :]), ALU.add,
                                                           ALU.subtract).then_inc(in_dve.sem, 1)
                        elif kind == "v":
                            j, o = i % NJ, i // NJ
                            wait(dve, in_ready, b, in_items.index((kind, i)) + 1)
                            wait(dve, mix_ready, b, 0)
                            src = ps_in[bank_of[x]][:, 0:VN]
                            if HPT > 1:
                                wide = TW // HPT
                                dst = v_sb[:, j, :].rearrange("p (t e w) -> p t e w", e=HPT, w=TW)
                                sv = src.rearrange("p (t e w) -> p t e w", e=HPT, w=wide)
                                for e in range(HPT):
                                    ins = nc.vector.tensor_copy(dst[:, :, e, e * wide:(e + 1) * wide], sv[:, :, e, :])
                            elif v_row is not None:
                                ins = nc.vector.tensor_tensor(v_sb[:, j, o * VN:(o + 1) * VN], src,
                                                              v_bias[:, o * VN:(o + 1) * VN], ALU.add)
                            else:
                                ins = nc.vector.tensor_copy(v_sb[:, j, o * VN:(o + 1) * VN], src)
                            ins.then_inc(in_dve.sem, 1)
                        elif kind == "score":
                            if i == 0 and (key_mask is not None or score_mask is not None):
                                wait(dve, mask_ready, b, 1)
                            wait(dve, scored, b, i + 1, back)
                            wait(dve, exped, b, freed(i, SLOTS), back)
                            if key_mask is not None:
                                dve.sem_inc(passed_dve, 1)
                            s = ps_score[i % SCORES][:, :].rearrange("p (t k) -> p t k", t=II)
                            if not masked:
                                nc.vector.tensor_reduce(neg_max[:, i % SLOTS, :], s, AX.X, ALU.max, negate=True
                                                        ).then_inc(maxed.sem, 1)
                            else:
                                sm = s_masked[:, i % SLOTS, :].rearrange("p (t k) -> p t k", t=II)
                                if key_mask is None:
                                    linked(nc.vector.tensor_tensor(sm, s, mask_mul[:, :, :], ALU.mult), apart=True)
                                for t in range(II):
                                    ins = nc.vector.tensor_tensor_reduce(
                                        sm[:, t, :], s[:, t, :] if key_mask is not None else sm[:, t, :],
                                        mask_add[:, 0 if key_mask is not None else t, :],
                                        1.0, LOWEST, ALU.add, ALU.max, row_max[:, i % SLOTS, t:t + 1])
                                linked(ins)
                                nc.vector.tensor_scalar(neg_max[:, i % SLOTS, :], row_max[:, i % SLOTS, :], -1.0, None,
                                                        ALU.mult).then_inc(maxed.sem, 1)
                        elif kind == "turn":
                            if i % 2 == 1:
                                wait(dve, turned_ready, b, i + 1, back)
                                nc.vector.tensor_copy(turned[:, (i // G) % 2, i % G, :], ps_turn[i % 2][:, :]
                                                      ).then_inc(kept_dve.sem, 1)
                            if i % G == G - 1:
                                s = i // G
                                wait(dve, exped, b, i + 1, back)
                                linked(nc.vector.reciprocal(inv_sum[:, s % 2, :, :], row_sum[:, s % 2, :, :]))
                                src = inv_sum[:, s % 2, :, :].unsqueeze(3).to_broadcast([P, II, G, head_dim])
                                dst = inv_wide[:, s % 2, :, :].rearrange("p t (g d) -> p t g d", g=G)
                                nc.vector.tensor_copy(dst, src).then_inc(inv_ready.sem, 1)
                        elif kind == "mix":
                            wait(dve, mix_ready, b, i + 1, back)
                            wait(dve, mix_taken, b, i, back)
                            linked(nc.vector.tensor_copy(inv_cols[:, :], mix_at[i % 2][:, 1, :]))
                            wait(dve, mixed_low, b, i - 1, back)
                            nc.vector.tensor_tensor(mixed32[:, i % 2, :], mix_at[i % 2][:, 0, :],
                                                    inv_cols[:, :], ALU.mult).then_inc(mix_taken.sem, 1)
                        elif kind == "keep":
                            g, st = divmod(i, SPG)
                            at = slice(st * QW, (st + 1) * QW)
                            wait(dve, mixed_high, b, i + 1, back)
                            nc.vector.tensor_tensor(mixed2[1][:, g, at], mixed32[:, i % 2, :],
                                                    raw(mixed2[0][:, g, at]), ALU.subtract).then_inc(mixed_low.sem, 1)
                        elif kind == "out":
                            wait(dve, out_ready, b, i + 1, back)
                            ps_out = ps_in[bank_of[x]][:, :]
                            if i == 0:
                                if out_row is not None:
                                    wait(dve, res_ready, b, 1, back)
                                else:
                                    dve.wait_ge(res_loaded, b * 16)
                                dve.wait_ge(stored, b * 16)
                            dst = res if norm_out else y_sb
                            if "o" in at_col:
                                c = at_col["o"] + i
                                ins = nc.vector.scalar_tensor_tensor(dst[:, i, :], ps_out, col[:, c:c + 1],
                                                                     res[:, i, :], ALU.add, ALU.add)
                            else:
                                ins = nc.vector.tensor_tensor(dst[:, i, :], ps_out, res[:, i, :], ALU.add)
                            ins.then_inc(out_taken.sem, 1)
                        elif kind == "stat" and i == 0:
                            wait(dve, stat_ready, b, 1, back)
                            for t in range(2):
                                ins = nc.vector.tensor_tensor(res[:, t, :], res[:, t, :], ps_in[bank_of[x]][:, :],
                                                              ALU.subtract)
                            ins.then_inc(stat_taken.sem, 1)
                        elif kind == "stat" and i == 1:
                            wait(dve, stat_ready, b, 2, back)
                            nc.vector.tensor_scalar(rstd_n, ps_in[bank_of[x]][:, :], 1.0, EPS, ALU.mult, ALU.add
                                                    ).then_inc(stat_taken.sem, 1)
                        elif kind == "stat" and i == 3:
                            wait(dve, std_n_ready, b, 1, back)
                            linked(nc.vector.reciprocal(rstd_n, rstd_n))
                            for t in range(2):
                                ins = nc.vector.tensor_tensor(y_sb[:, t, :], res[:, t, :], rstd_n, ALU.mult)
                            ins.then_inc(normed_out.sem, 1)
                    if first:
                        chained["first"] = done[0]

                iterations(dve, run)

            @block.tensor
            def _(pe):
                pe.wait_ge(consts_in, 16 * n_consts)
                pe.wait_ge(setup, n_setup)

                def bank_free(x, b, first, last):
                    n = bank_users.index(x) - 2
                    while n >= 0 and (first if plan[bank_users[n]][2] else last):
                        n -= 2
                    wait_taken(n, b)
                    while n < 0 and plan[bank_users[n]][2]:
                        n -= 2
                        wait_taken(n, b)

                def wait_taken(n, b):
                    kind, i, back = plan[bank_users[n]]
                    assert n >= 0 or not back or kind == "out"
                    back += 1 if n < 0 else 0
                    if kind in ("stat", "out"):
                        wait(pe, stat_taken if kind == "stat" else out_taken, b, i + 1, back)
                    elif kind == "q":
                        wait(pe, in_act, b, i + 1, back)
                    else:
                        wait(pe, in_dve, b, in_dve_items.index((kind, i)) + 1, back)

                def operand(src, part, at):
                    kind, k = src
                    return (x2 if kind == "x" else c2)[part][:, k, at]

                def run(b, first, last):
                    seen = set()

                    def have(kinds):
                        for kind, _ in kinds:
                            if kind not in seen:
                                seen.add(kind)
                                wait(pe, x_low if kind == "x" else c_low, b, NXS if kind == "x" else 1)

                    def weights_split(which):
                        if first and which not in seen:
                            seen.add(which)
                            pe.wait_ge(w_low, pieces_through(which))

                    for x, kind, i, back in steps(first, last):
                        if x in bank_of:
                            bank_free(x, b, first, last)
                            bank = ps_in[bank_of[x]]
                        if kind == "turnx":
                            wait(pe, xn_ready, b, 1)
                            for k in (2 * i, 2 * i + 1):
                                for t in range(2):
                                    a = (k % 2) * ROWS + t * P
                                    ins = nc.tensor.transpose(bank[:, a:a + P], xn[:, t, k * P:(k + 1) * P], ident[:, :])
                            ins.then_inc(in_ready.sem, 1)
                        elif kind in ("q", "k"):
                            srcs = q_from if kind == "q" else kv_from
                            if not back:
                                have(srcs)
                                weights_split(kind)
                            hl = (queries if kind == "q" else keys) // halves
                            for h in range(halves):
                                at = slice(h * hl, (h + 1) * hl)
                                for m, s in enumerate(srcs):
                                    wb = h * len(srcs) + m
                                    ins = product(nc, bank[:, at],
                                                  [part[:, wb, i * P:(i + 1) * P] for part in w[kind]],
                                                  [operand(s, e, at) for e in range(2)],
                                                  m == 0, m == len(srcs) - 1)
                            ins.then_inc(in_ready.sem, 1)
                        elif kind == "v":
                            j, o = i % NJ, i // NJ
                            have(kv_from)
                            weights_split(kind)
                            at = slice(j * P, (j + 1) * P)
                            for m, s in enumerate(kv_from):
                                wb = (j * halves // NJ) * len(kv_from) + m
                                ins = product(nc, bank[:, 0:VN], [operand(s, e, at) for e in range(2)],
                                              [part[:, wb, o * VN:(o + 1) * VN] for part in w["v"]],
                                              m == 0, m == len(kv_from) - 1)
                            ins.then_inc(in_ready.sem, 1)
                        elif kind == "score":
                            g, r = divmod(i, UPG)
                            st, h = divmod(r, G)
                            if st == 0:
                                wait(pe, q_padded, b, g * G + h + 1, back)
                            if r == 0:
                                wait(pe, in_dve, b, in_dve_items.index(("k", g)) + 1, back)
                            wait(pe, maxed if masked else exped, b, freed(i, SCORES), back)
                            for t in range(II):
                                a = (st * II + t) * P
                                ins = product(nc, ps_score[i % SCORES][:, t * keys:(t + 1) * keys],
                                              [part[:, g % 2, h, a:a + P] for part in q2],
                                              [part[:, g % 2, :] for part in k2], True, True)
                            ins.then_inc(scored.sem, 1)
                        elif kind == "turn":
                            wait(pe, exped, b, i + 1, back)
                            wait(pe, kept_act if i % 2 == 0 else kept_dve, b, i // 2, back)
                            for t in range(II):
                                for jc in range(NJ):
                                    a = (jc * II + t) * P
                                    c = t * keys + jc * P
                                    ins = nc.tensor.transpose(ps_turn[i % 2][:, a:a + P], probs[:, i % SLOTS, c:c + P],
                                                              ident[:, :])
                            ins.then_inc(turned_ready.sem, 1)
                        elif kind == "mix":
                            g, st = divmod(i, SPG)
                            wait(pe, inv_ready, b, i + 1, back)
                            wait(pe, mix_taken, b, i + 1 - len(ps_mix), back)
                            wait(pe, kept_act, b, (i + 1) * G // 2, back)
                            wait(pe, kept_dve, b, (i + 1) * G // 2, back)
                            if i == 0:
                                wait(pe, in_dve, b, in_dve_items.index(("v", NV - 1)) + 1, back)
                            bank = mix_at[i % 2]
                            for t in range(II):
                                nc.tensor.transpose(bank[:, 1, t * P:(t + 1) * P], inv_wide[:, i % 2, t, :], ident[:, :])
                            order = [(jc, e) for jc in range(NJ) for e in range(HPT)]
                            for jc, e in order:
                                for t in range(TILES):
                                    h = t * HPT + e
                                    head = g * G + h
                                    ins = nc.tensor.matmul(bank[t * TW:(t + 1) * TW, 0, 0:QW],
                                                           v_sb[:, jc, head * TW:(head + 1) * TW],
                                                           turned[:, i % 2, h, jc * QW:(jc + 1) * QW],
                                                           start=((jc, e) == order[0]), stop=((jc, e) == order[-1]))
                            ins.then_inc(mix_ready.sem, 1)
                        elif kind == "out":
                            if i == 0:
                                wait(pe, mixed_low, b, S, back)
                                pe.wait_ge(w_low, len(pieces))
                            for g in range(NG):
                                part_w = [part[:, g, i * P:(i + 1) * P] if channel_out else part[:, g, :]
                                          for part in w["o"]]
                                part_m = [part[:, g, :] if channel_out else part[:, g, i * P:(i + 1) * P]
                                          for part in mixed2]
                                lhs, rhs = (part_w, part_m) if channel_out else (part_m, part_w)
                                ins = product(nc, bank[:, :], lhs, rhs, g == 0, g == NG - 1)
                            ins.then_inc(out_ready.sem, 1)
                        elif kind == "stat" and i < 2:
                            if i == 0:
                                wait(pe, out_taken, b, 2, back)
                            else:
                                wait(pe, sq_ready, b, 1, back)
                            src = res if i == 0 else sq
                            for t in range(2):
                                ins = nc.tensor.matmul(bank[:, :], ones[:, :], src[:, t, :], start=(t == 0), stop=(t == 1))
                            ins.then_inc(stat_ready.sem, 1)

                iterations(pe, run)

        nc.clear_and_free_semaphores(sems)
        nc.all_engine_barrier()


def mlp_stage(nc, name, x_in, x_out, w_up, w_down, out_row, cols, ident_dram):
    cols_dram, at_col, n_cols = cols
    KD = COLS // P
    HC = w_up.shape[1] // P
    UPS = HC * ROWS // BANK
    UP_BANKS = 4
    EACH = HC // UPS

    plan = [("stats", 0, 0), ("root", 0, 0), ("norm", 0, 0), ("out", 0, 1), ("turnx", 0, 0), ("turnx", 1, 0),
            ("xsplit", 0, 0), ("xsplit", 1, 0), ("out", 1, 1), ("res", 0, 0)]
    plan += [("up", c, 0) for c in range(UPS)]

    pieces = [("up", k, c * BANK, w_up[k * P:(k + 1) * P, c * BANK:(c + 1) * BANK])
              for c in range(HC * P // BANK) for k in range(KD)]
    N_UP = len(pieces)
    pieces += [("down", m, 0, w_down[m * P:(m + 1) * P, :]) for m in range(HC)]
    with ExitStack() as ctx:
        def sb(what, shape, dt=F32):
            return ctx.enter_context(nc.sbuf_tensor(f"{name}_{what}", shape, dt))

        def pair(what, shape):
            return sb(what + "_high", shape, F32R), sb(what + "_low", shape, F32R)

        sems = []

        def sem(what):
            sems.append(nc.alloc_semaphore(f"{name}_{what}"))
            return sems[-1]

        def count(what, per, base=0):
            return Count(sem(what), per, base)

        ident = sb("ident", [P, P])
        up2 = pair("w_up", [P, KD, HC * P])
        down2 = pair("w_down", [P, HC, COLS])
        col = sb("cols", [P, n_cols])
        o_bias = sb("o_bias", [P, COLS])
        x_raw = sb("x_raw", [P, 2, COLS])
        res = sb("res", [P, 2, COLS])
        xn = sb("xn", [P, 2, COLS])
        xt32 = sb("xt32", [P, KD, ROWS])
        x2 = pair("x", [P, KD, ROWS])
        h32 = sb("hidden32", [P, 2, EACH, ROWS])
        h2 = pair("hidden", [P, HC, ROWS])
        y_sb = sb("y", [P, 2, COLS])
        staged = sb("staged", [P, 2, BANK])
        stats = sb("stats", [P, 2, 6])
        mean_var = sb("mean_var", [P, 2, 2])
        std = sb("std", [P, 2])
        rstd = sb("rstd", [P, 2])
        eps_col = sb("eps", [P, 1])
        places = [staged[:, 0, :], staged[:, 1, :], y_sb[:, 0, :], y_sb[:, 1, :]] + [
            h32[:, i, :, :].rearrange("p m n -> p (m n)") for i in range(2)]

        def place(n):
            if n < N_UP:
                return n % 6, n // 6, n - 6 + 1
            m = n - N_UP
            had = len([u for u in range(N_UP) if u % 6 == m % 4])
            return m % 4, had + m // 4, N_UP if m < 4 else n - 4 + 1

        def ps(what):
            return ctx.enter_context(nc.psum_tensor(f"{name}_{what}", [P, BANK], F32))

        ps_up = [ps(f"up{i}") for i in range(UP_BANKS)]
        ps_out = [ps(f"out{i}") for i in range(2)]
        ps_turn = [ps(f"turn{i}") for i in range(2)]

        w_loaded = [sem(f"weights_loaded{i}") for i in range(len(places))]
        consts_in, x_loaded, stored, setup = sem("consts_in"), sem("x_loaded"), sem("stored"), sem("setup")
        w_high, w_low = sem("weights_high"), sem("weights_low")
        passed_dve, passed_pool = sem("passed_dve"), sem("passed_pool")
        turned_ready, up_ready, out_ready = count("turned", 2), count("up_ready", UPS), count("out_ready", 2)
        mv_ready, std_ready, xn_ready = count("mean_var", 1), count("std", 1), count("x_normed", 1)
        turned_taken, x_high, x_low = count("turned_taken", 2), count("x_high", 2), count("x_low", 2)
        h_high, h_low = count("hidden_high", UPS), count("hidden_low", UPS)
        out_taken, res_ready = count("out_taken", 2, base=2), count("res_ready", 1)
        dve_chain = count("dve_chain", 2)

        x_src = x_in.rearrange("b (k p) l -> b p k l", p=P)
        y_dst = x_out.rearrange("b (k p) l -> b p k l", p=P)

        def steps(first, last):
            for kind, i, back in plan:
                if not (first and back) and not (last and not back):
                    yield kind, i, back

        def down_pieces(c):
            return range(N_UP + c * EACH, N_UP + (c + 1) * EACH)

        with nc.Block() as block:
            @block.sync
            def _(sp):
                sp.dma_start(x_raw[:, :, :], x_src[0]).then_inc(x_loaded, 16)
                sp.dma_start(ident[:, :], ident_dram).then_inc(consts_in, 16)
                sp.dma_start(col[:, :], cols_dram).then_inc(consts_in, 16)
                sp.dma_start(o_bias[:, :], out_row.partition_broadcast(P)).then_inc(consts_in, 16)
                for n, (_, _, _, src) in enumerate(pieces):
                    at, _, split_first = place(n)
                    if split_first > 0:
                        sp.wait_ge(w_low, split_first)
                    sp.dma_start(places[at], src).then_inc(w_loaded[at], 16)
                sp.sem_inc(stored, 16)
                with sp.Fori(1, NB) as b:
                    wait(sp, xn_ready, b, 0)
                    wait(sp, res_ready, b, 0)
                    sp.dma_start(x_raw[:, :, :], x_src[b]).then_inc(x_loaded, 16)
                    wait(sp, out_taken, b, 2, back=1)
                    sp.dma_start(y_dst[b - 1], y_sb[:, :, :]).then_inc(stored, 16)
                wait(sp, out_taken, NB, 2, back=1)
                sp.dma_start(y_dst[NB - 1], y_sb[:, :, :]).then_inc(stored, 16)
                sp.wait_ge(stored, 16 * NB + 16)

            @block.gpsimd
            def _(pool):
                nc.gpsimd.memset(eps_col[:, :], EPS).then_inc(setup, 1)
                pool.wait_ge(consts_in, 16 * 3)

                def run(b, first, last):
                    for kind, i, back in steps(first, last):
                        if kind == "res":
                            pool.wait_ge(x_loaded, 16 * b + 16)
                            wait(pool, out_taken, b, 0)
                            pool.sem_inc(passed_pool, 1)
                            for t in range(2):
                                ins = nc.gpsimd.tensor_tensor(res[:, t, :], x_raw[:, t, :], o_bias[:, :], ALU.add)
                            ins.then_inc(res_ready.sem, 1)

                iterations(pool, run)

            @block.scalar
            def _(act):
                def split(n):
                    which, i, c, src = pieces[n]
                    at, had, _ = place(n)
                    act.wait_ge(w_loaded[at], 16 * (had + 1))
                    w = up2 if which == "up" else down2
                    nc.scalar.activation(w[0][:, i, c:c + BANK], places[place(n)[0]], ACT.Copy).then_inc(w_high, 1)

                act.wait_ge(consts_in, 16 * 3)
                act.wait_ge(setup, 1)

                def run(b, first, last):
                    for kind, i, back in steps(first, last):
                        if kind == "root":
                            wait(act, mv_ready, b, 1)
                            nc.scalar.activation(std[:, :], mean_var[:, :, 1], ACT.Sqrt, bias=eps_col[:, 0:1]
                                                 ).then_inc(std_ready.sem, 1)
                        elif kind == "xsplit":
                            wait(act, turned_taken, b, i + 1)
                            wait(act, up_ready, b, 0)
                            nc.scalar.activation(x2[0][:, 2 * i:2 * i + 2, :], xt32[:, 2 * i:2 * i + 2, :], ACT.Copy
                                                 ).then_inc(x_high.sem, 1)
                        elif kind == "up":
                            if first and i == 0:
                                for n in range(N_UP):
                                    split(n)
                                act.wait_ge(w_low, N_UP)
                            wait(act, up_ready, b, i + 1)
                            wait(act, h_low, b, i - 1)
                            wait(act, out_ready, b, 0)
                            bank = ps_up[i % UP_BANKS]
                            for e in range(EACH):
                                m = EACH * i + e
                                bias = col[:, at_col["up"] + m:at_col["up"] + m + 1]
                                for dst in (h32[:, i % 2, e, :], h2[0][:, m, :]):
                                    ins = nc.scalar.activation(dst, bank[:, e * ROWS:(e + 1) * ROWS],
                                                               ACT.Gelu_apprx_tanh, bias=bias)
                            ins.then_inc(h_high.sem, 1)
                            if first:
                                for n in down_pieces(i):
                                    split(n)

                iterations(act, run)

            @block.vector
            def _(dve):
                def split(n):
                    which, i, c, src = pieces[n]
                    w = up2 if which == "up" else down2
                    dve.wait_ge(w_high, n + 1)
                    nc.vector.tensor_tensor(w[1][:, i, c:c + BANK], places[place(n)[0]], raw(w[0][:, i, c:c + BANK]), ALU.subtract
                                            ).then_inc(w_low, 1)

                dve.sem_inc(out_taken.sem, out_taken.base)
                dve.wait_ge(consts_in, 16 * 3)

                def run(b, first, last):
                    for kind, i, back in steps(first, last):
                        if kind == "stats":
                            dve.wait_ge(x_loaded, 16 * b + 16)
                            for t in range(2):
                                ins = nc.vector.bn_stats(stats[:, t, :], x_raw[:, t, :])
                            ins.then_inc(dve_chain.sem, 1)
                            wait(dve, dve_chain, b, 1)
                            dve.sem_inc(passed_dve, 1)
                            for t in range(2):
                                ins = nc.vector.bn_aggr(mean_var[:, t, :], stats[:, t, :])
                            ins.then_inc(mv_ready.sem, 1)
                        elif kind == "norm":
                            wait(dve, std_ready, b, 1)
                            nc.vector.reciprocal(rstd[:, :], std[:, :]).then_inc(dve_chain.sem, 1)
                            wait(dve, dve_chain, b, 2)
                            for t in range(2):
                                ins = nc.vector.tensor_scalar(xn[:, t, :], x_raw[:, t, :], mean_var[:, t, 0:1],
                                                              rstd[:, t:t + 1], ALU.subtract, ALU.mult)
                            ins.then_inc(xn_ready.sem, 1)
                        elif kind == "turnx":
                            wait(dve, turned_ready, b, i + 1)
                            for k in (2 * i, 2 * i + 1):
                                a, c = at_col["ln_w"] + k, at_col["ln_b"] + k
                                ins = nc.vector.tensor_scalar(
                                    xt32[:, k, :], ps_turn[i][:, (k % 2) * ROWS:(k % 2 + 1) * ROWS],
                                    col[:, a:a + 1], col[:, c:c + 1], ALU.mult, ALU.add)
                            ins.then_inc(turned_taken.sem, 1)
                        elif kind == "xsplit":
                            wait(dve, x_high, b, i + 1)
                            nc.vector.tensor_tensor(x2[1][:, 2 * i:2 * i + 2, :], xt32[:, 2 * i:2 * i + 2, :],
                                                    raw(x2[0][:, 2 * i:2 * i + 2, :]), ALU.subtract
                                                    ).then_inc(x_low.sem, 1)
                        elif kind == "up":
                            if first and i == 0:
                                for n in range(N_UP):
                                    split(n)
                            wait(dve, h_high, b, i + 1)
                            m = EACH * i
                            nc.vector.tensor_tensor(h2[1][:, m:m + EACH, :], h32[:, i % 2, :, :],
                                                    raw(h2[0][:, m:m + EACH, :]), ALU.subtract
                                                    ).then_inc(h_low.sem, 1)
                            if first:
                                for n in down_pieces(i):
                                    split(n)
                        elif kind == "out":
                            if i == 0:
                                wait(dve, res_ready, b, 1, back)
                                dve.wait_ge(stored, b * 16)
                            wait(dve, out_ready, b, i + 1, back)
                            nc.vector.tensor_tensor(y_sb[:, i, :], ps_out[i][:, :], res[:, i, :], ALU.add
                                                    ).then_inc(out_taken.sem, 1)

                iterations(dve, run)

            @block.tensor
            def _(pe):
                pe.wait_ge(consts_in, 16 * 3)

                def run(b, first, last):
                    for kind, i, back in steps(first, last):
                        if kind == "turnx":
                            wait(pe, xn_ready, b, 1)
                            for k in (2 * i, 2 * i + 1):
                                for t in range(2):
                                    a = (k % 2) * ROWS + t * P
                                    ins = nc.tensor.transpose(ps_turn[i][:, a:a + P], xn[:, t, k * P:(k + 1) * P],
                                                              ident[:, :])
                            ins.then_inc(turned_ready.sem, 1)
                        elif kind == "up":
                            if i == 0:
                                wait(pe, x_low, b, 2)
                            if first:
                                pe.wait_ge(w_low, KD * (((i + 1) * EACH * P - 1) // BANK + 1))
                            wait(pe, h_high, b, i + 1 - UP_BANKS)
                            for e in range(EACH):
                                m = EACH * i + e
                                for k in range(KD):
                                    ins = product(nc, ps_up[i % UP_BANKS][:, e * ROWS:(e + 1) * ROWS],
                                                  [part[:, k, m * P:(m + 1) * P] for part in up2],
                                                  [part[:, k, :] for part in x2], k == 0, k == KD - 1)
                            ins.then_inc(up_ready.sem, 1)
                        elif kind == "out":
                            if i == 0:
                                pe.wait_ge(w_low, len(pieces))
                            wait(pe, out_taken, b, i + 1 - 2, back)
                            for m in range(HC):
                                if i == 0 and m % EACH == 0:
                                    wait(pe, h_low, b, m // EACH + 1, back)
                                ins = product(nc, ps_out[i][:, :], [part[:, m, i * P:(i + 1) * P] for part in h2],
                                              [part[:, m, :] for part in down2], m == 0, m == HC - 1)
                            ins.then_inc(out_ready.sem, 1)

                iterations(pe, run)

        nc.clear_and_free_semaphores(sems)
        nc.all_engine_barrier()


def program(nc, t, out):
    step = [nc.dram_tensor(f"step{i}", (NB, ROWS, COLS), F32).ap() for i in range(7)]
    ctx_c, ctx_t = t["ctx"], t["ctx_t"]

    def rows(name, first, n, c0, c1):
        return [t[name][first + i * P:first + (i + 1) * P, c0:c1] for i in range(n)]

    def cols(name, **at):
        return t[name], at, t[name].shape[1]

    attention_stage(nc, "l0", t["x"], step[0], ctx_c,
                    {"q": [rows("l0_wq", 0, 2, 0, 256)], "k": [rows("l0_wk", 0, 2, 0, 256)],
                     "v": [rows("l0_wv", 0, 2, 0, 256)], "o": t["l0_wo"], "head_mask": t["mask16"]},
                    cols("l0_cols", q=0, k=2, o=4), t["ident"],
                    head_dim=16, queries=512, keys=512, channel_out=True)
    attention_stage(nc, "l1", step[0], step[1], ctx_t,
                    {"q": [rows("l1_wq", 0, 4, 0, 512)], "k": [rows("l1_wk", 0, 4, 0, 512)],
                     "v": [rows("l1_wv", 0, 4, 0, 512)], "o": t["l1_wo"], "head_mask": t["mask32"]},
                    cols("l1_cols", q=0, k=4, ln_w=8, ln_b=12), t["ident"],
                    head_dim=32, queries=256, keys=256, norm=True, key_mask=t["key_mask"],
                    v_row=t["l1_vb"], out_row=t["l1_ob"])
    mlp_stage(nc, "m1", step[1], step[2], t["l1_up"], t["l1_down"], t["l1_db"],
              cols("m1_cols", ln_w=0, ln_b=4, up=8), t["ident"])
    for part, x_out, more in ((0, step[6], dict(cols=cols("l2_cols", q=0, k=8, o=16))),
                              (1, step[3], dict(cols=cols("l2_cols", q=4, k=12), res_in=step[6], norm_out=True))):
        l2 = {}
        for what, c0 in (("q", 0), ("k", 1024), ("v", 2048)):
            c0 += part * 512
            l2[what] = [rows(f"l2_z{h}", 0, 2, c0, c0 + 512) + rows(f"l2_u{h}", 0, 2, c0, c0 + 512) for h in range(2)]
        attention_stage(nc, f"l2{'ab'[part]}", step[2], x_out, ctx_c,
                        {**l2, "o": t["l2_wo"][part * 512:(part + 1) * 512, :], "head_mask": t["mask64"]},
                        ident_dram=t["ident"], head_dim=64, queries=512, keys=512, halves=2, kv_also_q=True,
                        channel_out=True, **more)
    causal = t["causal_mask"].rearrange("a c (t p) k -> a c p t k", p=P)
    attention_stage(nc, "l3s", step[3], step[4], None,
                    {"q": [rows("l3_qkv", 0, 4, 0, 512)], "k": [rows("l3_qkv", 0, 4, 512, 1024)],
                     "v": [rows("l3_qkv", 0, 4, 1024, 1536)], "o": t["l3_ao"], "head_mask": t["mask32"]},
                    cols("l3s_cols", q=0, k=4, ln_w=8, ln_b=12), t["ident"],
                    head_dim=32, queries=256, keys=256, norm=True, self_kv=True,
                    fixed_mask=causal[0, 0], v_row=t["l3_svb"], out_row=t["l3_aob"])
    cross = t["cross_mask"].rearrange("b c (t p) k -> b (c p) t k", p=P)
    attention_stage(nc, "l3c", step[4], step[5], ctx_t,
                    {"q": [rows("l3_wq", 0, 4, 0, 512)], "k": [rows("l3_kv", 0, 4, 0, 512)],
                     "v": [rows("l3_kv", 0, 4, 512, 1024)], "o": t["l3_co"], "head_mask": t["mask32"]},
                    cols("l3c_cols", q=0, k=4, ln_w=8, ln_b=12), t["ident"],
                    head_dim=32, queries=256, keys=256, norm=True,
                    score_mask=lambda b: cross[b], v_row=t["l3_cvb"], out_row=t["l3_cob"])
    mlp_stage(nc, "m3", step[5], out, t["l3_up"], t["l3_down"], t["l3_db"],
              cols("m3_cols", ln_w=0, ln_b=4, up=8), t["ident"])


def layout(i):
    import numpy as np

    def a(name):
        return np.asarray(i[name])

    def col(*vectors):
        return np.ascontiguousarray(np.concatenate([v.reshape(-1, P).T for v in vectors], axis=1))

    def turned(m):
        return np.ascontiguousarray(m.T)

    def head_mask(d):
        return np.ascontiguousarray(np.kron(np.eye(P // d, dtype=np.float32), np.ones((d, 1), np.float32)))

    zero = np.zeros
    f = np.float32
    ctx = a("ctx_2048")
    qkv_b, kv_b = a("L3_xattn_b_qkv"), a("L3_xattn_b_kv")
    return {
        "x": a("x"), "ctx": ctx, "ctx_t": np.ascontiguousarray(ctx.transpose(0, 2, 1)),
        "ident": np.eye(P, dtype=f), "mask16": head_mask(16), "mask32": head_mask(32), "mask64": head_mask(64),
        "key_mask": a("mask_BxS2_bf1"), "causal_mask": a("mask_1x1xSxS2_fc1"), "cross_mask": a("mask_Bx1xSxS2_ff1"),
        "l0_wq": turned(a("L0_xattn_Wq")), "l0_wk": turned(a("L0_xattn_Wk")), "l0_wv": turned(a("L0_xattn_Wv")),
        "l0_wo": turned(a("L0_xattn_Wo")), "l0_cols": col(zero(256, f), zero(256, f), a("L0_xattn_bo")),
        "l1_wq": a("L1_xattn_q_w"), "l1_wk": a("L1_xattn_k_w"), "l1_wv": a("L1_xattn_v_w"), "l1_wo": a("L1_xattn_cproj_w"),
        "l1_cols": col(a("L1_xattn_q_b"), a("L1_xattn_k_b"), a("L1_xattn_ln1_w"), a("L1_xattn_ln1_b")),
        "l1_vb": a("L1_xattn_v_b"), "l1_ob": a("L1_xattn_cproj_b"),
        "l1_up": a("L1_xattn_fc_w"), "l1_down": a("L1_xattn_proj_w"), "l1_db": a("L1_xattn_proj_b"),
        "m1_cols": col(a("L1_xattn_ln2_w"), a("L1_xattn_ln2_b"), a("L1_xattn_fc_b")),
        "l2_z0": turned(a("L2_xattn_Wqkv0")), "l2_z1": turned(a("L2_xattn_Wqkv1")),
        "l2_u0": turned(a("L2_xattn_Winj0")), "l2_u1": turned(a("L2_xattn_Winj1")),
        "l2_wo": turned(a("L2_xattn_Wo")),
        "l2_cols": col(a("L2_xattn_r_w_bias").reshape(-1), zero(1024, f), a("L2_xattn_bo")),
        "l3_qkv": a("L3_xattn_w_qkv"), "l3_ao": a("L3_xattn_w_ao"),
        "l3s_cols": col(qkv_b[0:512], qkv_b[512:1024], a("L3_xattn_ln1_s"), a("L3_xattn_ln1_b")),
        "l3_svb": np.ascontiguousarray(qkv_b[1024:1536]), "l3_aob": a("L3_xattn_b_ao"),
        "l3_wq": a("L3_xattn_w_q"), "l3_kv": a("L3_xattn_w_kv"), "l3_co": a("L3_xattn_w_co"),
        "l3c_cols": col(a("L3_xattn_b_q"), kv_b[0:512], a("L3_xattn_ln2_s"), a("L3_xattn_ln2_b")),
        "l3_cvb": np.ascontiguousarray(kv_b[512:1024]), "l3_cob": a("L3_xattn_b_co"),
        "l3_up": a("L3_xattn_w1"), "l3_down": a("L3_xattn_w2"), "l3_db": a("L3_xattn_b2"),
        "m3_cols": col(a("L3_xattn_ln3_s"), a("L3_xattn_ln3_b"), a("L3_xattn_b1")),
    }


def kernel(**inputs):
    import concourse.bacc as bacc
    import numpy as np
    from concourse.bass_utils import run_bass_kernel_spmd

    nc = bacc.Bacc("TRN2", target_bir_lowering=False, num_devices=1)
    arrays = {f"in_{k}": np.ascontiguousarray(v) for k, v in layout(inputs).items()}
    t = {k[3:]: nc.dram_tensor(k, v.shape, mybir.dt.from_np(v.dtype), kind="ExternalInput").ap()
         for k, v in arrays.items()}
    out = nc.dram_tensor("out", (NB, ROWS, COLS), F32, kind="ExternalOutput").ap()
    program(nc, t, out)
    r = run_bass_kernel_spmd(nc, [arrays], core_ids=[0])
    return r.results[0]["out"]
```
